# Optimizing a Trainium2 kernel written in Bass

```python
import numpy as np
import jax
import jax.numpy as jnp

def _softmax(x, axis=-1):
    return jax.nn.softmax(x, axis=axis)

def _gelu(x):
    return jax.nn.gelu(x, approximate=True)

def _silu(x):
    return jax.nn.silu(x)

def _sigmoid(x):
    return jax.nn.sigmoid(x)

def _layernorm(x, axis=-1, eps=1e-05):
    m = jnp.mean(x, axis=axis, keepdims=True)
    v = jnp.var(x, axis=axis, keepdims=True)
    return (x - m) / jnp.sqrt(v + eps)

def _scatter_add(tgt, idx, src, axis=0):
    return tgt.at[idx].add(src)

def _segment_sum(src, seg, n):
    return jax.ops.segment_sum(src, seg, n)
kernel_name = 'mk_vit_tower_d2_tok_img768_r4_30be56'

def setup_inputs(seed: int=0):
    np.random.seed(seed)
    _w = jnp.asarray

    def _rec_inputs():
        import jax
        import jax.numpy as jnp
        _rk = jax.random.key(seed)
        x = 7.57192e-06 + 1.00007 * jax.random.normal(jax.random.fold_in(_rk, 1), (64, 3, 64, 64), jnp.float32)
        return x
    x = _rec_inputs()

    def _L0_tok_setup():
        import jax, jax.numpy as jnp
        import numpy as np
        PATCH = 16
        HALF = PATCH // 2
        DIM = 192
        CH = 3
        PATCH_DIM = PATCH * PATCH * 5 * CH
        LN_EPS = 1e-05

        def _shift2d(x, t, l):
            H, W = (x.shape[-2], x.shape[-1])
            at, al = (abs(t), abs(l))
            xp = jnp.pad(x, ((0, 0), (0, 0), (at, at), (al, al)))
            return xp[:, :, at - t:at - t + H, al - l:al - l + W]
        key = jax.random.key(seed)
        k1, k2 = jax.random.split(key, 2)
        x = jax.random.normal(k1, (64, CH, 224, 224), dtype=jnp.float32)
        ln_gamma = jnp.ones((PATCH_DIM,), dtype=jnp.float32)
        ln_beta = jnp.zeros((PATCH_DIM,), dtype=jnp.float32)
        W = jax.random.normal(k2, (DIM, PATCH_DIM), dtype=jnp.float32) * np.float32(1.0 / np.sqrt(PATCH_DIM))
        b = jnp.zeros((DIM,), dtype=jnp.float32)
        return {'x': x, 'ln_gamma': ln_gamma, 'ln_beta': ln_beta, 'W': W, 'b': b}
    _L0_tok_all = _L0_tok_setup()
    _L0_tok_in = {k: v for k, v in _L0_tok_all.items() if k in ('ln_gamma', 'ln_beta', 'W', 'b')}
    del _L0_tok_all

    def _L0_attn_setup():
        import jax, jax.numpy as jnp
        import numpy as np
        D_MODEL = 192
        D_STATE = 16
        D_CONV = 4
        EXPAND = 2
        D_INNER = EXPAND * D_MODEL
        DT_RANK = (D_MODEL + 15) // 16
        BATCH = 2
        SEQLEN = 256

        def _mamba(x, in_w, conv_w, conv_b, xproj_w, dt_w, dt_b, A_log, Dp, out_w):
            B, L, _ = x.shape
            xz = x @ in_w.T
            xc, z = jnp.split(xz, 2, axis=-1)
            K = conv_w.shape[1]
            xpad = jnp.pad(xc, ((0, 0), (K - 1, 0), (0, 0)))
            xconv = conv_b + sum((conv_w[:, k] * xpad[:, k:k + L, :] for k in range(K)))
            u = jax.nn.silu(xconv)
            proj = u @ xproj_w.T
            dt_rank = dt_w.shape[1]
            n = A_log.shape[1]
            dtx, Bm, Cm = jnp.split(proj, [dt_rank, dt_rank + n], axis=-1)
            dt = jax.nn.softplus(dtx @ dt_w.T + dt_b)
            A = -jnp.exp(A_log)
            dA = jnp.exp(dt[..., None] * A)
            dBu = dt[..., None] * Bm[:, :, None, :] * u[..., None]

            def step(h, inp):
                dA_t, dBu_t, C_t = inp
                h = dA_t * h + dBu_t
                y = jnp.einsum('bdn,bn->bd', h, C_t)
                return (h, y)
            h0 = jnp.zeros((B, u.shape[-1], n), x.dtype)
            _, ys = jax.lax.scan(step, h0, (dA.transpose(1, 0, 2, 3), dBu.transpose(1, 0, 2, 3), Cm.transpose(1, 0, 2)))
            y = ys.transpose(1, 0, 2) + u * Dp
            y = y * jax.nn.silu(z)
            return y @ out_w.T
        key = jax.random.key(seed)
        ks = jax.random.split(key, 10)
        s = 0.02
        f32 = jnp.float32
        x = jax.random.normal(ks[0], (BATCH, SEQLEN, D_MODEL), f32)
        bm_in_w = jax.random.normal(ks[1], (2 * D_MODEL, D_MODEL), f32) * s
        bm_in_b = jnp.zeros((2 * D_MODEL,), f32)
        bm_out_w = jax.random.normal(ks[2], (D_MODEL, D_MODEL), f32) * s
        bm_out_b = jnp.zeros((D_MODEL,), f32)
        m_in_w = jax.random.normal(ks[3], (2 * D_INNER, D_MODEL), f32) * s
        m_conv_w = jax.random.normal(ks[4], (D_INNER, D_CONV), f32) * s
        m_conv_b = jnp.zeros((D_INNER,), f32)
        m_xproj_w = jax.random.normal(ks[5], (DT_RANK + 2 * D_STATE, D_INNER), f32) * s
        m_dt_w = jax.random.normal(ks[6], (D_INNER, DT_RANK), f32) * s
        m_dt_b = jnp.full((D_INNER,), -4.6, f32)
        m_A_log = jnp.log(jnp.broadcast_to(jnp.arange(1, D_STATE + 1, dtype=f32), (D_INNER, D_STATE)))
        m_D = jnp.ones((D_INNER,), f32)
        m_out_w = jax.random.normal(ks[7], (D_MODEL, D_INNER), f32) * s
        ln_g = jnp.ones((D_MODEL,), f32)
        ln_b = jnp.zeros((D_MODEL,), f32)
        return {'x': x, 'bm_in_w': bm_in_w, 'bm_in_b': bm_in_b, 'bm_out_w': bm_out_w, 'bm_out_b': bm_out_b, 'm_in_w': m_in_w, 'm_conv_w': m_conv_w, 'm_conv_b': m_conv_b, 'm_xproj_w': m_xproj_w, 'm_dt_w': m_dt_w, 'm_dt_b': m_dt_b, 'm_A_log': m_A_log, 'm_D': m_D, 'm_out_w': m_out_w, 'ln_g': ln_g, 'ln_b': ln_b}
    _L0_attn_all = _L0_attn_setup()
    _L0_attn_in = {k: v for k, v in _L0_attn_all.items() if k in ('bm_in_w', 'bm_in_b', 'bm_out_w', 'bm_out_b', 'm_in_w', 'm_conv_w', 'm_conv_b', 'm_xproj_w', 'm_dt_w', 'm_dt_b', 'm_A_log', 'm_D', 'm_out_w', 'ln_g', 'ln_b')}
    del _L0_attn_all

    def _L0_ffn_setup():
        import jax, jax.numpy as jnp
        import numpy as np
        EPS_NORM = 1e-05
        RMS_EPS = 1e-05

        def _l2_normalize(v):
            n = jnp.sqrt(jnp.sum(v * v, axis=-1, keepdims=True))
            return v / jnp.maximum(n, EPS_NORM)

        def _rms_norm(x, weight, eps):
            ms = jnp.mean(x * x, axis=-1, keepdims=True)
            return x * jax.lax.rsqrt(ms + eps) * weight
        key = jax.random.key(seed)
        ks = jax.random.split(key, 6)
        B, T, D = (8, 1024, 192)
        S, F = (64, 768)
        x = jax.random.normal(ks[0], (B, T, D), dtype=jnp.float32)
        slots = 0.02 * jax.random.normal(ks[1], (S, D), dtype=jnp.float32)
        scale = jnp.ones((S,), dtype=jnp.float32)
        fc1_weight = 0.02 * jax.random.normal(ks[2], (S, D, F), dtype=jnp.float32)
        fc1_bias = jnp.zeros((S, F), dtype=jnp.float32)
        fc2_weight = 0.02 * jax.random.normal(ks[3], (S, F, D), dtype=jnp.float32)
        fc2_bias = jnp.zeros((S, D), dtype=jnp.float32)
        norm_weight = jnp.ones((D,), dtype=jnp.float32)
        return {'x': x, 'slots': slots, 'scale': scale, 'fc1_weight': fc1_weight, 'fc1_bias': fc1_bias, 'fc2_weight': fc2_weight, 'fc2_bias': fc2_bias, 'norm_weight': norm_weight}
    _L0_ffn_all = _L0_ffn_setup()
    _L0_ffn_in = {k: v for k, v in _L0_ffn_all.items() if k in ('slots', 'scale', 'fc1_weight', 'fc1_bias', 'fc2_weight', 'fc2_bias', 'norm_weight')}
    del _L0_ffn_all

    def _L1_attn_setup():
        import jax, jax.numpy as jnp
        import numpy as np
        B, L, D, H, F, NL, K, G = (2, 512, 192, 12, 768, 12, 128, 16)
        HD = D // H
        SCALE = HD ** (-0.5)

        def _ln(x, g, b, eps=1e-05):
            m = jnp.mean(x, axis=-1, keepdims=True)
            v = jnp.mean(jnp.square(x - m), axis=-1, keepdims=True)
            return (x - m) * jax.lax.rsqrt(v + eps) * g + b
        key = jax.random.key(seed)
        ks = jax.random.split(key, 8)
        n = lambda k, s, std=0.02: jax.random.normal(k, s, dtype=jnp.float32) * std
        return {'x': jax.random.normal(ks[0], (B, L, D), dtype=jnp.float32), 'pos_conv_w': n(ks[1], (D, D // G, K)), 'pos_conv_b': jnp.zeros((D,), jnp.float32), 'ln0_g': jnp.ones((D,), jnp.float32), 'ln0_b': jnp.zeros((D,), jnp.float32), 'Wq': n(ks[2], (NL, D, D)), 'bq': jnp.zeros((NL, D), jnp.float32), 'Wk': n(ks[3], (NL, D, D)), 'bk': jnp.zeros((NL, D), jnp.float32), 'Wv': n(ks[4], (NL, D, D)), 'bv': jnp.zeros((NL, D), jnp.float32), 'Wo': n(ks[5], (NL, D, D)), 'bo': jnp.zeros((NL, D), jnp.float32), 'ln1_g': jnp.ones((NL, D), jnp.float32), 'ln1_b': jnp.zeros((NL, D), jnp.float32), 'W1': n(ks[6], (NL, D, F)), 'b1': jnp.zeros((NL, F), jnp.float32), 'W2': n(ks[7], (NL, F, D)), 'b2': jnp.zeros((NL, D), jnp.float32), 'ln2_g': jnp.ones((NL, D), jnp.float32), 'ln2_b': jnp.zeros((NL, D), jnp.float32)}
    _L1_attn_all = _L1_attn_setup()
    _L1_attn_in = {k: v for k, v in _L1_attn_all.items() if k in ('pos_conv_w', 'pos_conv_b', 'ln0_g', 'ln0_b', 'Wq', 'bq', 'Wk', 'bk', 'Wv', 'bv', 'Wo', 'bo', 'ln1_g', 'ln1_b', 'W1', 'b1', 'W2', 'b2', 'ln2_g', 'ln2_b')}
    del _L1_attn_all

    def _L1_ffn_setup():
        import jax, jax.numpy as jnp
        import numpy as np
        B, S, D, F, E = (8, 512, 192, 768, 16)
        CAP = 64
        EPS = 1e-06

        def _switch_moe_block(x, ln_w, w_router, wi, wo):
            var = jnp.mean(jnp.square(x.astype(jnp.float32)), axis=-1, keepdims=True)
            normed = (x * jax.lax.rsqrt(var + EPS)).astype(x.dtype) * ln_w
            logits = jnp.einsum('bsd,de->bse', normed.astype(jnp.float32), w_router.astype(jnp.float32))
            probs = jax.nn.softmax(logits, axis=-1)
            expert_idx = jnp.argmax(probs, axis=-1)
            onehot = jax.nn.one_hot(expert_idx, E, dtype=jnp.float32)
            priority = jnp.cumsum(onehot, axis=1)
            keep = onehot * (priority <= CAP)
            pos = (priority - 1.0).astype(jnp.int32)
            dispatch = keep[..., None] * jax.nn.one_hot(pos, CAP, dtype=jnp.float32)
            expert_in = jnp.einsum('bsec,bsd->becd', dispatch, normed)
            h = jax.nn.relu(jnp.einsum('becd,edf->becf', expert_in, wi))
            expert_out = jnp.einsum('becf,efd->becd', h, wo)
            combined = jnp.einsum('bsec,becd->bsd', dispatch, expert_out)
            routed = jnp.sum(dispatch, axis=(2, 3)) > 0
            next_states = jnp.where(routed[..., None], combined.astype(x.dtype), normed)
            router_prob = jnp.max(probs, axis=-1, keepdims=True).astype(x.dtype)
            return x + router_prob * next_states
        key = jax.random.key(seed)
        k_x, k_r, k_wi, k_wo = jax.random.split(key, 4)
        x = jax.random.normal(k_x, (B, S, D), dtype=jnp.float32)
        ln_w = jnp.ones((D,), dtype=jnp.float32)
        w_router = jax.random.normal(k_r, (D, E), dtype=jnp.float32) * 0.02
        wi = jax.random.normal(k_wi, (E, D, F), dtype=jnp.float32) * D ** (-0.5)
        wo = jax.random.normal(k_wo, (E, F, D), dtype=jnp.float32) * F ** (-0.5)
        return {'x': x, 'ln_w': ln_w, 'w_router': w_router, 'wi': wi, 'wo': wo}
    _L1_ffn_all = _L1_ffn_setup()
    _L1_ffn_in = {k: v for k, v in _L1_ffn_all.items() if k in ('ln_w', 'w_router', 'wi', 'wo')}
    del _L1_ffn_all
    return {'x': x, 'L0_tok_ln_gamma': _L0_tok_in['ln_gamma'], 'L0_tok_ln_beta': _L0_tok_in['ln_beta'], 'L0_tok_W': _L0_tok_in['W'], 'L0_tok_b': _L0_tok_in['b'], 'L0_attn_bm_in_w': _L0_attn_in['bm_in_w'], 'L0_attn_bm_in_b': _L0_attn_in['bm_in_b'], 'L0_attn_bm_out_w': _L0_attn_in['bm_out_w'], 'L0_attn_bm_out_b': _L0_attn_in['bm_out_b'], 'L0_attn_m_in_w': _L0_attn_in['m_in_w'], 'L0_attn_m_conv_w': _L0_attn_in['m_conv_w'], 'L0_attn_m_conv_b': _L0_attn_in['m_conv_b'], 'L0_attn_m_xproj_w': _L0_attn_in['m_xproj_w'], 'L0_attn_m_dt_w': _L0_attn_in['m_dt_w'], 'L0_attn_m_dt_b': _L0_attn_in['m_dt_b'], 'L0_attn_m_A_log': _L0_attn_in['m_A_log'], 'L0_attn_m_D': _L0_attn_in['m_D'], 'L0_attn_m_out_w': _L0_attn_in['m_out_w'], 'L0_attn_ln_g': _L0_attn_in['ln_g'], 'L0_attn_ln_b': _L0_attn_in['ln_b'], 'L0_ffn_slots': _L0_ffn_in['slots'], 'L0_ffn_scale': _L0_ffn_in['scale'], 'L0_ffn_fc1_weight': _L0_ffn_in['fc1_weight'], 'L0_ffn_fc1_bias': _L0_ffn_in['fc1_bias'], 'L0_ffn_fc2_weight': _L0_ffn_in['fc2_weight'], 'L0_ffn_fc2_bias': _L0_ffn_in['fc2_bias'], 'L0_ffn_norm_weight': _L0_ffn_in['norm_weight'], 'L1_attn_pos_conv_w': _L1_attn_in['pos_conv_w'], 'L1_attn_pos_conv_b': _L1_attn_in['pos_conv_b'], 'L1_attn_ln0_g': _L1_attn_in['ln0_g'], 'L1_attn_ln0_b': _L1_attn_in['ln0_b'], 'L1_attn_Wq': _L1_attn_in['Wq'], 'L1_attn_bq': _L1_attn_in['bq'], 'L1_attn_Wk': _L1_attn_in['Wk'], 'L1_attn_bk': _L1_attn_in['bk'], 'L1_attn_Wv': _L1_attn_in['Wv'], 'L1_attn_bv': _L1_attn_in['bv'], 'L1_attn_Wo': _L1_attn_in['Wo'], 'L1_attn_bo': _L1_attn_in['bo'], 'L1_attn_ln1_g': _L1_attn_in['ln1_g'], 'L1_attn_ln1_b': _L1_attn_in['ln1_b'], 'L1_attn_W1': _L1_attn_in['W1'], 'L1_attn_b1': _L1_attn_in['b1'], 'L1_attn_W2': _L1_attn_in['W2'], 'L1_attn_b2': _L1_attn_in['b2'], 'L1_attn_ln2_g': _L1_attn_in['ln2_g'], 'L1_attn_ln2_b': _L1_attn_in['ln2_b'], 'L1_ffn_ln_w': _L1_ffn_in['ln_w'], 'L1_ffn_w_router': _L1_ffn_in['w_router'], 'L1_ffn_wi': _L1_ffn_in['wi'], 'L1_ffn_wo': _L1_ffn_in['wo']}

def reference(x, L0_tok_ln_gamma, L0_tok_ln_beta, L0_tok_W, L0_tok_b, L0_attn_bm_in_w, L0_attn_bm_in_b, L0_attn_bm_out_w, L0_attn_bm_out_b, L0_attn_m_in_w, L0_attn_m_conv_w, L0_attn_m_conv_b, L0_attn_m_xproj_w, L0_attn_m_dt_w, L0_attn_m_dt_b, L0_attn_m_A_log, L0_attn_m_D, L0_attn_m_out_w, L0_attn_ln_g, L0_attn_ln_b, L0_ffn_slots, L0_ffn_scale, L0_ffn_fc1_weight, L0_ffn_fc1_bias, L0_ffn_fc2_weight, L0_ffn_fc2_bias, L0_ffn_norm_weight, L1_attn_pos_conv_w, L1_attn_pos_conv_b, L1_attn_ln0_g, L1_attn_ln0_b, L1_attn_Wq, L1_attn_bq, L1_attn_Wk, L1_attn_bk, L1_attn_Wv, L1_attn_bv, L1_attn_Wo, L1_attn_bo, L1_attn_ln1_g, L1_attn_ln1_b, L1_attn_W1, L1_attn_b1, L1_attn_W2, L1_attn_b2, L1_attn_ln2_g, L1_attn_ln2_b, L1_ffn_ln_w, L1_ffn_w_router, L1_ffn_wi, L1_ffn_wo):
    import jax
    import jax.numpy as jnp

    def _L0_tok_ref(x, ln_gamma, ln_beta, W, b):
        import jax, jax.numpy as jnp
        import numpy as np
        PATCH = 16
        HALF = PATCH // 2
        DIM = 192
        CH = 3
        PATCH_DIM = PATCH * PATCH * 5 * CH
        LN_EPS = 1e-05

        def _shift2d(x, t, l):
            H, W = (x.shape[-2], x.shape[-1])
            at, al = (abs(t), abs(l))
            xp = jnp.pad(x, ((0, 0), (0, 0), (at, at), (al, al)))
            return xp[:, :, at - t:at - t + H, al - l:al - l + W]
        p = PATCH
        shifts = ((1, -1, 1, -1), (-1, 1, -1, 1), (-1, 1, 1, -1), (1, -1, -1, 1))
        parts = [x] + [_shift2d(x, HALF * s[2], HALF * s[0]) for s in shifts]
        xc = jnp.concatenate(parts, axis=1)
        B, C5, H, Wd = xc.shape
        h, w = (H // p, Wd // p)
        patches = xc.reshape(B, C5, h, p, w, p)
        patches = patches.transpose(0, 2, 4, 3, 5, 1).reshape(B, h * w, p * p * C5)
        mu = patches.mean(axis=-1, keepdims=True)
        var = patches.var(axis=-1, keepdims=True)
        xn = (patches - mu) * jax.lax.rsqrt(var + LN_EPS) * ln_gamma + ln_beta
        return jnp.einsum('bnp,dp->bnd', xn, W) + b

    def _L0_attn_ref(x, bm_in_w, bm_in_b, bm_out_w, bm_out_b, m_in_w, m_conv_w, m_conv_b, m_xproj_w, m_dt_w, m_dt_b, m_A_log, m_D, m_out_w, ln_g, ln_b):
        import jax, jax.numpy as jnp
        import numpy as np
        D_MODEL = 192
        D_STATE = 16
        D_CONV = 4
        EXPAND = 2
        D_INNER = EXPAND * D_MODEL
        DT_RANK = (D_MODEL + 15) // 16
        BATCH = 2
        SEQLEN = 256

        def _mamba(x, in_w, conv_w, conv_b, xproj_w, dt_w, dt_b, A_log, Dp, out_w):
            B, L, _ = x.shape
            xz = x @ in_w.T
            xc, z = jnp.split(xz, 2, axis=-1)
            K = conv_w.shape[1]
            xpad = jnp.pad(xc, ((0, 0), (K - 1, 0), (0, 0)))
            xconv = conv_b + sum((conv_w[:, k] * xpad[:, k:k + L, :] for k in range(K)))
            u = jax.nn.silu(xconv)
            proj = u @ xproj_w.T
            dt_rank = dt_w.shape[1]
            n = A_log.shape[1]
            dtx, Bm, Cm = jnp.split(proj, [dt_rank, dt_rank + n], axis=-1)
            dt = jax.nn.softplus(dtx @ dt_w.T + dt_b)
            A = -jnp.exp(A_log)
            dA = jnp.exp(dt[..., None] * A)
            dBu = dt[..., None] * Bm[:, :, None, :] * u[..., None]

            def step(h, inp):
                dA_t, dBu_t, C_t = inp
                h = dA_t * h + dBu_t
                y = jnp.einsum('bdn,bn->bd', h, C_t)
                return (h, y)
            h0 = jnp.zeros((B, u.shape[-1], n), x.dtype)
            _, ys = jax.lax.scan(step, h0, (dA.transpose(1, 0, 2, 3), dBu.transpose(1, 0, 2, 3), Cm.transpose(1, 0, 2)))
            y = ys.transpose(1, 0, 2) + u * Dp
            y = y * jax.nn.silu(z)
            return y @ out_w.T
        mparams = (m_in_w, m_conv_w, m_conv_b, m_xproj_w, m_dt_w, m_dt_b, m_A_log, m_D, m_out_w)
        xp = x @ bm_in_w.T + bm_in_b
        x_f, x_b = jnp.split(xp, 2, axis=-1)
        out_f = _mamba(x_f, *mparams)
        out_b = jnp.flip(_mamba(jnp.flip(x_b, axis=1), *mparams), axis=1)
        mo = (out_f + out_b) @ bm_out_w.T + bm_out_b
        h = mo + x
        mu = jnp.mean(h, axis=-1, keepdims=True)
        var = jnp.mean(jnp.square(h - mu), axis=-1, keepdims=True)
        return (h - mu) * jax.lax.rsqrt(var + 1e-05) * ln_g + ln_b

    def _L0_ffn_ref(x, slots, scale, fc1_weight, fc1_bias, fc2_weight, fc2_bias, norm_weight):
        import jax, jax.numpy as jnp
        import numpy as np
        EPS_NORM = 1e-05
        RMS_EPS = 1e-05

        def _l2_normalize(v):
            n = jnp.sqrt(jnp.sum(v * v, axis=-1, keepdims=True))
            return v / jnp.maximum(n, EPS_NORM)

        def _rms_norm(x, weight, eps):
            ms = jnp.mean(x * x, axis=-1, keepdims=True)
            return x * jax.lax.rsqrt(ms + eps) * weight
        xn = _rms_norm(x, norm_weight, RMS_EPS)
        tok = _l2_normalize(xn)
        sl = _l2_normalize(slots) * scale[:, None]
        logits = jnp.einsum('sd,btd->bst', sl, tok)
        dispatch_w = jax.nn.softmax(logits, axis=-1)
        combine_w = jax.nn.softmax(logits, axis=-2)
        y = jnp.einsum('btd,bst->bsd', xn, dispatch_w)
        y = jnp.einsum('sio,bsi->bso', fc1_weight, y) + fc1_bias
        y = jax.nn.gelu(y, approximate=False)
        y = jnp.einsum('sio,bsi->bso', fc2_weight, y) + fc2_bias
        out = jnp.einsum('bsd,bst->btd', y, combine_w)
        return out

    def _L1_attn_ref(x, pos_conv_w, pos_conv_b, ln0_g, ln0_b, Wq, bq, Wk, bk, Wv, bv, Wo, bo, ln1_g, ln1_b, W1, b1, W2, b2, ln2_g, ln2_b):
        import jax, jax.numpy as jnp
        import numpy as np
        B, L, D, H, F, NL, K, G = (2, 512, 192, 12, 768, 12, 128, 16)
        HD = D // H
        SCALE = HD ** (-0.5)

        def _ln(x, g, b, eps=1e-05):
            m = jnp.mean(x, axis=-1, keepdims=True)
            v = jnp.mean(jnp.square(x - m), axis=-1, keepdims=True)
            return (x - m) * jax.lax.rsqrt(v + eps) * g + b
        b_, l_, d_ = x.shape
        pos = jax.lax.conv_general_dilated(x.transpose(0, 2, 1), pos_conv_w, (1,), [(K // 2, K // 2)], feature_group_count=G)
        pos = pos[:, :, :l_] + pos_conv_b[None, :, None]
        h = x + jax.nn.gelu(pos, approximate=False).transpose(0, 2, 1)
        h = _ln(h, ln0_g, ln0_b)

        def layer(h, p):
            wq, bq_, wk, bk_, wv, bv_, wo, bo_, g1, be1, w1, bf1, w2, bf2, g2, be2 = p
            r = h
            q = (h @ wq + bq_).reshape(b_, l_, H, HD)
            k = (h @ wk + bk_).reshape(b_, l_, H, HD)
            v = (h @ wv + bv_).reshape(b_, l_, H, HD)
            w = jax.nn.softmax(SCALE * jnp.einsum('blhd,bmhd->bhlm', q, k), axis=-1)
            o = jnp.einsum('bhlm,bmhd->blhd', w, v).reshape(b_, l_, d_)
            h = r + (o @ wo + bo_)
            h = _ln(h, g1, be1)
            ff = jax.nn.gelu(h @ w1 + bf1, approximate=False) @ w2 + bf2
            h = _ln(h + ff, g2, be2)
            return (h, None)
        h, _ = jax.lax.scan(layer, h, (Wq, bq, Wk, bk, Wv, bv, Wo, bo, ln1_g, ln1_b, W1, b1, W2, b2, ln2_g, ln2_b))
        return h

    def _L1_ffn_ref(x, ln_w, w_router, wi, wo):
        import jax, jax.numpy as jnp
        import numpy as np
        B, S, D, F, E = (8, 512, 192, 768, 16)
        CAP = 64
        EPS = 1e-06

        def _switch_moe_block(x, ln_w, w_router, wi, wo):
            var = jnp.mean(jnp.square(x.astype(jnp.float32)), axis=-1, keepdims=True)
            normed = (x * jax.lax.rsqrt(var + EPS)).astype(x.dtype) * ln_w
            logits = jnp.einsum('bsd,de->bse', normed.astype(jnp.float32), w_router.astype(jnp.float32))
            probs = jax.nn.softmax(logits, axis=-1)
            expert_idx = jnp.argmax(probs, axis=-1)
            onehot = jax.nn.one_hot(expert_idx, E, dtype=jnp.float32)
            priority = jnp.cumsum(onehot, axis=1)
            keep = onehot * (priority <= CAP)
            pos = (priority - 1.0).astype(jnp.int32)
            dispatch = keep[..., None] * jax.nn.one_hot(pos, CAP, dtype=jnp.float32)
            expert_in = jnp.einsum('bsec,bsd->becd', dispatch, normed)
            h = jax.nn.relu(jnp.einsum('becd,edf->becf', expert_in, wi))
            expert_out = jnp.einsum('becf,efd->becd', h, wo)
            combined = jnp.einsum('bsec,becd->bsd', dispatch, expert_out)
            routed = jnp.sum(dispatch, axis=(2, 3)) > 0
            next_states = jnp.where(routed[..., None], combined.astype(x.dtype), normed)
            router_prob = jnp.max(probs, axis=-1, keepdims=True).astype(x.dtype)
            return x + router_prob * next_states
        return _switch_moe_block(x, ln_w, w_router, wi, wo)
    h = _L0_tok_ref(x, L0_tok_ln_gamma, L0_tok_ln_beta, L0_tok_W, L0_tok_b)
    h = h + _L0_attn_ref(_layernorm(h, axis=-1), L0_attn_bm_in_w, L0_attn_bm_in_b, L0_attn_bm_out_w, L0_attn_bm_out_b, L0_attn_m_in_w, L0_attn_m_conv_w, L0_attn_m_conv_b, L0_attn_m_xproj_w, L0_attn_m_dt_w, L0_attn_m_dt_b, L0_attn_m_A_log, L0_attn_m_D, L0_attn_m_out_w, L0_attn_ln_g, L0_attn_ln_b)
    h = h + _L0_ffn_ref(_layernorm(h, axis=-1), L0_ffn_slots, L0_ffn_scale, L0_ffn_fc1_weight, L0_ffn_fc1_bias, L0_ffn_fc2_weight, L0_ffn_fc2_bias, L0_ffn_norm_weight)
    h = h + _L1_attn_ref(_layernorm(h, axis=-1), L1_attn_pos_conv_w, L1_attn_pos_conv_b, L1_attn_ln0_g, L1_attn_ln0_b, L1_attn_Wq, L1_attn_bq, L1_attn_Wk, L1_attn_bk, L1_attn_Wv, L1_attn_bv, L1_attn_Wo, L1_attn_bo, L1_attn_ln1_g, L1_attn_ln1_b, L1_attn_W1, L1_attn_b1, L1_attn_W2, L1_attn_b2, L1_attn_ln2_g, L1_attn_ln2_b)
    h = h + _L1_ffn_ref(_layernorm(h, axis=-1), L1_ffn_ln_w, L1_ffn_w_router, L1_ffn_wi, L1_ffn_wo)
    return h

_drawn_inputs = setup_inputs


def setup_inputs(seed=0):
    import zlib

    import numpy as np

    out = dict(_drawn_inputs(seed))
    spreads = {'L0_tok_ln_gamma': (1.0, 0.2),
     'L0_tok_ln_beta': (0.0, 0.1),
     'L0_tok_b': (0.0, 0.1),
     'L0_attn_bm_in_b': (0.0, 0.8),
     'L0_attn_bm_out_b': (0.0, 2.0),
     'L0_attn_m_conv_b': (0.0, 0.8),
     'L0_attn_m_dt_b': (-4.599999904632568, 0.6),
     'L0_attn_m_D': (1.0, 0.6),
     'L0_attn_ln_g': (1.0, 0.2),
     'L0_attn_ln_b': (0.0, 0.1),
     'L0_ffn_scale': (1.0, 0.6),
     'L0_ffn_fc1_bias': (0.0, 0.8),
     'L0_ffn_fc2_bias': (0.0, 0.8),
     'L0_ffn_norm_weight': (1.0, 0.6),
     'L1_attn_pos_conv_b': (0.0, 0.404),
     'L1_attn_ln0_g': (1.0, 0.2),
     'L1_attn_ln0_b': (0.0, 0.334),
     'L1_attn_bq': (0.0, 0.8),
     'L1_attn_bk': (0.0, 2.0),
     'L1_attn_bv': (0.0, 0.279),
     'L1_attn_bo': (0.0, 0.1),
     'L1_attn_ln1_g': (1.0, 0.2),
     'L1_attn_ln1_b': (0.0, 0.1),
     'L1_attn_b1': (0.0, 0.1),
     'L1_attn_b2': (0.0, 0.1),
     'L1_attn_ln2_g': (1.0, 0.2),
     'L1_attn_ln2_b': (0.0, 0.1),
     'L1_ffn_ln_w': (1.0, 0.6)}
    factors = {'L0_attn_bm_in_w': 8.0,
     'L0_attn_bm_out_w': 8.0,
     'L0_attn_m_in_w': 8.0,
     'L0_attn_m_conv_w': 8.0,
     'L0_attn_m_xproj_w': 8.0,
     'L0_attn_m_dt_w': 8.0,
     'L0_attn_m_A_log': 8.0,
     'L0_attn_m_out_w': 8.0,
     'L0_ffn_slots': 8.0,
     'L0_ffn_fc1_weight': 8.0,
     'L0_ffn_fc2_weight': 8.0,
     'L1_attn_Wq': 8.0,
     'L1_attn_Wk': 8.0,
     'L1_ffn_w_router': 3.023,
     'L1_ffn_wi': 3.553,
     'L1_ffn_wo': 2.975}
    for name, (base, spread) in spreads.items():
        noise = np.random.default_rng([zlib.crc32(name.encode()), seed]).standard_normal(out[name].shape)
        drawn = base * np.exp(spread * noise) if base else spread * noise
        out[name] = jnp.asarray(drawn.astype(out[name].dtype))
    for name, factor in factors.items():
        out[name] = (out[name] * factor).astype(out[name].dtype)
    return out
```

```python
from contextlib import ExitStack

import numpy as np

import concourse.bass as bass
from concourse import mybir

F32 = mybir.dt.float32
BF16 = mybir.dt.bfloat16
ALU = mybir.AluOpType
ACT = mybir.ActivationFunctionType
AX = mybir.AxisListType

P = 128
IMG, CH, SIDE = 64, 3, 64
PATCH = 16
BLK = PATCH // 2
SEQ = (SIDE // PATCH) ** 2
D = 192
HD2 = D // 2
TOK = IMG * SEQ
TPI = P // SEQ
NT = TOK // P
HT = NT // 2
HTOK = TOK // 2
HIMG = IMG // 2
GRID = 9
CELLS = GRID * GRID
XCOLS = IMG * CELLS
PDIM = 5 * CH * PATCH * PATCH
NCHUNK = PDIM // P
SHIFTS = ((0, 0), (-1, -1), (1, 1), (-1, 1), (1, -1))
EPS = 1e-5
BIG = 1e30


def place(delta):
    return {0: 0, 1: GRID // 2 + 1, -1: GRID // 2, 2: 1}[delta]


def patch_chunks():
    first = [(0, dy + sy, dx + sx) for sy, sx in SHIFTS for dy in (0, 1) for dx in (0, 1)]
    second = [(1 if sx == 0 else 2, dy + sy, sx) for sy, sx in SHIFTS for dy in (0, 1)]
    return first + second


class Steps:

    def __init__(self, eng, sem):
        self.eng, self.sem, self.before, self.local, self.i, self.per = eng, sem, 0, 0, None, 0

    def __call__(self, ins):
        ins.then_inc(self.sem, 1)
        self.local += 1
        self.wait()
        return ins

    def wait(self):
        base = self.before if self.i is None else self.i * self.per + self.before
        self.eng.wait_ge(self.sem, base + self.local)

    def enter(self, i, per):
        self.before, self.local, self.i, self.per = self.before + self.local, 0, i, per

    def leave(self, rounds):
        assert self.local == self.per, (self.local, self.per)
        self.before, self.local, self.i = self.before + rounds * self.per, 0, None


def scope(nc):
    ctx = ExitStack()

    def sb(name, shape, dt=F32):
        return ctx.enter_context(nc.sbuf_tensor("s_" + name, shape, dt))

    def bank(name, shape=(P, 512), dt=F32):
        return ctx.enter_context(nc.psum_tensor(name, list(shape), dt))

    def sem(name):
        return ctx.enter_context(nc.semaphore(name))

    return ctx, sb, bank, sem


def tokenize(nc, a, kept):
    chunks = patch_chunks()
    ctx, sb, bank, sem = scope(nc)
    with ctx:
        xg = [sb(f"tok_x{i}", [P, XCOLS]) for i in range(3)]
        sq = sb("tok_squares", [P, XCOLS])
        w_raw = sb("tok_w_raw", [P, NCHUNK, D])
        w_gam = sb("tok_w_gamma", [P, NCHUNK, D + 1])
        gb = sb("tok_gamma_beta", [P, 2, NCHUNK])
        ones = sb("tok_ones", [P, P])
        wsum = sb("tok_w_sum", [P, D])
        wbeta = sb("tok_w_beta", [P, D])
        cols = sb("tok_colsum", [P, D])
        bias = sb("tok_bias", [P, D])
        blk = sb("tok_block_sq", [64, XCOLS])
        r4 = sb("tok_row4", [1, IMG, GRID, 4])
        r2 = sb("tok_row2", [1, IMG, GRID, 4])
        ssq = sb("tok_ssq_row", [1, IMG, 4, 4])
        st = sb("tok_stats", [P, 8, NT])
        bn = sb("tok_bn", [P, NT, 8])
        half = sb("tok_neg_half", [P, 1])
        xc = [sb(f"tok_chunk{i}", [P, HTOK]) for i in range(3)]
        acc = [bank(f"tok_acc{i}") for i in range(4)]
        blk_ps = [bank(f"tok_blk_ps{i}") for i in range(2)]
        bc_ps = bank("tok_bc_ps")
        ssq_ps = bank("tok_ssq_ps")
        x_in = [sem(f"tok_x_in{i}") for i in range(3)]
        w_in = [sem(f"tok_w_in{i}") for i in range(3)]
        small_in = sem("tok_small_in")
        squares = sem("tok_squares_done")
        sq_ready = sem("tok_sq_ready")
        ones_set = sem("tok_ones_set")
        w_scaled = sem("tok_w_scaled")
        blk_full = sem("tok_blk_full")
        blk_free = sem("tok_blk_free")
        ssq_row = sem("tok_ssq_row_ready")
        ssq_full = sem("tok_ssq_full")
        sums = sem("tok_w_sums")
        bc_full = sem("tok_bc_full")
        acc_full = sem("tok_acc_full")
        gathered = sem("tok_gathered")
        chunk_used = sem("tok_chunk_used")
        var_ready = sem("tok_var_ready")
        rstd_ready = sem("tok_rstd_ready")
        half_set = sem("tok_half_set")
        dve_steps = sem("tok_dve_steps")
        block = ctx.enter_context(nc.Block())
        NB = -(-XCOLS // 512)
        W3 = NCHUNK // 3

        @block.sync
        def _(sp):
            sp.dma_start(xg[0][:, :], a["x_grid01"]).then_inc(x_in[0], 16)
            for i in range(3):
                sp.dma_start(w_raw[:, W3 * i:W3 * (i + 1), :], a["tok_w"][:, W3 * i:W3 * (i + 1), :]).then_inc(w_in[i], 16)

        @block.scalar
        def _(act):
            act.dma_start(gb[:, :, :], a["tok_gb"]).then_inc(small_in, 16)
            for i, shift in ((1, 5), (2, -4)):
                act.dma_start(xg[i][0:64, :], a["x_grid2"][:, 8:8 + XCOLS]).then_inc(x_in[i], 16)
                act.dma_start(xg[i][64:128, :], a["x_grid2"][:, 8 + shift:8 + shift + XCOLS]).then_inc(x_in[i], 16)
            act.dma_start(bias[:, :], a["tok_b"].partition_broadcast(P)).then_inc(small_in, 16)
            act.wait_ge(x_in[0], 16)
            nc.scalar.activation(sq[:, :], xg[0][:, :], ACT.Square).then_inc(squares, 1)
            act.wait_ge(x_in[1], 32)
            nc.scalar.activation(blk[0:64, :], xg[1][0:64, :], ACT.Square).then_inc(squares, 1)
            act.wait_ge(small_in, 32)
            for c in range(NCHUNK):
                act.wait_ge(w_in[c // W3], 16)
                nc.scalar.activation(w_gam[:, c, 0:D], w_raw[:, c, :], ACT.Copy, scale=gb[:, 0, c:c + 1]).then_inc(w_scaled, 1)

        @block.gpsimd
        def _(pool):
            nc.gpsimd.memset(ones[:, :], 1.0).then_inc(ones_set, 1)
            nc.gpsimd.memset(w_gam[:, :, D:D + 1], 1.0).then_inc(ones_set, 1)
            nc.gpsimd.memset(half[:, :], -0.5).then_inc(half_set, 1)
            pool.wait_ge(half_set, 1)
            for hh in range(2):
                for k, (src, dst) in enumerate(((1, 2), (4, 5))):
                    pool.wait_ge(var_ready, 2 * hh + k + 1)
                    nc.gpsimd.tensor_tensor(st[:, src, hh * HT:(hh + 1) * HT], st[:, src, hh * HT:(hh + 1) * HT],
                                            half[:, 0:1].broadcast_to([P, HT]), ALU.pow).then_inc(rstd_ready, 1)

        @block.tensor
        def _(pe):
            def region(t):
                return acc[t // 2][:, 256 * (t % 2):256 * (t % 2) + D + 1]

            def product(hh):
                for c in range(NCHUNK):
                    if hh == 0:
                        pe.wait_ge(w_scaled, c + 1)
                        if c == 0:
                            pe.wait_ge(ones_set, 2)
                    pe.wait_ge(gathered, hh * NCHUNK + c + 1)
                    for t in range(HT):
                        mm = nc.tensor.matmul(region(hh * HT + t), xc[c % 3][:, t * P:(t + 1) * P], w_gam[:, c, :],
                                              start=(c == 0 and t % 2 == 0), stop=(c == NCHUNK - 1), skip_group_check=True)
                    mm.then_inc(chunk_used, 1)
                    if hh == 0 and 8 <= c < 8 + NB:
                        block_sums(c - 8)

            def block_sums(n):
                if n == 0:
                    pe.wait_ge(sq_ready, 1)
                w = min(512, XCOLS - 512 * n)
                if n >= 2:
                    pe.wait_ge(blk_free, n - 1)
                nc.tensor.matmul(blk_ps[n % 2][0:1, 0:w], ones[:, 0:1], sq[:, 512 * n:512 * n + w],
                                 start=True, stop=True).then_inc(blk_full, 1)

            def spread_sums():
                pe.wait_ge(sums, 2)
                nc.tensor.matmul(bc_ps[:, 0:D], ones[:, :], wsum[:, :], start=True, stop=True)
                nc.tensor.matmul(bc_ps[:, D:2 * D], ones[:, :], wbeta[:, :], start=True, stop=True).then_inc(bc_full, 1)

            def turn_squares():
                pe.wait_ge(ssq_row, 1)
                flat = ssq[:, :, :, :].rearrange("p b i j -> p (b i j)")
                for t in range(NT):
                    mm = nc.tensor.matmul(ssq_ps[:, t:t + 1], flat[:, t * P:(t + 1) * P], ones[0:1, 0:1], start=True, stop=True)
                mm.then_inc(ssq_full, 1)

            product(0)
            spread_sums()
            turn_squares()
            product(1)

        @block.vector
        def _(dve):
            step = Steps(dve, dve_steps)
            grids = [x[:, :].rearrange("p (b y x) -> p b y x", b=IMG, y=GRID) for x in xg]

            def gather(hh, c):
                src, dy, dx = chunks[c]
                n = hh * NCHUNK + c
                if n >= 3:
                    dve.wait_ge(chunk_used, n - 2)
                if n in (0, 20):
                    dve.wait_ge(x_in[1 if src else 0], 32 if src else 16)
                if src == 2:
                    dve.wait_ge(x_in[2], 32)
                y, x = place(dy), place(dx)
                out = xc[n % 3][:, :].rearrange("p (b i j) -> p b i j", b=HIMG, i=4)
                nc.vector.tensor_copy(out, grids[src][:, hh * HIMG:(hh + 1) * HIMG, y:y + 4, x:x + 4]).then_inc(gathered, 1)

            def finish(hh):
                dve.wait_ge(chunk_used, (hh + 1) * NCHUNK)
                ts = slice(hh * HT, (hh + 1) * HT)
                for b in range(2):
                    tt = slice(hh * HT + 2 * b, hh * HT + 2 * b + 2)
                    total = acc[2 * hh + b][:, :].rearrange("p (t n) -> p t n", t=2)[:, :, D]
                    step(nc.vector.tensor_scalar(st[:, 0, tt], total, -1.0 / PDIM, None, ALU.mult))
                step(nc.vector.tensor_tensor(st[:, 1, ts], st[:, 0, ts], st[:, 0, ts], ALU.mult))
                step(nc.vector.tensor_tensor(st[:, 1, ts], st[:, 3, ts], st[:, 1, ts], ALU.subtract))
                nc.vector.tensor_scalar(st[:, 1, ts], st[:, 1, ts], EPS, None, ALU.add).then_inc(var_ready, 1)
                for t in range(hh * HT, hh * HT + HT):
                    step(nc.vector.scalar_tensor_tensor(kept.h[:, t, :], cols[:, :], st[:, 0, t:t + 1],
                                                        acc[t // 2][:, 256 * (t % 2):256 * (t % 2) + D], ALU.mult, ALU.add))
                dve.wait_ge(rstd_ready, 2 * hh + 1)
                for t in range(hh * HT, hh * HT + HT):
                    step(nc.vector.scalar_tensor_tensor(kept.h[:, t, :], kept.h[:, t, :], st[:, 1, t:t + 1], bias[:, :], ALU.mult, ALU.add))
                    step(nc.vector.bn_stats(bn[:, t, 0:6], kept.h[:, t, :]))
                    step(nc.vector.bn_aggr(bn[:, t, 6:8], bn[:, t, 0:6]))
                nc.vector.tensor_scalar(st[:, 4, ts], bn[:, ts, 7], EPS, None, ALU.add).then_inc(var_ready, 1)
                dve.wait_ge(rstd_ready, 2 * hh + 2)
                for t in range(hh * HT, hh * HT + HT):
                    step(nc.vector.tensor_scalar(kept.x[:, t, :], kept.h[:, t, :], bn[:, t, 6:7], st[:, 4, t:t + 1], ALU.subtract, ALU.mult))

            dve.wait_ge(small_in, 32)
            for c in range(NCHUNK):
                gather(0, c)
                dve.wait_ge(w_in[c // W3], 16)
                if c == 0:
                    step(nc.vector.tensor_scalar(wbeta[:, :], w_raw[:, 0, :], gb[:, 1, 0:1], None, ALU.mult))
                else:
                    step(nc.vector.scalar_tensor_tensor(wbeta[:, :], w_raw[:, c, :], gb[:, 1, c:c + 1], wbeta[:, :], ALU.mult, ALU.add))
                if c == 4:
                    dve.wait_ge(squares, 2)
                    nc.vector.tensor_tensor(sq[0:64, :], sq[0:64, :], blk[0:64, :], ALU.add).then_inc(sq_ready, 1)
                    dve.wait_ge(sq_ready, 1)
                if 9 <= c < 9 + NB:
                    n = c - 9
                    w = min(512, XCOLS - 512 * n)
                    dve.wait_ge(blk_full, n + 1)
                    nc.vector.tensor_copy(blk[0:1, 512 * n:512 * n + w], blk_ps[n % 2][0:1, 0:w]).then_inc(blk_free, 1)
            gather(1, 0)
            gather(1, 1)
            dve.wait_ge(w_scaled, NCHUNK)
            nc.vector.tensor_reduce(wsum[:, :], w_gam[:, :, 0:D].rearrange("p c n -> p n c"), AX.X, ALU.add).then_inc(sums, 1)
            nc.vector.tensor_copy(bn[:, 0, 0:1], wbeta[:, 0:1]).then_inc(sums, 1)
            dve.wait_ge(blk_free, NB)
            g = blk[0:1, :].rearrange("p (b y x) -> p b y x", b=IMG, y=GRID)
            step(nc.vector.tensor_tensor(r2[:, :, :, :], g[:, :, :, 0:4], g[:, :, :, 5:9], ALU.add))
            step(nc.vector.tensor_tensor(r4[:, :, :, :], g[:, :, :, 4:8], g[:, :, :, 1:5], ALU.add))
            step(nc.vector.tensor_tensor(r4[:, :, :, :], r4[:, :, :, :], r2[:, :, :, :], ALU.add))
            step(nc.vector.tensor_tensor(ssq[:, :, :, :], r2[:, :, 0:4, :], r2[:, :, 5:9, :], ALU.add))
            for d in (0, 1, -1):
                step(nc.vector.tensor_tensor(ssq[:, :, :, :], ssq[:, :, :, :], r4[:, :, place(d):place(d) + 4, :], ALU.add))
            nc.vector.tensor_tensor(ssq[:, :, :, :], ssq[:, :, :, :], r4[:, :, place(2):place(2) + 4, :], ALU.add).then_inc(ssq_row, 1)
            dve.wait_ge(bc_full, 1)
            nc.vector.tensor_copy(cols[:, :], bc_ps[:, 0:D]).then_inc(sums, 1)
            step(nc.vector.tensor_tensor(bias[:, :], bias[:, :], bc_ps[:, D:2 * D], ALU.add))
            dve.wait_ge(sums, 3)
            dve.wait_ge(ssq_full, 1)
            step(nc.vector.tensor_scalar(st[:, 3, :], ssq_ps[:, 0:NT], 1.0 / PDIM, None, ALU.mult))
            for c in range(2, NCHUNK):
                gather(1, c)
                if c == 6:
                    finish(0)
            finish(1)


class Ring:

    def __init__(self, banks, full, free, plan):
        self.banks, self.fulls, self.frees = banks, full, free
        self.at = {name: n for n, name in enumerate(plan)}
        assert len(self.at) == len(plan)

    def bank(self, name):
        return self.banks[self.at[name] % len(self.banks)]

    def full(self, name):
        return self.fulls[self.at[name] % len(self.banks)]

    def free(self, name):
        return self.frees[self.at[name] % len(self.banks)]

    def wait_free(self, eng, name):
        n = self.at[name] // len(self.banks)
        if n:
            eng.wait_ge(self.free(name), n)

    def wait_full(self, eng, name):
        eng.wait_ge(self.full(name), self.at[name] // len(self.banks) + 1)

    def wait_read(self, eng, name):
        eng.wait_ge(self.free(name), self.at[name] // len(self.banks) + 1)


CI = 2 * D // P
NS = 16
RANK = 12
PAD = SEQ + 3


def mamba(nc, a, kept):
    ctx, sb, bank, sem = scope(nc)
    units = [(hh, d) for hh in range(2) for d in range(2)]
    with ctx:
        w_bm = sb("mam_bm_in_w", [HD2, 2, 2 * D])
        b_bm = sb("mam_bm_in_b", [HD2, 4])
        w_in = sb("mam_in_w", [HD2, 2, 4 * D])
        w_xp = sb("mam_xproj_w", [P, CI, 2 * NS + RANK])
        w_dt = sb("mam_dt_w", [44, 2 * D])
        w_out = sb("mam_out_w", [P, CI, D])
        w_bo = sb("mam_bm_out_w", [HD2, 2, D])
        cst = sb("mam_channel", [P, CI, 7 + NS])
        rows = sb("mam_rows", [P, 3, D])
        decay = sb("mam_decay", [P, CI, NS])
        pick = sb("mam_pick", [3 * 2 * NS, 2 * NS, P], BF16)
        ones_bf = sb("mam_ones", [3 * 2 * NS, P], BF16)
        xT = sb("mam_xT", [HD2, 2, HTOK])
        xd = sb("mam_xd", [HD2, 2, HTOK])
        xpad = sb("mam_xpad", [P, CI, HIMG, PAD])
        conv = sb("mam_conv", [P, CI, HTOK])
        u = sb("mam_u", [P, CI, HTOK])
        gate = [sb(f"mam_gate{d}", [P, CI, HTOK]) for d in range(2)]
        bc = sb("mam_bc", [44, HTOK])
        rest = sb("mam_rest", [2 * NS, HTOK])
        mid = sb("mam_mid", [2 * NS, HTOK], BF16)
        bc3 = sb("mam_bc3", [3 * 2 * NS, HTOK], BF16)
        dtx = sb("mam_dt_pre", [P, CI, HTOK])
        dte = sb("mam_dt_exp", [P, CI, HTOK])
        dt1 = sb("mam_dt_one", [P, CI, HTOK])
        dtl = sb("mam_dt_log", [P, CI, HTOK])
        dt = sb("mam_dt", [P, CI, HTOK])
        dtu = sb("mam_dtu", [P, CI, HTOK])
        b_sb = [sb(f"mam_b{i}", [P, HTOK]) for i in range(2)]
        da = [sb(f"mam_da{i}", [P, CI, HTOK]) for i in range(2)]
        dbu = [sb(f"mam_dbu{i}", [P, CI, HTOK]) for i in range(2)]
        state = sb("mam_state", [P, CI, HTOK])
        hc = [sb(f"mam_hc{i}", [P, CI, HTOK]) for i in range(2)]
        sumT = sb("mam_sumT", [HD2, 2, HTOK])
        res = sb("mam_res", [P, HT, D])
        bn = sb("mam_bn", [P, HT, 8])
        var = sb("mam_var", [P, 2, HT])
        half = sb("mam_neg_half", [P, 1])
        g_bank = [bank(f"mam_g{i}") for i in range(2)]
        b_bank = bank("mam_b_ps")
        c_bank = [bank(f"mam_c_ps{i}") for i in range(2)]
        y_bank = [bank(f"mam_y{i}") for i in range(3)]

        plan = []
        for hh in range(2):
            plan += [("xT", hh, m) for m in range(2)]
            for d in range(2):
                plan += [(n, hh, d, m) for n, k in (("xd", 2), ("c", CI), ("z", CI), ("proj", 1), ("dt", CI)) for m in range(k)]
            plan += [("sum", hh, m) for m in range(2)] + [("out", hh, t) for t in range(HT)]
        ring = Ring(g_bank, [sem(f"mam_g_full{i}") for i in range(2)], [sem(f"mam_g_free{i}") for i in range(2)], plan)
        w_sem = [sem(f"mam_w_in{i}") for i in range(4)]
        setup = sem("mam_setup")
        decay_ready = sem("mam_decay_ready")
        conv_ready, u_ready = sem("mam_conv_ready"), sem("mam_u_ready")
        bc_ready, exp_ready, one_ready, log_ready, dt_ready = (
            sem(f"mam_{n}_ready") for n in ("bc3", "dt_exp", "dt_one", "dt_log", "dt"))
        b_full, b_ready, c_full, da_ready, dbu_ready, scanned, hc_ready, hc_free = (
            sem(f"mam_{n}") for n in ("b_full", "b_ready", "c_full", "da_ready", "dbu_ready", "scanned", "hc_ready", "hc_free"))
        y_read, gated = sem("mam_y_read"), sem("mam_gated")
        var_ready, rstd_ready = sem("mam_var_ready"), sem("mam_rstd_ready")
        act_steps, dve_steps = sem("mam_act_steps"), sem("mam_dve_steps")
        block = ctx.enter_context(nc.Block())

        @block.sync
        def _(sp):
            for n, (dst, name) in enumerate(((w_bm[:, :, :], "mam_bm_in_w"), (b_bm[:, :], "mam_bm_in_b"), (w_in[:, :, :], "mam_in_w"),
                                             (cst[:, :, :], "mam_channel"))):
                sp.dma_start(dst, a[name]).then_inc(w_sem[0], 16)
            for dst, name in ((w_xp[:, :, :], "mam_xproj_w"), (w_dt[32:44, :], "mam_dt_w"), (w_out[:, :, :], "mam_out_w"),
                              (w_bo[:, :, :], "mam_bm_out_w")):
                sp.dma_start(dst, a[name]).then_inc(w_sem[1], 16)
            sp.dma_start(rows[:, :, :], a["mam_rows"].partition_broadcast(P)).then_inc(w_sem[2], 16)

        @block.gpsimd
        def _(pool):
            nc.gpsimd.memset(ones_bf[:, :], 1.0).then_inc(setup, 1)
            nc.gpsimd.memset(half[:, :], -0.5).then_inc(setup, 1)
            nc.gpsimd.memset(xpad[:, :, :, 0:3], 0.0).then_inc(setup, 1)
            for i in range(2):
                nc.gpsimd.memset(da[i][:, :, :].rearrange("p c (b t) -> p c b t", t=SEQ)[:, :, :, 0:1], 0.0).then_inc(setup, 1)
            pool.wait_ge(setup, 5)
            for n, (hh, d) in enumerate(units):
                pool.wait_ge(dt_ready, n + 1)

                def drive(s):
                    for j in range(2):
                        k = s + j
                        pool.wait_ge(b_ready, n * NS + k + 1)
                        pool.wait_ge(scanned, n * NS + k + 1)
                        nc.gpsimd.tensor_tensor(dbu[j][:, :, :], dtu[:, :, :], b_sb[j][:, :].unsqueeze(1).broadcast_to([P, CI, HTOK]),
                                                ALU.mult).then_inc(dbu_ready, 1)

                with pool.Fori(0, NS // 2) as i:
                    drive(i * 2)
                if d == 1:
                    for k in range(2):
                        pool.wait_ge(var_ready, 2 * hh + k + 1)
                        nc.gpsimd.tensor_tensor(var[:, k, :], var[:, k, :], half[:, 0:1].broadcast_to([P, HT]), ALU.pow).then_inc(rstd_ready, 1)

        @block.scalar
        def _(act):
            step = Steps(act, act_steps)
            act.wait_ge(w_sem[0], 64)
            step(nc.scalar.activation(decay[:, :, :], cst[:, :, 7:7 + NS], ACT.Exp))
            nc.scalar.mul(decay[:, :, :], decay[:, :, :], -1.0).then_inc(decay_ready, 1)
            act.wait_ge(decay_ready, 1)
            act.wait_ge(setup, 5)
            for n, (hh, d) in enumerate(units):
                if d == 0:
                    for m in range(2):
                        ring.wait_full(act, ("xT", hh, m))
                        nc.scalar.copy(xT[:, m, :], ring.bank(("xT", hh, m))[0:HD2, :]).then_inc(ring.free(("xT", hh, m)), 1)
                for m in range(2):
                    use = ("xd", hh, d, m)
                    ring.wait_full(act, use)
                    nc.scalar.activation(xd[:, m, :], ring.bank(use)[0:HD2, :], ACT.Identity,
                                         bias=b_bm[:, 2 * d + m:2 * d + m + 1]).then_inc(ring.free(use), 1)
                for c in range(CI):
                    use = ("c", hh, d, c)
                    ring.wait_full(act, use)
                    if c == 0 and n:
                        act.wait_ge(conv_ready, n)
                    x_t = xpad[:, c, :, 3:PAD] if d == 0 else xpad[:, c, :, PAD - 1:2:-1]
                    nc.scalar.copy(x_t, ring.bank(use)[:, :].rearrange("p (b t) -> p b t", t=SEQ)).then_inc(ring.free(use), 1)
                for c in range(CI):
                    use = ("z", hh, d, c)
                    ring.wait_full(act, use)
                    nc.scalar.activation(gate[d][:, c, :], ring.bank(use)[:, :], ACT.Silu).then_inc(ring.free(use), 1)
                act.wait_ge(conv_ready, n + 1)
                nc.scalar.activation(u[:, :, :], conv[:, :, :], ACT.Silu).then_inc(u_ready, 1)
                use = ("proj", hh, d, 0)
                ring.wait_full(act, use)
                nc.scalar.copy(bc[:, :], ring.bank(use)[0:44, :]).then_inc(ring.free(use), 1)
                for c in range(CI):
                    use = ("dt", hh, d, c)
                    ring.wait_full(act, use)
                    nc.scalar.activation(dtx[:, c, :], ring.bank(use)[:, :], ACT.Identity, bias=cst[:, c, 5:6]).then_inc(ring.free(use), 1)
                for c in range(CI):
                    ring.wait_read(act, ("dt", hh, d, c))
                step(nc.scalar.activation(dte[:, :, :], dtx[:, :, :], ACT.Abs))
                nc.scalar.activation(dte[:, :, :], dte[:, :, :], ACT.Exp, scale=-1.0).then_inc(exp_ready, 1)
                act.wait_ge(one_ready, n + 1)
                nc.scalar.activation(dtl[:, :, :], dt1[:, :, :], ACT.Ln).then_inc(log_ready, 1)
                act.wait_ge(dt_ready, n + 1)

                def decays(s):
                    for j in range(2):
                        k = s + j
                        act.wait_ge(b_full, n * NS + k + 1)
                        act.wait_ge(dbu_ready, n * NS + k + 1)
                        nc.scalar.copy(b_sb[j][:, :], b_bank[:, :]).then_inc(b_ready, 1)
                        act.wait_ge(scanned, n * NS + k + 1)
                        for c in range(CI):
                            t1 = dt[:, c, :].rearrange("p (b t) -> p b t", t=SEQ)[:, :, 1:SEQ]
                            o1 = da[j][:, c, :].rearrange("p (b t) -> p b t", t=SEQ)[:, :, 1:SEQ]
                            nc.scalar.activation(o1, t1, ACT.Exp, scale=decay[:, c, bass.ds(k, 1)]).then_inc(da_ready, 1)

                with act.Fori(0, NS // 2) as i:
                    decays(i * 2)
                if d == 1:
                    for m in range(2):
                        use = ("sum", hh, m)
                        ring.wait_full(act, use)
                        nc.scalar.copy(sumT[:, m, :], ring.bank(use)[0:HD2, :]).then_inc(ring.free(use), 1)

        @block.tensor
        def _(pe):
            for n, (hh, d) in enumerate(units):
                if d == 0:
                    if hh == 0:
                        pe.wait_ge(w_sem[0], 64)
                    for m in range(2):
                        use = ("xT", hh, m)
                        ring.wait_free(pe, use)
                        for t in range(HT):
                            mm = nc.tensor.transpose(ring.bank(use)[0:HD2, t * P:(t + 1) * P],
                                                     kept.x[:, hh * HT + t, m * HD2:(m + 1) * HD2], kept.ident[:, :])
                        mm.then_inc(ring.full(use), 1)
                    for m in range(2):
                        ring.wait_read(pe, ("xT", hh, m))
                for m in range(2):
                    use = ("xd", hh, d, m)
                    ring.wait_free(pe, use)
                    for k in range(2):
                        mm = nc.tensor.matmul(ring.bank(use)[0:HD2, :], w_bm[:, k, d * D + m * HD2:d * D + (m + 1) * HD2], xT[:, k, :],
                                              start=(k == 0), stop=(k == 1))
                    mm.then_inc(ring.full(use), 1)
                for m in range(2):
                    ring.wait_read(pe, ("xd", hh, d, m))
                for name, first in (("c", 0), ("z", CI)):
                    for c in range(CI):
                        use = (name, hh, d, c)
                        ring.wait_free(pe, use)
                        for k in range(2):
                            mm = nc.tensor.matmul(ring.bank(use)[:, :], w_in[:, k, (first + c) * P:(first + c + 1) * P], xd[:, k, :],
                                                  start=(k == 0), stop=(k == 1))
                        mm.then_inc(ring.full(use), 1)
                use = ("proj", hh, d, 0)
                ring.wait_free(pe, use)
                pe.wait_ge(u_ready, n + 1)
                pe.wait_ge(w_sem[1], 64)
                for k in range(CI):
                    mm = nc.tensor.matmul(ring.bank(use)[0:44, :], w_xp[:, k, :], u[:, k, :], start=(k == 0), stop=(k == CI - 1))
                mm.then_inc(ring.full(use), 1)
                ring.wait_read(pe, use)
                for c in range(CI):
                    use = ("dt", hh, d, c)
                    ring.wait_free(pe, use)
                    nc.tensor.matmul(ring.bank(use)[:, :], w_dt[32:44, c * P:(c + 1) * P], bc[32:44, :], start=True, stop=True).then_inc(ring.full(use), 1)
                pe.wait_ge(bc_ready, n + 1)
                if n:
                    pe.wait_ge(y_read, CI * n)

                def spread(k, j):
                    pe.wait_ge(b_ready, n * NS + k)
                    nc.tensor.matmul(b_bank[:, :], pick[:, bass.ds(k, 1), :].rearrange("p a b -> p (a b)"), bc3[:, :], start=True, stop=True).then_inc(b_full, 1)
                    pe.wait_ge(hc_ready, n * NS + k + 1)
                    nc.tensor.matmul(c_bank[j][:, :], pick[:, bass.ds(k + NS, 1), :].rearrange("p a b -> p (a b)"), bc3[:, :], start=True, stop=True).then_inc(c_full, 1)

                def add(k, j, first=False, last=False):
                    pe.wait_ge(hc_ready, n * NS + k + 3)
                    for c in range(CI):
                        mm = nc.tensor.matmul(y_bank[c][:, :], kept.ident[:, :], hc[j][:, c, :], start=first, stop=last)
                    mm.then_inc(hc_free, 1)

                spread(0, 0)
                spread(1, 1)
                add(0, 0, first=True)
                with pe.Fori(0, NS // 2 - 1) as i:
                    for j in range(2):
                        spread(i * 2 + 2 + j, j)
                        add(i * 2 + 1 + j, 1 - j)
                add(NS - 1, 1, last=True)
                if d == 1:
                    for m in range(2):
                        use = ("sum", hh, m)
                        ring.wait_free(pe, use)
                        pe.wait_ge(gated, 2 * CI * (hh + 1))
                        for e in range(2):
                            for k in range(CI):
                                mm = nc.tensor.matmul(ring.bank(use)[0:HD2, :], w_out[:, k, m * HD2:(m + 1) * HD2], gate[e][:, k, :],
                                                      start=(e == 0 and k == 0), stop=(e == 1 and k == CI - 1))
                        mm.then_inc(ring.full(use), 1)
                    for m in range(2):
                        ring.wait_read(pe, ("sum", hh, m))
                    for t in range(HT):
                        use = ("out", hh, t)
                        ring.wait_free(pe, use)
                        for k in range(2):
                            mm = nc.tensor.matmul(ring.bank(use)[:, 0:D], sumT[:, k, t * P:(t + 1) * P], w_bo[:, k, :], start=(k == 0), stop=(k == 1))
                        mm.then_inc(ring.full(use), 1)

        @block.vector
        def _(dve):
            step = Steps(dve, dve_steps)
            dve.wait_ge(setup, 5)
            for s in (scanned, hc_ready, hc_free, dbu_ready):
                dve.sem_inc(s, 2)
            step(nc.vector.tensor_tensor(pick[:, :, :], kept.pick_rows[0:96, :].unsqueeze(2).broadcast_to([96, 32, P]),
                                         ones_bf[:, :].unsqueeze(1).broadcast_to([96, 32, P]), ALU.mult))
            dve.wait_ge(w_sem[0], 64)
            dve.wait_ge(w_sem[2], 16)
            for n, (hh, d) in enumerate(units):
                for c in range(CI):
                    use = ("c", hh, d, c)
                    ring.wait_read(dve, use)
                    out = conv[:, c, :].rearrange("p (b t) -> p b t", t=SEQ)
                    if c == 0 and n:
                        dve.wait_ge(u_ready, n)
                    step(nc.vector.tensor_scalar(out, xpad[:, c, :, 0:SEQ], cst[:, c, 0:1], cst[:, c, 4:5], ALU.mult, ALU.add))
                    for k in range(1, 4):
                        ins = nc.vector.scalar_tensor_tensor(out, xpad[:, c, :, k:k + SEQ], cst[:, c, k:k + 1], out, ALU.mult, ALU.add)
                        if c == CI - 1 and k == 3:
                            ins.then_inc(conv_ready, 1)
                        else:
                            step(ins)
                use = ("proj", hh, d, 0)
                ring.wait_read(dve, use)
                step(nc.vector.tensor_copy(bc3[0:32, :], bc[0:32, :]))
                step(nc.vector.tensor_tensor(rest[:, :], bc[0:32, :], bc3[0:32, :], ALU.subtract))
                step(nc.vector.tensor_copy(mid[:, :], rest[:, :]))
                step(nc.vector.tensor_copy(bc3[32:64, :], mid[:, :]))
                step(nc.vector.tensor_tensor(rest[:, :], rest[:, :], mid[:, :], ALU.subtract))
                nc.vector.tensor_copy(bc3[64:96, :], rest[:, :]).then_inc(bc_ready, 1)
                dve.wait_ge(exp_ready, n + 1)
                nc.vector.tensor_scalar(dt1[:, :, :], dte[:, :, :], 1.0, None, ALU.add).then_inc(one_ready, 1)
                dve.wait_ge(one_ready, n + 1)
                step(nc.vector.scalar_tensor_tensor(dte[:, :, :], dt1[:, :, :], -1.0, dte[:, :, :], ALU.add, ALU.subtract))
                step(nc.vector.scalar_tensor_tensor(dte[:, :, :], dtx[:, :, :], 0.0, dte[:, :, :], ALU.max, ALU.subtract))
                dve.wait_ge(log_ready, n + 1)
                step(nc.vector.tensor_tensor(dt[:, :, :], dtl[:, :, :], dte[:, :, :], ALU.add))
                dve.wait_ge(u_ready, n + 1)
                nc.vector.tensor_tensor(dtu[:, :, :], dt[:, :, :], u[:, :, :], ALU.mult).then_inc(dt_ready, 1)

                def scan(s):
                    for j in range(2):
                        k = s + j
                        dve.wait_ge(da_ready, CI * (n * NS + k + 1))
                        dve.wait_ge(dbu_ready, n * NS + k + 3)
                        nc.vector.tensor_tensor_scan(state[:, :, :].rearrange("p c t -> p (c t)"), da[j][:, :, :].rearrange("p c t -> p (c t)"),
                                                     dbu[j][:, :, :].rearrange("p c t -> p (c t)"), 0.0, ALU.mult, ALU.add).then_inc(scanned, 1)
                        dve.wait_ge(scanned, n * NS + k + 3)
                        dve.wait_ge(c_full, n * NS + k + 1)
                        dve.wait_ge(hc_free, n * NS + k + 1)
                        nc.vector.tensor_tensor(hc[j][:, :, :], state[:, :, :], c_bank[j][:, :].unsqueeze(1).broadcast_to([P, CI, HTOK]),
                                                ALU.mult).then_inc(hc_ready, 1)
                        dve.wait_ge(hc_ready, n * NS + k + 3)

                with dve.Fori(0, NS // 2) as i:
                    scan(i * 2)
                dve.wait_ge(hc_free, n * NS + NS + 2)
                for c in range(CI):
                    use = ("z", hh, d, c)
                    ring.wait_read(dve, use)
                    nc.vector.scalar_tensor_tensor(conv[:, c, :], u[:, c, :], cst[:, c, 6:7], y_bank[c][:, :], ALU.mult, ALU.add).then_inc(y_read, 1)
                    dve.wait_ge(y_read, CI * n + c + 1)
                    y = conv[:, c, :].rearrange("p (b t) -> p b t", t=SEQ)
                    g = gate[d][:, c, :].rearrange("p (b t) -> p b t", t=SEQ)
                    nc.vector.tensor_tensor(g, g, y if d == 0 else y[:, :, ::-1], ALU.mult).then_inc(gated, 1)
                if d == 0:
                    continue
                hs, xs = kept.h[:, hh * HT:(hh + 1) * HT, :], kept.x[:, hh * HT:(hh + 1) * HT, :]
                wide = [rows[:, k:k + 1, :].broadcast_to([P, HT, D]) for k in range(3)]
                step(nc.vector.tensor_tensor(res[:, :, :], xs, wide[0], ALU.add))
                for t in range(HT):
                    use = ("out", hh, t)
                    ring.wait_full(dve, use)
                    nc.vector.tensor_tensor(res[:, t, :], res[:, t, :], ring.bank(use)[:, 0:D], ALU.add).then_inc(ring.free(use), 1)
                    ring.wait_read(dve, use)
                    step(nc.vector.bn_stats(bn[:, t, 0:6], res[:, t, :]))
                    step(nc.vector.bn_aggr(bn[:, t, 6:8], bn[:, t, 0:6]))
                nc.vector.tensor_scalar(var[:, 0, :], bn[:, :, 7], EPS, None, ALU.add).then_inc(var_ready, 1)
                dve.wait_ge(rstd_ready, 2 * hh + 1)
                for t in range(HT):
                    step(nc.vector.tensor_scalar(res[:, t, :], res[:, t, :], bn[:, t, 6:7], var[:, 0, t:t + 1], ALU.subtract, ALU.mult))
                step(nc.vector.tensor_tensor(res[:, :, :], res[:, :, :], wide[1], ALU.mult))
                step(nc.vector.tensor_tensor(res[:, :, :], res[:, :, :], wide[2], ALU.add))
                step(nc.vector.tensor_tensor(hs, hs, res[:, :, :], ALU.add))
                for t in range(HT):
                    step(nc.vector.bn_stats(bn[:, t, 0:6], hs[:, t, :]))
                    step(nc.vector.bn_aggr(bn[:, t, 6:8], bn[:, t, 0:6]))
                nc.vector.tensor_scalar(var[:, 1, :], bn[:, :, 7], EPS, None, ALU.add).then_inc(var_ready, 1)
                dve.wait_ge(rstd_ready, 2 * hh + 2)
                for t in range(HT):
                    step(nc.vector.tensor_scalar(xs[:, t, :], hs[:, t, :], bn[:, t, 6:7], var[:, 1, t:t + 1], ALU.subtract, ALU.mult))


SLOTS, F = 64, 768
FC = F // P
WR = 4


def need(eng, sem, value):
    if not isinstance(value, int) or value > 0:
        eng.wait_ge(sem, value)


def slot_experts(nc, a, kept):
    ctx, sb, bank, sem = scope(nc)
    with ctx:
        w1 = [sb(f"ffn_w1_{i}", [HD2 + 1, 2, F]) for i in range(WR)]
        w2 = [sb(f"ffn_w2_{i}", [P, FC, D]) for i in range(WR)]
        slots = sb("ffn_slots", [SLOTS, D])
        scale = sb("ffn_scale", [SLOTS, 1])
        b2 = sb("ffn_b2", [SLOTS, D])
        gain = sb("ffn_norm_w", [P, D])
        slT = sb("ffn_slT", [HD2, 2, SLOTS])
        xn = sb("ffn_xn", [P, NT, D])
        sqr = kept.n
        xnT = sb("ffn_xnT", [HD2, 2, TOK])
        st = sb("ffn_stats", [P, 8, NT])
        sst = sb("ffn_slot_stats", [SLOTS, 2])
        half = sb("ffn_neg_half", [P, 1])
        logit = sb("ffn_logit", [P, NT, SLOTS])
        comb = sb("ffn_combine", [P, NT, SLOTS])
        disp = sb("ffn_dispatch", [SLOTS, IMG, SEQ])
        dst = sb("ffn_dispatch_stats", [SLOTS, 2, IMG])
        disp_bd = [sb(f"ffn_dispatch_bd{i}", [P, TPI, SLOTS]) for i in range(2)]
        yT = sb("ffn_yT", [HD2 + 1, 2, SLOTS, IMG])
        ys = [sb(f"ffn_ys{i}", [HD2 + 1, 2, IMG]) for i in range(2)]
        g = [sb(f"ffn_g{i}", [IMG, F]) for i in range(2)]
        gT = [sb(f"ffn_gT{i}", [P, FC, IMG]) for i in range(2)]
        y2 = [sb(f"ffn_y2_{i}", [IMG, D]) for i in range(WR)]
        y2s = sb("ffn_y2s", [SLOTS, IMG, D])
        combT = sb("ffn_combT", [SLOTS, TOK])
        comb_bd = [sb(f"ffn_combine_bd{i}", [SLOTS, TPI, P]) for i in range(2)]
        bn = sb("ffn_bn", [P, NT, 8])
        big = [bank(f"ffn_big{i}", (P, 1024)) for i in range(2)]
        mid = [bank(f"ffn_mid{i}") for i in range(2)]
        low = [bank(f"ffn_low{i}") for i in range(2)]
        w1_in = [sem(f"ffn_w1_in{i}") for i in range(WR)]
        w2_in = [sem(f"ffn_w2_in{i}") for i in range(WR)]
        small_in = sem("ffn_small_in")
        y_out = [sem(f"ffn_y_out{i}") for i in range(WR)]
        y_in = [sem(f"ffn_y_in{i}") for i in range(2)]
        y_dram = nc.dram_tensor("ffn_y_scratch", [SLOTS, IMG, D], F32, kind="Internal").ap()
        setup = sem("ffn_setup")
        pow_asked, pow_done = sem("ffn_pow_asked"), sem("ffn_pow_done")
        pe_pre, dve_pre, act_pre = sem("ffn_pe_pre"), sem("ffn_dve_pre"), sem("ffn_act_pre")
        ys_ready, fc1_done, gelu_done, t_done, gT_ready, fc2_done, y2_ready = (
            sem(f"ffn_{n}") for n in ("ys_ready", "fc1_done", "gelu_done", "t_done", "gT_ready", "fc2_done", "y2_ready"))
        comb_bd_ready, comb_used, bd_ready, bd_used = (sem(f"ffn_{n}") for n in ("comb_bd_ready", "comb_used", "bd_ready", "bd_used"))
        yT_full, yT_ready, g_waited = sem("ffn_yT_full"), sem("ffn_yT_ready"), sem("ffn_g_waited")
        dve_steps = sem("ffn_dve_steps")
        block = ctx.enter_context(nc.Block())
        LOOPS = SLOTS // WR - 1

        @block.sync
        def _(sp):
            for dst_, name in ((slots[:, :], "ffn_slots"), (scale[:, :], "ffn_scale"), (b2[:, :], "ffn_b2")):
                sp.dma_start(dst_, a[name]).then_inc(small_in, 16)
            sp.dma_start(gain[:, :], a["ffn_norm_w"].partition_broadcast(P)).then_inc(small_in, 16)

            def load(i, c):
                n = i * WR + c
                need(sp, fc1_done, n - WR + 1)
                sp.dma_start(w1[c][0:HD2, :, :], a["ffn_w1"][bass.ds(n, 1), :, :].rearrange("s (p k) f -> p (s k) f", k=2)).then_inc(w1_in[c], 16)
                sp.dma_start(w1[c][HD2:HD2 + 1, 0, :], a["ffn_b1"][bass.ds(n, 1), :]).then_inc(w1_in[c], 16)
                need(sp, fc2_done, n - WR + 1)
                sp.dma_start(w2[c][:, :, :], a["ffn_w2"][bass.ds(n, 1), :, :].rearrange("s (p c) d -> p (s c) d", c=FC)).then_inc(w2_in[c], 16)

            def store(i, c):
                n = i * WR + c
                sp.wait_ge(y2_ready, n + 1)
                sp.dma_start(y_dram[bass.ds(n, 1), :, :].rearrange("s b d -> b (s d)"), y2[c][:, :]).then_inc(y_out[c], 16)

            for c in range(WR):
                load(0, c)
            with sp.Fori(0, LOOPS) as i:
                for c in range(WR):
                    load(i + 1, c)
                    store(i, c)
            for c in range(WR):
                store(LOOPS, c)
            for c in range(WR):
                sp.wait_ge(y_out[c], (LOOPS + 1) * 16)
            for k in range(2):
                sp.dma_start(y2s[:, k * HIMG:(k + 1) * HIMG, :], y_dram[:, k * HIMG:(k + 1) * HIMG, :]).then_inc(y_in[k], 16)

        @block.gpsimd
        def _(pool):
            nc.gpsimd.memset(half[:, :], -0.5).then_inc(setup, 1)
            pool.wait_ge(setup, 1)
            nc.gpsimd.memset(yT[HD2:HD2 + 1, :, :, :], 1.0).then_inc(setup, 1)
            for i in range(2):
                pool.wait_ge(setup, 2 + i)
                nc.gpsimd.memset(comb_bd[i][:, :, :], 0.0).then_inc(setup, 1)
            pool.wait_ge(setup, 4)
            for k, (t, n) in enumerate(((sst[:, 0:1], SLOTS), (st[:, 0, :], P), (st[:, 1, :], P), (st[:, 7, :], P))):
                pool.wait_ge(pow_asked, k + 1)
                width = t.shape[1]
                nc.gpsimd.tensor_tensor(t, t, half[0:n, 0:1].broadcast_to([n, width]), ALU.pow).then_inc(pow_done, 1)
                if k == 2:
                    pool.wait_ge(yT_ready, 2 * NT)

                    def stage(n, j):
                        need(pool, fc1_done, n - 1)
                        nc.gpsimd.tensor_copy(ys[j][:, :, :], yT[:, :, bass.ds(n, 1), :].rearrange("p k s b -> p (k s) b")).then_inc(ys_ready, 1)

                    stage(0, 0)
                    stage(1, 1)
                    with pool.Fori(0, SLOTS // 2 - 1) as i:
                        for j in range(2):
                            stage(i * 2 + 2 + j, j)

        @block.scalar
        def _(act):
            act.wait_ge(dve_pre, 5)
            nc.scalar.activation(comb[:, :, :], comb[:, :, :], ACT.Exp).then_inc(act_pre, 1)
            act.wait_ge(dve_pre, 6)
            nc.scalar.activation(disp[:, :, :], disp[:, :, :], ACT.Exp).then_inc(act_pre, 1)
            for t in range(NT):
                for m in range(2):
                    act.wait_ge(yT_full, 2 * t + m + 1)
                    out = yT[0:HD2, m, :, t * TPI:(t + 1) * TPI].rearrange("p s b -> p b s")
                    nc.scalar.copy(out, big[t % 2][0:HD2, m * 512:(m + 1) * 512].rearrange("p (b s) -> p b s", s=SLOTS)).then_inc(yT_ready, 1)

            def gelu(n, j):
                act.wait_ge(fc1_done, n + 1)
                need(act, t_done, n - 1)
                nc.scalar.activation(g[j][:, :], big[j][0:IMG, 0:F], ACT.Gelu).then_inc(gelu_done, 1)

            gelu(0, 0)
            gelu(1, 1)
            with act.Fori(0, SLOTS // 2 - 1) as i:
                for j in range(2):
                    gelu(i * 2 + 2 + j, j)

        @block.tensor
        def _(pe):
            pe.wait_ge(dve_pre, 1)
            for k in range(2):
                mm = nc.tensor.transpose(low[0][0:HD2, k * 64:(k + 1) * 64], slots[:, k:D:2], kept.ident[0:SLOTS, 0:SLOTS])
            mm.then_inc(pe_pre, 1)
            pe.wait_ge(dve_pre, 3)
            for k in range(2):
                for t in range(NT):
                    mm = nc.tensor.transpose(big[k][0:HD2, t * P:(t + 1) * P], xn[:, t, k:D:2], kept.ident[:, :])
                mm.then_inc(pe_pre, 1)
            pe.wait_ge(dve_pre, 4)
            for t in range(NT):
                for k in range(2):
                    mm = nc.tensor.matmul(low[1][:, t * SLOTS:(t + 1) * SLOTS], xnT[:, k, t * P:(t + 1) * P], slT[:, k, :], start=(k == 0), stop=(k == 1))
            mm.then_inc(pe_pre, 1)
            pe.wait_ge(dve_pre, 5)
            for t in range(NT):
                mm = nc.tensor.transpose(big[0][0:SLOTS, t * P:(t + 1) * P], logit[:, t, :], kept.ident[:, :])
            mm.then_inc(pe_pre, 1)
            pe.wait_ge(dve_pre, 7)
            for t in range(NT):
                mm = nc.tensor.transpose(big[1][0:SLOTS, t * P:(t + 1) * P], comb[:, t, :], kept.ident[:, :])
            mm.then_inc(pe_pre, 1)
            pe.wait_ge(dve_pre, 8)
            flat = disp[:, :, :].rearrange("p b t -> p (b t)")
            for t in range(NT):
                mm = nc.tensor.transpose(low[0][:, t * SLOTS:(t + 1) * SLOTS], flat[:, t * P:(t + 1) * P], kept.ident[0:SLOTS, 0:SLOTS])
            mm.then_inc(pe_pre, 1)
            pe.wait_ge(dve_pre, 9)
            for t in range(NT):
                pe.wait_ge(bd_ready, t + 1)
                if t >= 2:
                    pe.wait_ge(yT_ready, 2 * (t - 1))
                for m in range(2):
                    mm = nc.tensor.matmul(big[t % 2][0:HD2, m * 512:(m + 1) * 512], xn[:, t, m:D:2],
                                          disp_bd[t % 2][:, :, :].rearrange("p b s -> p (b s)"), start=True, stop=True)
                    mm.then_inc(yT_full, 1)
            pe.wait_ge(yT_ready, 2 * NT)

            def fc1(i, c):
                n, j = i * WR + c, c % 2
                need(pe, gelu_done, n - 1)
                pe.wait_ge(ys_ready, n + 1)
                pe.wait_ge(w1_in[c % WR], (i + c // WR + 1) * 32)
                for lo, hi in ((0, 512), (512, F)):
                    nc.tensor.matmul(big[j][0:IMG, lo:hi], ys[j][:, 0, :], w1[c % WR][:, 0, lo:hi], start=True, stop=False)
                    mm = nc.tensor.matmul(big[j][0:IMG, lo:hi], ys[j][0:HD2, 1, :], w1[c % WR][0:HD2, 1, lo:hi], start=False, stop=True)
                mm.then_inc(fc1_done, 1)

            def turn(i, c):
                n, j = i * WR + c, c % 2
                pe.wait_ge(gelu_done, n + 1)
                need(pe, gT_ready, n - 1)
                pe.sem_inc(g_waited, 1)
                for k in range(FC):
                    mm = nc.tensor.transpose(mid[j][:, k * IMG:(k + 1) * IMG], g[j][:, k:F:FC], kept.ident[0:IMG, 0:IMG])
                mm.then_inc(t_done, 1)

            def fc2(i, c):
                n, j = i * WR + c, c % 2
                pe.wait_ge(gT_ready, n + 1)
                need(pe, y2_ready, n - 1)
                pe.wait_ge(w2_in[c % WR], (i + c // WR + 1) * 16)
                for k in range(FC):
                    mm = nc.tensor.matmul(low[j][0:IMG, 0:D], gT[j][:, k, :], w2[c % WR][:, k, :], start=(k == 0), stop=(k == FC - 1))
                mm.then_inc(fc2_done, 1)

            for s in range(WR):
                fc1(0, s)
                if s >= 1:
                    turn(0, s - 1)
                if s >= 2:
                    fc2(0, s - 2)
            with pe.Fori(0, LOOPS) as i:
                for s in range(WR, 2 * WR):
                    fc1(i, s)
                    turn(i, s - 1)
                    fc2(i, s - 2)
            turn(LOOPS, WR - 1)
            fc2(LOOPS, WR - 2)
            fc2(LOOPS, WR - 1)
            for t in range(NT):
                if t % HT == 0:
                    pe.wait_ge(y_in[t // HT], 16)
                pe.wait_ge(comb_bd_ready, t + 1)
                if t >= 2:
                    pe.wait_ge(comb_used, t - 1)
                else:
                    pe.wait_ge(y2_ready, SLOTS)
                nc.tensor.matmul(low[t % 2][:, 0:D], combT[:, t * P:(t + 1) * P], b2[:, :], start=True, stop=False)
                for b in range(TPI):
                    mm = nc.tensor.matmul(low[t % 2][:, 0:D], comb_bd[t % 2][:, b, :], y2s[:, t * TPI + b, :], start=False, stop=(b == TPI - 1))
                mm.then_inc(pe_pre, 1)

        @block.vector
        def _(dve):
            step = Steps(dve, dve_steps)
            dve.wait_ge(small_in, 64)
            step(nc.vector.tensor_tensor(sqr[0:SLOTS, 0, :], slots[:, :], slots[:, :], ALU.mult))
            step(nc.vector.tensor_reduce(sst[:, 0:1], sqr[0:SLOTS, 0, :], AX.X, ALU.add))
            nc.vector.tensor_scalar(sst[:, 0:1], sst[:, 0:1], EPS * EPS, None, ALU.max).then_inc(pow_asked, 1)
            step(nc.vector.tensor_tensor(sqr[:, :, :], kept.x[:, :, :], kept.x[:, :, :], ALU.mult))
            step(nc.vector.tensor_reduce(st[:, 0, :], sqr[:, :, :], AX.X, ALU.add))
            nc.vector.tensor_scalar(st[:, 0, :], st[:, 0, :], 1.0 / D, EPS, ALU.mult, ALU.add).then_inc(pow_asked, 1)
            dve.wait_ge(pow_done, 1)
            nc.vector.tensor_scalar(slots[:, :], slots[:, :], sst[:, 0:1], scale[:, 0:1], ALU.mult, ALU.mult).then_inc(dve_pre, 1)
            dve.wait_ge(pow_done, 2)
            for t in range(NT):
                step(nc.vector.scalar_tensor_tensor(xn[:, t, :], kept.x[:, t, :], st[:, 0, t:t + 1], gain[:, :], ALU.mult, ALU.mult))
            dve.wait_ge(pe_pre, 1)
            nc.vector.tensor_copy(slT[:, :, :], low[0][0:HD2, 0:2 * SLOTS].rearrange("p (k s) -> p k s", k=2)).then_inc(dve_pre, 1)
            nc.vector.tensor_tensor(sqr[:, :, :], xn[:, :, :], xn[:, :, :], ALU.mult).then_inc(dve_pre, 1)
            dve.wait_ge(dve_pre, 3)
            step(nc.vector.tensor_reduce(st[:, 1, :], sqr[:, :, :], AX.X, ALU.add))
            nc.vector.tensor_scalar(st[:, 1, :], st[:, 1, :], EPS * EPS, None, ALU.max).then_inc(pow_asked, 1)
            dve.wait_ge(pe_pre, 3)
            step(nc.vector.tensor_copy(xnT[:, 0, :], big[0][0:HD2, :]))
            nc.vector.tensor_copy(xnT[:, 1, :], big[1][0:HD2, :]).then_inc(dve_pre, 1)
            dve.wait_ge(pow_done, 3)
            dve.wait_ge(pe_pre, 4)
            step(nc.vector.tensor_tensor(logit[:, :, :], low[1][:, :].rearrange("p (t s) -> p t s", s=SLOTS),
                                         st[:, 1, :].unsqueeze(2).broadcast_to([P, NT, SLOTS]), ALU.mult))
            step(nc.vector.tensor_reduce(st[:, 2, :], logit[:, :, :], AX.X, ALU.max))
            nc.vector.tensor_tensor(comb[:, :, :], logit[:, :, :], st[:, 2, :].unsqueeze(2).broadcast_to([P, NT, SLOTS]), ALU.subtract).then_inc(dve_pre, 1)
            dve.wait_ge(pe_pre, 5)
            lt = big[0][0:SLOTS, :].rearrange("p (b t) -> p b t", t=SEQ)
            step(nc.vector.tensor_reduce(dst[:, 0, :], lt, AX.X, ALU.max))
            nc.vector.tensor_tensor(disp[:, :, :], lt, dst[:, 0, :].unsqueeze(2).broadcast_to([SLOTS, IMG, SEQ]), ALU.subtract).then_inc(dve_pre, 1)
            dve.wait_ge(act_pre, 1)
            step(nc.vector.tensor_reduce(st[:, 3, :], comb[:, :, :], AX.X, ALU.add))
            step(nc.vector.reciprocal(st[:, 3, :], st[:, 3, :]))
            nc.vector.tensor_tensor(comb[:, :, :], comb[:, :, :], st[:, 3, :].unsqueeze(2).broadcast_to([P, NT, SLOTS]), ALU.mult).then_inc(dve_pre, 1)
            dve.wait_ge(act_pre, 2)
            step(nc.vector.tensor_reduce(dst[:, 1, :], disp[:, :, :], AX.X, ALU.add))
            step(nc.vector.reciprocal(dst[:, 1, :], dst[:, 1, :]))
            nc.vector.tensor_tensor(disp[:, :, :], disp[:, :, :], dst[:, 1, :].unsqueeze(2).broadcast_to([SLOTS, IMG, SEQ]), ALU.mult).then_inc(dve_pre, 1)
            dve.wait_ge(pe_pre, 6)
            nc.vector.tensor_copy(combT[:, :], big[1][0:SLOTS, :]).then_inc(dve_pre, 1)
            dve.wait_ge(pe_pre, 7)
            for t in range(NT):
                if t >= 2:
                    dve.wait_ge(yT_full, 2 * (t - 1))
                nc.vector.tensor_tensor(disp_bd[t % 2][:, :, :], low[0][:, t * SLOTS:(t + 1) * SLOTS].unsqueeze(1).broadcast_to([P, TPI, SLOTS]),
                                        kept.same_image[:, :].unsqueeze(2).broadcast_to([P, TPI, SLOTS]), ALU.mult).then_inc(bd_ready, 1)
            dve.wait_ge(bd_ready, NT)
            dve.wait_ge(setup, 4)

            def turned(i, c):
                n, j = i * WR + c, c % 2
                dve.wait_ge(t_done, n + 1)
                need(dve, fc2_done, n - 1)
                nc.vector.tensor_copy(gT[j][:, :, :], mid[j][:, 0:FC * IMG].rearrange("p (k b) -> p k b", b=IMG)).then_inc(gT_ready, 1)

            def output(i, c):
                n, j = i * WR + c, c % 2
                dve.wait_ge(fc2_done, n + 1)
                need(dve, y_out[c % WR], (i + c // WR) * 16)
                nc.vector.tensor_copy(y2[c % WR][:, :], low[j][0:IMG, 0:D]).then_inc(y2_ready, 1)

            for s in range(1, WR):
                turned(0, s - 1)
                if s >= 2:
                    output(0, s - 2)
            with dve.Fori(0, LOOPS) as i:
                for s in range(WR, 2 * WR):
                    turned(i, s - 1)
                    output(i, s - 2)
            turned(LOOPS, WR - 1)
            output(LOOPS, WR - 2)
            output(LOOPS, WR - 1)
            for t in range(NT):
                j = t % 2
                if t >= 2:
                    dve.wait_ge(pe_pre, 7 + t - 1)
                v = comb_bd[j][:, :, :].rearrange("p b t -> p (b t)")
                src = combT[:, t * P:(t + 1) * P].rearrange("p (b t) -> p b t", t=SEQ)
                nc.vector.tensor_copy(diagonal(comb_bd[j]), src).then_inc(comb_bd_ready, 1)
                if t >= 1:
                    finish_tile(nc, dve, step, t - 1, pe_pre, comb_used, low, kept, bn, st)
            finish_tile(nc, dve, step, NT - 1, pe_pre, comb_used, low, kept, bn, st)
            nc.vector.tensor_scalar(st[:, 7, :], bn[:, :, 7], EPS, None, ALU.add).then_inc(pow_asked, 1)
            dve.wait_ge(pow_done, 4)
            for t in range(NT):
                step(nc.vector.tensor_scalar(kept.x[:, t, :], kept.h[:, t, :], bn[:, t, 6:7], st[:, 7, t:t + 1], ALU.subtract, ALU.mult))


def diagonal(t):
    v = t[:, :, 0:SEQ]
    (ps, pn), (bs, bn), (ts, tn) = v.ap
    return bass.AP(v.tensor, v.offset, [[ps, pn], [bs + SEQ, bn], [ts, tn]])


def finish_tile(nc, dve, step, t, pe_pre, comb_used, low, kept, bn, st):
    dve.wait_ge(pe_pre, 7 + t + 1)
    nc.vector.tensor_tensor(kept.h[:, t, :], kept.h[:, t, :], low[t % 2][:, 0:D], ALU.add).then_inc(comb_used, 1)
    dve.wait_ge(comb_used, t + 1)
    step(nc.vector.bn_stats(bn[:, t, 0:6], kept.h[:, t, :]))
    step(nc.vector.bn_aggr(bn[:, t, 6:8], bn[:, t, 0:6]))


TAPS = 2 * SEQ - 1
L = 12


def position(nc, a, kept):
    ctx, sb, bank, sem = scope(nc)
    with ctx:
        w = sb("pos_w", [HD2, 2, TAPS, HD2])
        cols = sb("pos_cols", [HD2, 2])
        rows = sb("pos_rows", [P, 2, D])
        xT = sb("pos_xT", [HD2, 2, TOK])
        pT = sb("pos_pT", [HD2, 2, TOK])
        bn = sb("pos_bn", [P, NT, 8])
        var = sb("pos_var", [P, NT])
        half = sb("pos_neg_half", [P, 1])
        acc = [bank(f"pos_acc{i}") for i in range(4)]
        turn = [bank(f"pos_turn{i}") for i in range(2)]
        w_in = sem("pos_w_in")
        small_in = sem("pos_small_in")
        turned, xT_ready, conv_done, pos_ready, back_full, back_read = (
            sem(f"pos_{n}") for n in ("turned", "xT_ready", "conv_done", "gelu_done", "back_full", "back_read"))
        half_set, pow_asked, pow_done, dve_steps = (sem(f"pos_{n}") for n in ("half_set", "pow_asked", "pow_done", "dve_steps"))
        block = ctx.enter_context(nc.Block())

        @block.sync
        def _(sp):
            sp.dma_start(w[:, :, :, :], a["pos_w"]).then_inc(w_in, 16)
            sp.dma_start(cols[:, :], a["pos_b"]).then_inc(small_in, 16)
            sp.dma_start(rows[:, :, :], a["pos_rows"].partition_broadcast(P)).then_inc(small_in, 16)

        @block.gpsimd
        def _(pool):
            nc.gpsimd.memset(half[:, :], -0.5).then_inc(half_set, 1)
            pool.wait_ge(half_set, 1)
            pool.wait_ge(pow_asked, 1)
            nc.gpsimd.tensor_tensor(var[:, :], var[:, :], half[:, 0:1].broadcast_to([P, NT]), ALU.pow).then_inc(pow_done, 1)

        @block.scalar
        def _(act):
            act.wait_ge(small_in, 32)
            for n in range(4):
                hh, m = n // 2, n % 2
                act.wait_ge(conv_done, n + 1)
                nc.scalar.activation(pT[:, m, hh * HTOK:(hh + 1) * HTOK], acc[n][0:HD2, :], ACT.Gelu, bias=cols[:, m:m + 1]).then_inc(pos_ready, 1)

        @block.tensor
        def _(pe):
            for n in range(4):
                hh, m = n // 2, n % 2
                if n >= 2:
                    pe.wait_ge(xT_ready, n - 1)
                for t in range(HT):
                    mm = nc.tensor.transpose(turn[n % 2][0:HD2, t * P:(t + 1) * P], kept.x[:, hh * HT + t, m * HD2:(m + 1) * HD2], kept.ident[:, :])
                mm.then_inc(turned, 1)
            pe.wait_ge(w_in, 16)
            x = xT[:, :, :].rearrange("p m (b t) -> p m b t", t=SEQ)
            for n in range(4):
                hh, m = n // 2, n % 2
                pe.wait_ge(xT_ready, n + 1)
                out = acc[n][0:HD2, :].rearrange("p (b t) -> p b t", t=SEQ)
                order = sorted(range(-(SEQ - 1), SEQ), key=abs)
                for off in order:
                    lo, hi = max(0, -off), min(SEQ, SEQ - off)
                    mm = nc.tensor.matmul(out[:, :, lo:hi], w[:, m, off + SEQ - 1, :], x[:, m, hh * HIMG:(hh + 1) * HIMG, lo + off:hi + off],
                                          start=(off == 0), stop=(off == order[-1]), skip_group_check=True)
                mm.then_inc(conv_done, 1)
                if n == 3:
                    for t in range(NT):
                        pe.wait_ge(pos_ready, 2 * (t // HT + 1))
                        if t >= 2:
                            pe.wait_ge(back_read, t - 1)
                        for k in range(2):
                            mm = nc.tensor.transpose(turn[t % 2][:, k * HD2:(k + 1) * HD2], pT[:, k, t * P:(t + 1) * P], kept.ident[0:HD2, 0:HD2])
                        mm.then_inc(back_full, 1)

        @block.vector
        def _(dve):
            step = Steps(dve, dve_steps)
            for n in range(4):
                hh, m = n // 2, n % 2
                dve.wait_ge(turned, n + 1)
                nc.vector.tensor_copy(xT[:, m, hh * HTOK:(hh + 1) * HTOK], turn[n % 2][0:HD2, :]).then_inc(xT_ready, 1)
            for t in range(NT):
                dve.wait_ge(back_full, t + 1)
                nc.vector.tensor_tensor(kept.n[:, t, :], kept.x[:, t, :], turn[t % 2][:, 0:D], ALU.add).then_inc(back_read, 1)
                dve.wait_ge(back_read, t + 1)
                step(nc.vector.bn_stats(bn[:, t, 0:6], kept.n[:, t, :]))
                step(nc.vector.bn_aggr(bn[:, t, 6:8], bn[:, t, 0:6]))
            nc.vector.tensor_scalar(var[:, :], bn[:, :, 7], EPS, None, ALU.add).then_inc(pow_asked, 1)
            dve.wait_ge(pow_done, 1)
            for t in range(NT):
                step(nc.vector.tensor_scalar(kept.n[:, t, :], kept.n[:, t, :], bn[:, t, 6:7], var[:, t:t + 1], ALU.subtract, ALU.mult))
            dve.wait_ge(small_in, 32)
            step(nc.vector.tensor_tensor(kept.r[:, :, :], kept.n[:, :, :], rows[:, 0:1, :].broadcast_to([P, NT, D]), ALU.mult))
            step(nc.vector.tensor_tensor(kept.r[:, :, :], kept.r[:, :, :], rows[:, 1:2, :].broadcast_to([P, NT, D]), ALU.add))


class LoopRing(Ring):

    def __init__(self, banks, full, free, plan):
        super().__init__(banks, full, free, plan)
        assert len(plan) % len(banks) == 0
        self.per = len(plan) // len(banks)
        self.before = 0

    def count(self, i, name):
        return i * self.per + self.at[name] // len(self.banks)

    def wait_free(self, eng, name, i):
        eng.wait_ge(self.free(name), self.count(i, name))

    def wait_full(self, eng, name, i):
        eng.wait_ge(self.full(name), self.count(i, name) + 1)

    def wait_read(self, eng, name, i):
        eng.wait_ge(self.free(name), self.count(i, name) + 1)


HEADS = 12
HC = HEADS // 2
HU = HC // 2
NU = HT * 4
LAG_T, LAG_PV = 4, 5
PR = 8
PT = 4
SCALE = 0.25


def encoder(nc, a, kept):
    ctx, sb, bank, sem = scope(nc)
    with ctx:
        w_qkv = sb("enc_w_qkv", [HD2, 2, 3 * D])
        c_qk = sb("enc_c_qk", [HD2, 4])
        w_o = sb("enc_w_o", [HD2, 2, D])
        w_1 = sb("enc_w_1", [HD2, 2, F])
        w_2 = sb("enc_w_2", [P, FC, D])
        c_b = sb("enc_c_b", [HD2, 6])
        c_1 = sb("enc_c_1", [P, FC])
        rows = sb("enc_rows", [P, 6, D])
        c_n = sb("enc_c_n", [HD2, 4])
        hT = sb("enc_hT", [HD2, 2, 2, HTOK])
        h1T = sb("enc_h1T", [HD2, 2, 2, HTOK])
        qT = sb("enc_qT", [HD2, 2, HTOK])
        kT = sb("enc_kT", [HD2, 2, HTOK])
        kbd = sb("enc_kbd", [HD2, 2, HC, HTOK])
        vbd = [sb(f"enc_vbd{i}", [P, HT, 2, HC, HD2]) for i in range(2)]
        pr = [sb(f"enc_p{i}", [P, HU, P]) for i in range(PR)]
        mx = sb("enc_mx", [P, PR, HU])
        rs = sb("enc_rs", [P, PR, HU])
        pT = [sb(f"enc_pT{i}", [P, HU, P]) for i in range(PT)]
        oT = sb("enc_oT", [HD2, 2, HTOK])
        gT = sb("enc_gT", [P, 2, FC, HTOK])
        shift = sb("enc_shift", [P, D])
        other = sb("enc_other", [TPI, HU, P], BF16)
        mine = sb("enc_mine", [TPI, P], BF16)
        bn = sb("enc_bn", [P, NT, 8])
        var = sb("enc_var", [P, 4, HT])
        half = sb("enc_neg_half", [P, 1])
        ring = LoopRing([bank(f"enc_g{i}") for i in range(2)], [sem(f"enc_g_full{i}") for i in range(2)], [sem(f"enc_g_free{i}") for i in range(2)],
                        [(n, 0, k) for n, k in (("q", 0), ("k", 0), ("q", 1), ("k", 1))] + [("v", 0, t) for t in range(HT)]
                        + [("t2", 1, m) for m in range(2)]
                        + [(n, 1, k) for n, k in (("q", 0), ("k", 0), ("q", 1), ("k", 1))] + [("v", 1, t) for t in range(HT)]
                        + [("o", 0, t) for t in range(HT)] + [("t1", 0, m) for m in range(2)] + [("f", 0, m) for m in range(FC)]
                        + [("o", 1, t) for t in range(HT)] + [("g", 0, t) for t in range(HT)] + [("t1", 1, m) for m in range(2)]
                        + [("f", 1, m) for m in range(FC)] + [("t2", 0, m) for m in range(2)] + [("g", 1, t) for t in range(HT)])
        s_bank = [bank(f"enc_s{i}") for i in range(2)]
        t_bank = [bank(f"enc_t{i}") for i in range(2)]
        o_bank = [bank(f"enc_o{i}") for i in range(2)]
        a_in, b_in, n_in = (sem(f"enc_{n}_in") for n in ("attn_w", "rest_w", "norm_cols"))
        setup, mask_set, stats_waited = sem("enc_setup"), sem("enc_mask_set"), sem("enc_stats_waited")
        hT_ready, n_used, kbd_act, kbd_dve, s_full, sub_done, exp_done, recip_done, norm_done, t_full, pt_ready, pv_done = (
            sem(f"enc_{n}") for n in ("hT_ready", "n_used", "kbd_act", "kbd_dve", "s_full", "sub_done", "exp_done", "recip_done",
                                      "norm_done", "t_full", "pt_ready", "pv_done"))
        first_hT, oT_ready, n_ready, var_ready, rstd_ready, r_biased, r_ready = (
            sem(f"enc_{n}") for n in ("first_hT", "oT_ready", "n_ready", "var_ready", "rstd_ready", "r_biased", "r_ready"))
        shift_ready = sem("enc_shift_ready")
        dve_steps, pool_steps = sem("enc_dve_steps"), sem("enc_pool_steps")
        pe_first = sem("enc_first_turned")
        block = ctx.enter_context(nc.Block())

        def tiles(g):
            return slice(g * HT, (g + 1) * HT)

        @block.sync
        def _(sp):
            def attn_w(l):
                sp.dma_start(w_qkv[:, :, :], a["enc_w_qkv"][bass.ds(l, 1), :, :, :].rearrange("l p k n -> p (l k) n")).then_inc(a_in, 16)
                sp.dma_start(c_qk[:, :], a["enc_c_qk"][bass.ds(l, 1), :, :].rearrange("l p k -> p (l k)")).then_inc(a_in, 16)

            def rest_w(l):
                sp.dma_start(w_o[:, :, :], a["enc_w_o"][bass.ds(l, 1), :, :, :].rearrange("l p k n -> p (l k) n")).then_inc(b_in, 16)
                sp.dma_start(rows[:, :, :], a["enc_rows"][bass.ds(l, 1), :, :].partition_broadcast(P)).then_inc(b_in, 16)
                sp.dma_start(c_b[:, :], a["enc_c_b"][bass.ds(l, 1), :, :].rearrange("l p k -> p (l k)")).then_inc(b_in, 16)
                sp.dma_start(w_1[:, :, :], a["enc_w_1"][bass.ds(l, 1), :, :, :].rearrange("l p k n -> p (l k) n")).then_inc(b_in, 16)
                sp.dma_start(c_1[:, :], a["enc_c_1"][bass.ds(l, 1), :, :].rearrange("l p k -> p (l k)")).then_inc(b_in, 16)
                sp.dma_start(w_2[:, :, :], a["enc_w_2"][bass.ds(l, 1), :, :, :].rearrange("l p k n -> p (l k) n")).then_inc(b_in, 16)

            def norm_cols(l):
                sp.dma_start(c_n[:, :], a["enc_c_n"][bass.ds(l, 1), :, :].rearrange("l p k -> p (l k)")).then_inc(n_in, 16)

            norm_cols(0)
            attn_w(0)
            rest_w(0)
            with sp.Fori(0, L - 1) as l:
                sp.wait_ge(n_used, l + 1)
                norm_cols(l + 1)
                sp.wait_ge(sub_done, 2 * NU * (l + 1) + 2)
                attn_w(l + 1)
                sp.wait_ge(r_ready, 4 * (l + 1))
                rest_w(l + 1)
            sp.wait_ge(n_used, L)
            norm_cols(L)

        @block.gpsimd
        def _(pool):
            step = Steps(pool, pool_steps)
            for s, size in ((sub_done, 2), (pt_ready, 2), (pv_done, PT), (t_full, PR)):
                pool.sem_inc(s, size)
            nc.gpsimd.memset(half[:, :], -0.5).then_inc(setup, 1)
            for i in range(2):
                pool.wait_ge(setup, 1 + i)
                nc.gpsimd.memset(vbd[i][:, :, :, :, :], 0.0).then_inc(setup, 1)
            pool.wait_ge(setup, 3)
            per_layer = 4
            with pool.Fori(0, L) as l:
                step.enter(l, per_layer)

                def rstd(k):
                    pool.wait_ge(var_ready, 4 * l + k + 1)
                    nc.gpsimd.tensor_tensor(var[:, k, :], var[:, k, :], half[:, 0:1].broadcast_to([P, HT]), ALU.pow).then_inc(rstd_ready, 1)

                def normalise(g, u):
                    n = 2 * NU * l + g * NU + u
                    pool.wait_ge(recip_done, n + 1)
                    nc.gpsimd.tensor_tensor(pr[u % PR][:, :, :], pr[u % PR][:, :, :], rs[:, u % PR, :].unsqueeze(2).broadcast_to([P, HU, P]),
                                            ALU.mult).then_inc(norm_done, 1)

                def bias(g):
                    nc.gpsimd.tensor_tensor(kept.r[:, tiles(g), :], kept.r[:, tiles(g), :], rows[:, 0:1, :].broadcast_to([P, HT, D]), ALU.add).then_inc(r_biased, 1)

                def residual(g, k, second):
                    pool.wait_ge(n_ready, 4 * l + k + 1)
                    step(nc.gpsimd.tensor_tensor(kept.r[:, tiles(g), :], kept.n[:, tiles(g), :], rows[:, 4 if second else 1, :].unsqueeze(1).broadcast_to([P, HT, D]), ALU.mult))
                    add = rows[:, 5, :] if second else shift[:, :]
                    nc.gpsimd.tensor_tensor(kept.r[:, tiles(g), :], kept.r[:, tiles(g), :], add.unsqueeze(1).broadcast_to([P, HT, D]), ALU.add).then_inc(r_ready, 1)
                    pool.wait_ge(r_ready, 4 * l + k + 1)

                pool.wait_ge(b_in, 96 * (l + 1))
                nc.gpsimd.tensor_tensor(shift[:, :], rows[:, 2, :], rows[:, 3, :], ALU.add).then_inc(shift_ready, 1)
                pool.wait_ge(shift_ready, l + 1)
                for u in range(NU):
                    normalise(0, u)
                    if u == 8:
                        bias(0)
                    if u == 12:
                        bias(1)
                for u in range(NU):
                    normalise(1, u)
                    if u == 11:
                        rstd(0)
                residual(0, 0, False)
                rstd(1)
                residual(1, 1, False)
                rstd(2)
                residual(0, 2, True)
                rstd(3)
                residual(1, 3, True)
            step.leave(L)
            pool.wait_ge(var_ready, 4 * L + 1)
            nc.gpsimd.tensor_tensor(bn[:, :, 7], bn[:, :, 7], half[:, 0:1].broadcast_to([P, NT]), ALU.pow).then_inc(rstd_ready, 1)

        @block.scalar
        def _(act):
            act.wait_ge(n_in, 16)
            for m in range(2):
                act.wait_ge(pe_first, m + 1)
                nc.scalar.activation(hT[:, 0, m, :], o_bank[m][0:HD2, :], ACT.Identity, bias=c_n[:, 2 + m:3 + m], scale=c_n[:, m:m + 1]).then_inc(first_hT, 1)
            act.wait_ge(setup, 3)
            with act.Fori(0, L) as l:
                def qkv(g):
                    for k in range(2):
                        for name, dst, col in (("q", qT, k), ("k", kT, 2 + k)):
                            use = (name, g, k)
                            ring.wait_full(act, use, l)
                            nc.scalar.activation(dst[:, k, :], ring.bank(use)[0:HD2, :], ACT.Identity, bias=c_qk[:, col:col + 1]).then_inc(ring.free(use), 1)
                        if k == 0:
                            ring.wait_read(act, ("k", g, 0), l)
                            for h in range(HC):
                                nc.scalar.activation(kbd[:, 0, h, :], kT[:, 0, :], ACT.Copy, scale=kept.head_rows[:, h:h + 1]).then_inc(kbd_act, 1)
                    for t in range(HT):
                        use = ("v", g, t)
                        ring.wait_full(act, use, l)
                        nc.scalar.copy(own_columns(vbd[g], t), ring.bank(use)[:, 0:D].rearrange("p (c h d) -> p c h d", c=2, h=HC)).then_inc(ring.free(use), 1)

                def exponent(g, u):
                    act.wait_ge(sub_done, 2 * NU * l + g * NU + u + 1 + 2)
                    nc.scalar.activation(pr[u % PR][:, :, :], pr[u % PR][:, :, :], ACT.Exp, scale=SCALE).then_inc(exp_done, 1)

                def probs(g, u):
                    n = 2 * NU * l + g * NU + u
                    act.wait_ge(t_full, n + 1 + PR)
                    act.wait_ge(pv_done, n + 1)
                    nc.scalar.copy(pT[u % PT][:, :, :], t_bank[u % 2][:, 0:HU * P].rearrange("p (h t) -> p h t", h=HU)).then_inc(pt_ready, 1)

                def attended(g):
                    act.wait_ge(pv_done, 2 * NU * l + (g + 1) * NU + PT)
                    for m in range(2):
                        nc.scalar.activation(oT[:, m, :], o_bank[m][0:HD2, :], ACT.Identity, bias=c_b[:, m:m + 1]).then_inc(oT_ready, 1)

                def gain(use, dst, cols):
                    m = use[2]
                    ring.wait_full(act, use, l)
                    nc.scalar.activation(dst[:, use[1], m, :], ring.bank(use)[0:HD2, :], ACT.Identity,
                                         bias=cols[:, m + 2:m + 3], scale=cols[:, m:m + 1]).then_inc(ring.free(use), 1)

                def gelu(g, m):
                    use = ("f", g, m)
                    ring.wait_full(act, use, l)
                    nc.scalar.activation(gT[:, g, m, :], ring.bank(use)[:, :], ACT.Gelu, bias=c_1[:, m:m + 1]).then_inc(ring.free(use), 1)

                act.wait_ge(a_in, 32 * (l + 1))
                qkv(0)
                for u in range(NU):
                    exponent(0, u)
                    if u >= LAG_T:
                        probs(0, u - LAG_T)
                for m in range(2):
                    gain(("t2", 1, m), hT, c_n)
                for m in range(2):
                    ring.wait_read(act, ("t2", 1, m), l)
                act.sem_inc(n_used, 1)
                qkv(1)
                for u in range(NU - LAG_T, NU):
                    probs(0, u)
                act.wait_ge(b_in, 96 * (l + 1))
                attended(0)
                for u in range(NU):
                    exponent(1, u)
                    if u >= LAG_T:
                        probs(1, u - LAG_T)
                for m in range(2):
                    gain(("t1", 0, m), h1T, c_b[:, 2:6])
                for m in range(FC):
                    gelu(0, m)
                    if m == 2:
                        for u in range(NU - LAG_T, NU):
                            probs(1, u)
                attended(1)
                for m in range(2):
                    gain(("t1", 1, m), h1T, c_b[:, 2:6])
                for m in range(FC):
                    gelu(1, m)
                act.wait_ge(n_in, 16 * (l + 2))
                for m in range(2):
                    gain(("t2", 0, m), hT, c_n)

        @block.tensor
        def _(pe):
            for m in range(2):
                for t in range(HT):
                    mm = nc.tensor.transpose(o_bank[m][0:HD2, t * P:(t + 1) * P], kept.n[:, t, m * HD2:(m + 1) * HD2], kept.ident[:, :])
                mm.then_inc(pe_first, 1)
            pe.wait_ge(first_hT, 2)
            pe.wait_ge(mask_set, 2)
            with pe.Fori(0, L) as l:
                def qkv(g):
                    for k in range(2):
                        for name, first in (("q", 0), ("k", D)):
                            use = (name, g, k)
                            ring.wait_free(pe, use, l)
                            for j in range(2):
                                mm = nc.tensor.matmul(ring.bank(use)[0:HD2, :], w_qkv[:, j, first + k * HD2:first + (k + 1) * HD2], hT[:, g, j, :],
                                                      start=(j == 0), stop=(j == 1))
                            mm.then_inc(ring.full(use), 1)
                    for t in range(HT):
                        use = ("v", g, t)
                        ring.wait_free(pe, use, l)
                        for j in range(2):
                            mm = nc.tensor.matmul(ring.bank(use)[:, 0:D], hT[:, g, j, t * P:(t + 1) * P], w_qkv[:, j, 2 * D:3 * D],
                                                  start=(j == 0), stop=(j == 1))
                        mm.then_inc(ring.full(use), 1)

                def scores(g, u):
                    n = 2 * NU * l + g * NU + u
                    t, c, hf = u // 4, u // 2 % 2, u % 2
                    if u == 0:
                        ring.wait_read(pe, ("k", g, 1), l)
                        ring.wait_read(pe, ("q", g, 1), l)
                        pe.wait_ge(kbd_act, HC * (2 * l + g + 1))
                    if u == 2:
                        pe.wait_ge(kbd_dve, HC * (2 * l + g + 1))
                    pe.wait_ge(sub_done, n + 1)
                    out = s_bank[u % 2][:, 0:HU * P].rearrange("p (h t) -> p h t", h=HU)
                    nc.tensor.matmul(out, mine[:, :], other[:, :, :], start=True, stop=False)
                    nc.tensor.matmul(out, qT[:, c, t * P:(t + 1) * P], kbd[:, c, hf * HU:(hf + 1) * HU, t * P:(t + 1) * P],
                                     start=False, stop=True).then_inc(s_full, 1)

                def turn(g, u):
                    n = 2 * NU * l + g * NU + u
                    pe.wait_ge(norm_done, n + 1)
                    pe.wait_ge(pt_ready, n + 1)
                    for h in range(HU):
                        mm = nc.tensor.transpose(t_bank[u % 2][:, h * P:(h + 1) * P], pr[u % PR][:, h, :], kept.ident[:, :])
                    mm.then_inc(t_full, 1)

                def pv(g, u):
                    n = 2 * NU * l + g * NU + u
                    t, c, hf = u // 4, u // 2 % 2, u % 2
                    if u == 0:
                        ring.wait_read(pe, ("v", g, HT - 1), l)
                        ring.wait_read(pe, ("v", g, HT - 2), l)
                        pe.wait_ge(oT_ready, 2 * (2 * l + g))
                    pe.wait_ge(pt_ready, n + 1 + 2)
                    for h in range(HU):
                        mm = nc.tensor.matmul(o_bank[c][0:HD2, t * P:(t + 1) * P], vbd[g][:, t, c, hf * HU + h, :], pT[u % PT][:, h, :],
                                              start=(hf == 0 and h == 0), stop=(hf == 1 and h == HU - 1))
                    mm.then_inc(pv_done, 1)

                def unit_tail(g):
                    for u in range(NU - LAG_T, NU + 1):
                        if u < NU:
                            turn(g, u)
                        pv(g, u - 1)

                def units(g):
                    for u in range(NU):
                        scores(g, u)
                        if u >= LAG_T:
                            turn(g, u - LAG_T)
                        if u >= LAG_PV:
                            pv(g, u - LAG_PV)

                def turn_norm(name, g):
                    for m in range(2):
                        use = (name, g, m)
                        ring.wait_free(pe, use, l)
                        for t in range(HT):
                            mm = nc.tensor.transpose(ring.bank(use)[0:HD2, t * P:(t + 1) * P], kept.n[:, g * HT + t, m * HD2:(m + 1) * HD2], kept.ident[:, :])
                        mm.then_inc(ring.full(use), 1)

                def out_proj(g):
                    pe.wait_ge(oT_ready, 2 * (2 * l + g + 1))
                    for t in range(HT):
                        use = ("o", g, t)
                        ring.wait_free(pe, use, l)
                        for j in range(2):
                            mm = nc.tensor.matmul(ring.bank(use)[:, 0:D], oT[:, j, t * P:(t + 1) * P], w_o[:, j, :], start=(j == 0), stop=(j == 1))
                        mm.then_inc(ring.full(use), 1)

                def ffn_in(g, ms):
                    for m in ms:
                        use = ("f", g, m)
                        ring.wait_free(pe, use, l)
                        if m == 0:
                            for j in range(2):
                                ring.wait_read(pe, ("t1", g, j), l)
                        for j in range(2):
                            mm = nc.tensor.matmul(ring.bank(use)[:, :], w_1[:, j, m * P:(m + 1) * P], h1T[:, g, j, :], start=(j == 0), stop=(j == 1))
                        mm.then_inc(ring.full(use), 1)

                def ffn_out(g):
                    for m in (FC - 2, FC - 1):
                        ring.wait_read(pe, ("f", g, m), l)
                    for t in range(HT):
                        use = ("g", g, t)
                        ring.wait_free(pe, use, l)
                        for m in range(FC):
                            mm = nc.tensor.matmul(ring.bank(use)[:, 0:D], gT[:, g, m, t * P:(t + 1) * P], w_2[:, m, :], start=(m == 0), stop=(m == FC - 1))
                        mm.then_inc(ring.full(use), 1)

                pe.wait_ge(a_in, 32 * (l + 1))
                qkv(0)
                units(0)
                pe.wait_ge(n_ready, 4 * l)
                turn_norm("t2", 1)
                for m in range(2):
                    ring.wait_read(pe, ("t2", 1, m), l)
                qkv(1)
                unit_tail(0)
                pe.wait_ge(b_in, 96 * (l + 1))
                out_proj(0)
                units(1)
                pe.wait_ge(n_ready, 4 * l + 1)
                turn_norm("t1", 0)
                ffn_in(0, range(3))
                unit_tail(1)
                ffn_in(0, range(3, FC))
                out_proj(1)
                ffn_out(0)
                pe.wait_ge(n_ready, 4 * l + 2)
                turn_norm("t1", 1)
                ffn_in(1, range(FC))
                pe.wait_ge(n_ready, 4 * l + 3)
                turn_norm("t2", 0)
                ffn_out(1)
                for m in range(2):
                    ring.wait_read(pe, ("t2", 0, m), l)

        @block.vector
        def _(dve):
            step = Steps(dve, dve_steps)
            nc.vector.tensor_copy(mine[:, :], kept.image_rows[:, :]).then_inc(mask_set, 1)
            nc.vector.tensor_scalar(other[:, :, :], kept.image_rows[:, :].unsqueeze(1).broadcast_to([TPI, HU, P]), -1.0, BIG,
                                    ALU.add, ALU.mult).then_inc(mask_set, 1)
            with dve.Fori(0, L) as l:
                step.enter(l, DVE_STEPS)

                def masked_k(g):
                    ring.wait_read(dve, ("k", g, 1), l)
                    for h in range(HC):
                        nc.vector.tensor_scalar(kbd[:, 1, h, :], kT[:, 1, :], kept.head_rows[:, h:h + 1], None, ALU.mult).then_inc(kbd_dve, 1)

                def shifted(g, u):
                    n = 2 * NU * l + g * NU + u
                    sc = s_bank[u % 2][:, 0:HU * P].rearrange("p (h t) -> p h t", h=HU)
                    dve.wait_ge(s_full, n + 1)
                    step(nc.vector.tensor_reduce(mx[:, u % PR, :], sc, AX.X, ALU.max))
                    dve.wait_ge(t_full, n + 1)
                    nc.vector.tensor_tensor(pr[u % PR][:, :, :], sc, mx[:, u % PR, :].unsqueeze(2).broadcast_to([P, HU, P]),
                                            ALU.subtract).then_inc(sub_done, 1)

                def totals(g, u):
                    dve.wait_ge(exp_done, 2 * NU * l + g * NU + u + 1)
                    step(nc.vector.tensor_reduce(rs[:, u % PR, :], pr[u % PR][:, :, :], AX.X, ALU.add))
                    nc.vector.reciprocal(rs[:, u % PR, :], rs[:, u % PR, :]).then_inc(recip_done, 1)

                def norm_tile(name, g, t):
                    use, a_t = (name, g, t), g * HT + t
                    ring.wait_full(dve, use, l)
                    nc.vector.tensor_tensor(kept.n[:, a_t, :], kept.r[:, a_t, :], ring.bank(use)[:, 0:D], ALU.add).then_inc(ring.free(use), 1)
                    ring.wait_read(dve, use, l)
                    step(nc.vector.bn_stats(bn[:, a_t, 0:6], kept.n[:, a_t, :]))
                    dve.sem_inc(stats_waited, 1)
                    step(nc.vector.bn_aggr(bn[:, a_t, 6:8], bn[:, a_t, 0:6]))

                def norm_var(g, k):
                    nc.vector.tensor_scalar(var[:, k, :], bn[:, tiles(g), 7], EPS, None, ALU.add).then_inc(var_ready, 1)

                def norm_end(g, k):
                    dve.wait_ge(rstd_ready, 4 * l + k + 1)
                    for t in range(HT):
                        a_t = g * HT + t
                        ins = nc.vector.tensor_scalar(kept.n[:, a_t, :], kept.n[:, a_t, :], bn[:, a_t, 6:7], var[:, k, t:t + 1], ALU.subtract, ALU.mult)
                        if t == HT - 1:
                            ins.then_inc(n_ready, 1)
                        else:
                            step(ins)

                def norm(name, g, k):
                    for t in range(HT):
                        norm_tile(name, g, t)
                    norm_var(g, k)
                    norm_end(g, k)

                masked_k(0)
                for u in range(NU):
                    shifted(0, u)
                    if u >= 2:
                        totals(0, u - 2)
                totals(0, NU - 2)
                totals(0, NU - 1)
                masked_k(1)
                dve.wait_ge(r_biased, 2 * l + 2)
                norm_tile("o", 0, 0)
                norm_tile("o", 0, 1)
                for u in range(NU):
                    shifted(1, u)
                    if u >= 2:
                        totals(1, u - 2)
                    if u in (2, 5):
                        norm_tile("o", 0, 2 if u == 2 else 3)
                    if u == 13:
                        norm_var(0, 0)
                totals(1, NU - 2)
                totals(1, NU - 1)
                norm_end(0, 0)
                norm("o", 1, 1)
                dve.wait_ge(r_ready, 4 * l + 1)
                norm("g", 0, 2)
                dve.wait_ge(r_ready, 4 * l + 2)
                norm("g", 1, 3)
            step.leave(L)
            dve.wait_ge(r_ready, 4 * L)
            step(nc.vector.tensor_tensor(kept.h[:, :, :], kept.h[:, :, :], kept.r[:, :, :], ALU.add))
            for t in range(NT):
                step(nc.vector.bn_stats(bn[:, t, 0:6], kept.h[:, t, :]))
                step(nc.vector.bn_aggr(bn[:, t, 6:8], bn[:, t, 0:6]))
            nc.vector.tensor_scalar(bn[:, :, 7], bn[:, :, 7], EPS, None, ALU.add).then_inc(var_ready, 1)
            dve.wait_ge(rstd_ready, 4 * L + 1)
            for t in range(NT):
                step(nc.vector.tensor_scalar(kept.x[:, t, :], kept.h[:, t, :], bn[:, t, 6:7], bn[:, t, 7:8], ALU.subtract, ALU.mult))


DVE_STEPS = 2 * NU * 2 + 2 * HT * 2 * 2 + 4 * (HT - 1)


def own_columns(v, t):
    w = v[:, t, :, :, 0:D // HEADS]
    (ps, pn), (cs, cn), (hs, hn), (ds, dn) = w.ap
    return bass.AP(w.tensor, w.offset, [[ps, pn], [cs, cn], [hs + D // HEADS, hn], [ds, dn]])


E = 16
RMS_EPS = 1e-6


def experts(nc, a, kept):
    ctx, sb, bank, sem = scope(nc)
    with ctx:
        w_i = [sb(f"moe_wi{i}", [HD2, 2, F]) for i in range(2)]
        w_o = [sb(f"moe_wo{i}", [P, FC, D]) for i in range(2)]
        gain = sb("moe_ln_w", [P, D])
        w_r = sb("moe_w_router", [HD2, 2, E])
        rank = sb("moe_rank", [P, E])
        sqr = sb("moe_sqr", [P, NT, D])
        ms = sb("moe_ms", [P, NT])
        half = sb("moe_neg_half", [P, 1])
        nT = sb("moe_normedT", [HD2, 2, TOK])
        pe_ = sb("moe_p", [P, NT, E])
        first = sb("moe_first", [P, NT, E])
        st = sb("moe_stats", [P, 3, NT])
        hT = [sb(f"moe_hT{i}", [P, FC, HTOK]) for i in range(2)]
        f_bank = [bank(f"moe_f{i}") for i in range(4)]
        o_bank = [bank(f"moe_o{i}") for i in range(2)]
        t_bank = [bank(f"moe_t{i}") for i in range(2)]
        small_in = sem("moe_small_in")
        wi_in = [sem(f"moe_wi_in{i}") for i in range(2)]
        wo_in = [sem(f"moe_wo_in{i}") for i in range(2)]
        half_set, pow_asked, pow_done = sem("moe_half_set"), sem("moe_pow_asked"), sem("moe_pow_done")
        turned, nT_ready, logits_done, exp_asked, exp_done = (
            sem(f"moe_{n}") for n in ("turned", "nT_ready", "logits_done", "exp_asked", "exp_done"))
        f_full, f_read, o_full, o_read = (sem(f"moe_{n}") for n in ("f_full", "f_read", "o_full", "o_read"))
        dve_steps = sem("moe_dve_steps")
        block = ctx.enter_context(nc.Block())
        PAIRS = E // 2

        @block.sync
        def _(sp):
            sp.dma_start(gain[:, :], a["moe_ln_w"].partition_broadcast(P)).then_inc(small_in, 16)
            sp.dma_start(w_r[:, :, :], a["moe_w_router"]).then_inc(small_in, 16)
            sp.dma_start(rank[:, :], a["moe_rank"].partition_broadcast(P)).then_inc(small_in, 16)

            def load(i, j, first=False):
                e = i * 2 + j
                need(sp, f_full, 0 if first else (e - 1) * 2 * FC)
                sp.dma_start(w_i[j][:, :, :], a["moe_wi"][bass.ds(e, 1), :, :, :].rearrange("e p k f -> (e p) k f")).then_inc(wi_in[j], 16)
                need(sp, o_full, 0 if first else (e - 1) * 2 * HT + HT)
                sp.dma_start(w_o[j][:, :, :], a["moe_wo"][bass.ds(e, 1), :, :, :].rearrange("e p c d -> (e p) c d")).then_inc(wo_in[j], 16)

            for j in range(2):
                load(0, j, first=True)
            with sp.Fori(0, PAIRS - 1) as i:
                load(i + 1, 0)
                load(i + 1, 1)

        @block.gpsimd
        def _(pool):
            nc.gpsimd.memset(half[:, :], -0.5).then_inc(half_set, 1)
            pool.wait_ge(half_set, 1)
            pool.wait_ge(pow_asked, 1)
            nc.gpsimd.tensor_tensor(ms[:, :], ms[:, :], half[:, 0:1].broadcast_to([P, NT]), ALU.pow).then_inc(pow_done, 1)

        @block.scalar
        def _(act):
            act.wait_ge(exp_asked, 1)
            nc.scalar.activation(pe_[:, :, :], pe_[:, :, :], ACT.Exp).then_inc(exp_done, 1)

            def relu(i, j, hh):
                e2 = (i * 2 + j) * 2 + hh
                act.wait_ge(o_full, e2 * HT)
                for m in range(FC):
                    n = e2 * FC + m
                    act.wait_ge(f_full, n + 1)
                    nc.scalar.activation(hT[hh][:, m, :], f_bank[(hh * FC + m) % 4][:, :], ACT.Relu).then_inc(f_read, 1)

            with act.Fori(0, PAIRS) as i:
                for j in range(2):
                    for hh in range(2):
                        relu(i, j, hh)

        @block.tensor
        def _(pe):
            pe.sem_inc(o_full, HT)
            for n in range(4):
                hh, k = n // 2, n % 2
                if k == 0:
                    pe.wait_ge(pow_asked, 2 + hh)
                if n >= 2:
                    pe.wait_ge(nT_ready, n - 1)
                for t in range(HT):
                    mm = nc.tensor.transpose(t_bank[n % 2][0:HD2, t * P:(t + 1) * P], kept.n[:, hh * HT + t, k * HD2:(k + 1) * HD2], kept.ident[:, :])
                mm.then_inc(turned, 1)
            pe.wait_ge(nT_ready, 4)
            pe.wait_ge(small_in, 48)
            for t in range(NT):
                for k in range(2):
                    mm = nc.tensor.matmul(o_bank[1][:, t * E:(t + 1) * E], nT[:, k, t * P:(t + 1) * P], w_r[:, k, :], start=(k == 0), stop=(k == 1))
            mm.then_inc(logits_done, 1)

            def fc1(i, j, hh):
                pe.wait_ge(wi_in[j], (i + 1) * 16)
                for m in range(FC):
                    n = ((i * 2 + j) * 2 + hh) * FC + m
                    need(pe, f_read, n - 3)
                    for k in range(2):
                        mm = nc.tensor.matmul(f_bank[(hh * FC + m) % 4][:, :], w_i[j][:, k, m * P:(m + 1) * P], nT[:, k, hh * HTOK:(hh + 1) * HTOK],
                                              start=(k == 0), stop=(k == 1))
                    mm.then_inc(f_full, 1)

            def fc2(i, j, hh):
                pe.wait_ge(wo_in[j], (i + 1) * 16)
                e2 = (i * 2 + j) * 2 + hh
                pe.wait_ge(f_read, (e2 + 1) * FC)
                for t in range(HT):
                    pe.wait_ge(o_read, e2 * HT + t + 1)
                    for m in range(FC):
                        mm = nc.tensor.matmul(o_bank[t % 2][:, 0:D], hT[hh][:, m, t * P:(t + 1) * P], w_o[j][:, m, :], start=(m == 0), stop=(m == FC - 1))
                    mm.then_inc(o_full, 1)

            fc1(0, 0, 0)
            pe.wait_ge(exp_asked, 1)
            with pe.Fori(0, PAIRS - 1) as i:
                for j in range(2):
                    fc1(i, j, 1)
                    fc2(i, j, 0)
                    fc1(i + j, 1 - j, 0)
                    fc2(i, j, 1)
            fc1(PAIRS - 1, 0, 1)
            fc2(PAIRS - 1, 0, 0)
            fc1(PAIRS - 1, 1, 0)
            fc2(PAIRS - 1, 0, 1)
            fc1(PAIRS - 1, 1, 1)
            fc2(PAIRS - 1, 1, 0)
            fc2(PAIRS - 1, 1, 1)

        @block.vector
        def _(dve):
            step = Steps(dve, dve_steps)
            dve.sem_inc(o_read, 2)
            step(nc.vector.tensor_tensor(sqr[:, :, :], kept.x[:, :, :], kept.x[:, :, :], ALU.mult))
            step(nc.vector.tensor_reduce(ms[:, :], sqr[:, :, :], AX.X, ALU.add))
            nc.vector.tensor_scalar(ms[:, :], ms[:, :], 1.0 / D, RMS_EPS, ALU.mult, ALU.add).then_inc(pow_asked, 1)
            dve.wait_ge(small_in, 48)
            dve.wait_ge(pow_done, 1)
            for t in range(NT):
                ins = nc.vector.scalar_tensor_tensor(kept.n[:, t, :], kept.x[:, t, :], ms[:, t:t + 1], gain[:, :], ALU.mult, ALU.mult)
                if t % HT == HT - 1:
                    ins.then_inc(pow_asked, 1)
                else:
                    step(ins)
            for n in range(4):
                hh, k = n // 2, n % 2
                dve.wait_ge(turned, n + 1)
                nc.vector.tensor_copy(nT[:, k, hh * HTOK:(hh + 1) * HTOK], t_bank[n % 2][0:HD2, :]).then_inc(nT_ready, 1)
            step(nc.vector.tensor_tensor(kept.h[:, :, :], kept.h[:, :, :], kept.x[:, :, :], ALU.add))
            dve.wait_ge(logits_done, 1)
            lg = o_bank[1][:, 0:NT * E].rearrange("p (t e) -> p t e", e=E)
            each = [P, NT, E]
            step(nc.vector.tensor_reduce(st[:, 0, :], lg, AX.X, ALU.max))
            nc.vector.tensor_tensor(pe_[:, :, :], lg, st[:, 0, :].unsqueeze(2).broadcast_to(each), ALU.subtract).then_inc(exp_asked, 1)
            dve.wait_ge(exp_done, 1)
            step(nc.vector.tensor_reduce(st[:, 1, :], pe_[:, :, :], AX.X, ALU.add))
            step(nc.vector.reciprocal(st[:, 1, :], st[:, 1, :]))
            step(nc.vector.tensor_reduce(st[:, 0, :], pe_[:, :, :], AX.X, ALU.max))
            step(nc.vector.tensor_tensor(st[:, 1, :], st[:, 0, :], st[:, 1, :], ALU.mult))
            step(nc.vector.tensor_tensor(first[:, :, :], pe_[:, :, :], st[:, 0, :].unsqueeze(2).broadcast_to(each), ALU.is_equal))
            step(nc.vector.tensor_tensor(first[:, :, :], first[:, :, :], rank[:, :].unsqueeze(1).broadcast_to(each), ALU.mult))
            step(nc.vector.tensor_reduce(st[:, 2, :], first[:, :, :], AX.X, ALU.max))
            step(nc.vector.tensor_tensor(first[:, :, :], first[:, :, :], st[:, 2, :].unsqueeze(2).broadcast_to(each), ALU.is_equal))
            step(nc.vector.tensor_tensor(first[:, :, :], first[:, :, :], st[:, 1, :].unsqueeze(2).broadcast_to(each), ALU.mult))

            with dve.Fori(0, PAIRS) as i:
                for j in range(2):
                    for hh in range(2):
                        for t in range(HT):
                            n = ((i * 2 + j) * 2 + hh) * HT + t
                            a_t = hh * HT + t
                            dve.wait_ge(o_full, n + 1 + HT)
                            nc.vector.scalar_tensor_tensor(kept.h[:, a_t, :], o_bank[t % 2][:, 0:D], first[:, a_t, bass.ds(i * 2 + j, 1)],
                                                           kept.h[:, a_t, :], ALU.mult, ALU.add).then_inc(o_read, 1)
                            if a_t == NT - 1:
                                dve.wait_ge(o_read, n + 1 + 2)



CONSTANTS = {"ident": (P, P), "pick_rows": (HD2, 2 * NS), "same_image": (P, TPI), "head_rows": (HD2, HC), "image_rows": (TPI, P)}


class Kept:
    pass


def build(nc, a, out):
    with ExitStack() as ctx:
        kept = Kept()
        kept.h, kept.x, kept.n, kept.r = (ctx.enter_context(nc.sbuf_tensor("s_kept_" + n, [P, NT, D], F32)) for n in "hxnr")
        const = {name: ctx.enter_context(nc.sbuf_tensor("s_kept_" + name, list(shape), F32)) for name, shape in CONSTANTS.items()}
        kept.ident, kept.pick_rows, kept.same_image, kept.head_rows, kept.image_rows = const.values()
        const_in = ctx.enter_context(nc.semaphore("const_in"))
        stored = ctx.enter_context(nc.semaphore("out_stored"))
        with nc.Block() as block:
            @block.sync
            def _(sp):
                for name, tile in const.items():
                    sp.dma_start(tile[:, :], a[name]).then_inc(const_in, 16)
                sp.wait_ge(const_in, 16 * len(const))
        tokenize(nc, a, kept)
        mamba(nc, a, kept)
        slot_experts(nc, a, kept)
        position(nc, a, kept)
        encoder(nc, a, kept)
        experts(nc, a, kept)
        with nc.Block() as block:
            @block.sync
            def _(sp):
                sp.dma_start(out.rearrange("(t b) n d -> (b n) t d", t=NT), kept.h[:, :, :]).then_inc(stored, 16)
                sp.wait_ge(stored, 16)



def lay_out(v):
    v = {k: np.asarray(x) for k, x in v.items()}
    o = {}
    stack = lambda fn: np.ascontiguousarray(np.stack([fn(layer) for layer in range(L)]))

    def by_rows(w, rows=HD2):
        return np.ascontiguousarray(w.reshape(-1, rows, w.shape[1]).transpose(1, 0, 2))

    def column(b, rows=HD2):
        return np.ascontiguousarray(b.reshape(-1, rows).T)

    n = SIDE // BLK
    blocks = v["x"].reshape(IMG, CH, n, BLK, n, BLK).transpose(1, 3, 5, 0, 2, 4)
    grid = np.zeros((CH, BLK, BLK, IMG, GRID, GRID), blocks.dtype)
    at = [i // 2 + (GRID // 2 + 1) * (i % 2) for i in range(n)]
    grid[..., np.ix_(at, at)[0], np.ix_(at, at)[1]] = blocks
    o["x_grid01"] = np.ascontiguousarray(grid[0:2].reshape(P, XCOLS))
    o["x_grid2"] = np.pad(grid[2].reshape(P // 2, XCOLS), ((0, 0), (8, 8)))

    def patch_rows(w):
        w = np.moveaxis(w, -1, 0).reshape(2, BLK, 2, BLK, len(SHIFTS), CH, -1)
        cells = [(s, dy) for s in range(len(SHIFTS)) for dy in range(2)]
        out = [w[dy, :, dx, :, s, 0:2].transpose(2, 0, 1, 3).reshape(P, -1) for s, dy in cells for dx in range(2)]
        out += [w[dy, :, :, :, s, 2].transpose(1, 0, 2, 3).reshape(P, -1) for s, dy in cells]
        return np.ascontiguousarray(np.stack(out, 1))

    o["tok_w"] = patch_rows(v["L0_tok_W"])
    o["tok_gb"] = np.stack([patch_rows(v["L0_tok_ln_" + k])[:, :, 0] for k in ("gamma", "beta")], 1)
    o["tok_b"] = v["L0_tok_b"][None]

    m = {k[8:]: x for k, x in v.items() if k.startswith("L0_attn_")}
    o["mam_bm_in_w"], o["mam_bm_in_b"] = by_rows(m["bm_in_w"].T), column(m["bm_in_b"])
    o["mam_in_w"] = by_rows(m["m_in_w"].T)
    o["mam_xproj_w"] = by_rows(np.concatenate([m["m_xproj_w"][RANK:], m["m_xproj_w"][:RANK]]).T, P)
    o["mam_dt_w"] = np.ascontiguousarray(m["m_dt_w"].T)
    o["mam_out_w"], o["mam_bm_out_w"] = by_rows(m["m_out_w"].T, P), by_rows(m["bm_out_w"].T)
    o["mam_channel"] = by_rows(np.concatenate([m["m_conv_w"], m["m_conv_b"][:, None], m["m_dt_b"][:, None], m["m_D"][:, None], m["m_A_log"]], 1), P)
    o["mam_rows"] = np.stack([m["bm_out_b"], m["ln_g"], m["ln_b"]])[None]

    for name, key in (("slots", "slots"), ("b2", "fc2_bias"), ("w1", "fc1_weight"), ("b1", "fc1_bias"), ("w2", "fc2_weight")):
        o["ffn_" + name] = v["L0_ffn_" + key]
    o["ffn_scale"], o["ffn_norm_w"] = v["L0_ffn_scale"][:, None], v["L0_ffn_norm_weight"][None]

    e = {k[8:]: x for k, x in v.items() if k.startswith("L1_attn_")}
    w = e["pos_conv_w"]
    group, mid = w.shape[1], w.shape[2] // 2
    pos = np.zeros((HD2, 2, TAPS, HD2), w.dtype)
    for k in range(2):
        for at in range(0, HD2, group):
            taps = w[k * HD2 + at:k * HD2 + at + group, :, mid - SEQ + 1:mid + SEQ]
            pos[at:at + group, k, :, at:at + group] = taps.transpose(1, 2, 0)
    o["pos_w"], o["pos_b"], o["pos_rows"] = pos, column(e["pos_conv_b"]), np.stack([e["ln0_g"], e["ln0_b"]])[None]
    o["enc_w_qkv"] = stack(lambda l: by_rows(np.concatenate([e[n][l] for n in ("Wq", "Wk", "Wv")], 1)))
    o["enc_c_qk"] = stack(lambda l: np.concatenate([column(e["bq"][l]), column(e["bk"][l])], 1))
    o["enc_w_o"], o["enc_w_1"] = (stack(lambda l: by_rows(e[n][l])) for n in ("Wo", "W1"))
    o["enc_w_2"] = stack(lambda l: by_rows(e["W2"][l], P))
    o["enc_c_b"] = stack(lambda l: np.concatenate([column(e[n][l]) for n in ("bv", "ln1_g", "ln1_b")], 1))
    o["enc_c_1"] = stack(lambda l: column(e["b1"][l], P))
    o["enc_rows"] = stack(lambda l: np.stack([e[n][l] for n in ("bo", "ln1_g", "ln1_b", "b2", "ln2_g", "ln2_b")]))
    before = [(e["ln0_g"], e["ln0_b"])] + list(zip(e["ln2_g"], e["ln2_b"]))
    o["enc_c_n"] = np.stack([np.concatenate([column(g), column(b)], 1) for g, b in before])

    o["moe_ln_w"], o["moe_w_router"] = v["L1_ffn_ln_w"][None], by_rows(v["L1_ffn_w_router"])
    o["moe_wi"] = np.stack([by_rows(w) for w in v["L1_ffn_wi"]])
    o["moe_wo"] = np.stack([by_rows(w, P) for w in v["L1_ffn_wo"]])

    p = np.arange(P)
    o["moe_rank"] = np.arange(E, 0, -1, dtype=np.float32)[None]
    o["ident"] = np.eye(P, dtype=np.float32)
    o["pick_rows"] = (p[:HD2, None] % (2 * NS) == np.arange(2 * NS)).astype(np.float32)
    o["same_image"] = (p[:, None] // SEQ == np.arange(TPI)).astype(np.float32)
    o["image_rows"] = np.ascontiguousarray(o["same_image"].T)
    o["head_rows"] = (p[:HD2, None] // (D // HEADS) == np.arange(HC)).astype(np.float32)
    return {k: np.ascontiguousarray(x) for k, x in o.items()}


def kernel(**inputs):
    import concourse.bacc as _bacc
    from concourse.bass_utils import run_bass_kernel_spmd as _run

    nc = _bacc.Bacc("TRN2", target_bir_lowering=False, num_devices=1)
    arrays = lay_out(inputs)
    a = {name: nc.dram_tensor(name, list(x.shape), mybir.dt.from_np(x.dtype), kind="ExternalInput").ap() for name, x in arrays.items()}
    out = nc.dram_tensor("out", [IMG, SEQ, D], F32, kind="ExternalOutput").ap()
    build(nc, a, out)
    r = _run(nc, [arrays], core_ids=[0])
    return r.results[0]["out"]
```

```python
from contextlib import ExitStack

import numpy as np

import concourse.bass as bass
from concourse import mybir

F32 = mybir.dt.float32
BF16 = mybir.dt.bfloat16
U32 = mybir.dt.uint32
I32 = mybir.dt.int32
ALU = mybir.AluOpType
ACT = mybir.ActivationFunctionType
AX = mybir.AxisListType

P = 128
IMG, CH, SIDE = 64, 3, 64
PATCH = 16
BLK = PATCH // 2
SEQ = (SIDE // PATCH) ** 2
D = 192
HD2 = D // 2
TOK = IMG * SEQ
TPI = P // SEQ
NT = TOK // P
HT = NT // 2
HTOK = TOK // 2
HIMG = IMG // 2
GRID = 9
CELLS = GRID * GRID
XCOLS = IMG * CELLS
PDIM = 5 * CH * PATCH * PATCH
NCHUNK = PDIM // P
SHIFTS = ((0, 0), (-1, -1), (1, 1), (-1, 1), (1, -1))
EPS = 1e-5
BIG = 1e30


def place(delta):
    return {0: 0, 1: GRID // 2 + 1, -1: GRID // 2, 2: 1}[delta]


def patch_chunks():
    first = [(0, dy + sy, dx + sx) for sy, sx in SHIFTS for dy in (0, 1) for dx in (0, 1)]
    second = [(1 if sx == 0 else 2, dy + sy, sx) for sy, sx in SHIFTS for dy in (0, 1)]
    return first + second


class Steps:

    def __init__(self, eng, sem):
        self.eng, self.sem, self.before, self.local, self.i, self.per = eng, sem, 0, 0, None, 0

    def __call__(self, ins):
        ins.then_inc(self.sem, 1)
        self.local += 1
        self.wait()
        return ins

    def wait(self):
        base = self.before if self.i is None else self.i * self.per + self.before
        self.eng.wait_ge(self.sem, base + self.local)

    def enter(self, i, per):
        self.before, self.local, self.i, self.per = self.before + self.local, 0, i, per

    def leave(self, rounds):
        assert self.local == self.per, (self.local, self.per)
        self.before, self.local, self.i = self.before + rounds * self.per, 0, None


def scope(nc):
    ctx = ExitStack()
    sems = []
    ctx.callback(nc.all_engine_barrier)
    ctx.callback(lambda: nc.clear_and_free_semaphores(sems))

    def sb(name, shape, dt=F32):
        return ctx.enter_context(nc.sbuf_tensor("s_" + name, shape, dt))

    def bank(name, shape=(P, 512), dt=F32):
        return ctx.enter_context(nc.psum_tensor(name, list(shape), dt))

    def sem(name):
        sems.append(nc.alloc_semaphore(name))
        return sems[-1]

    return ctx, sb, bank, sem


def tokenize(nc, a, kept):
    chunks = patch_chunks()
    ctx, sb, bank, sem = scope(nc)
    with ctx:
        xg = [sb(f"tok_x{i}", [P, XCOLS]) for i in range(3)]
        sq = sb("tok_squares", [P, XCOLS])
        w_raw = sb("tok_w_raw", [P, NCHUNK, D])
        w_gam = sb("tok_w_gamma", [P, NCHUNK, D + 1])
        gb = sb("tok_gamma_beta", [P, 2, NCHUNK])
        ones = sb("tok_ones", [P, P])
        wsum = sb("tok_w_sum", [P, D])
        wbeta = sb("tok_w_beta", [P, D])
        cols = sb("tok_colsum", [P, D])
        bias = sb("tok_bias", [P, D])
        blk = sb("tok_block_sq", [64, XCOLS])
        r4 = sb("tok_row4", [1, IMG, GRID, 4])
        r2 = sb("tok_row2", [1, IMG, GRID, 4])
        ssq = sb("tok_ssq_row", [1, IMG, 4, 4])
        st = sb("tok_stats", [P, 8, NT])
        bn = sb("tok_bn", [P, NT, 8])
        half = sb("tok_neg_half", [P, 1])
        xc = [sb(f"tok_chunk{i}", [P, HTOK]) for i in range(3)]
        acc = [bank(f"tok_acc{i}") for i in range(4)]
        blk_ps = [bank(f"tok_blk_ps{i}") for i in range(2)]
        bc_ps = bank("tok_bc_ps")
        ssq_ps = bank("tok_ssq_ps")
        x_in = [sem(f"tok_x_in{i}") for i in range(3)]
        w_in = [sem(f"tok_w_in{i}") for i in range(3)]
        small_in, x_rest_in = sem("tok_small_in"), sem("tok_x_rest_in")
        squares = sem("tok_squares_done")
        sq_ready = sem("tok_sq_ready")
        ones_set = sem("tok_ones_set")
        w_scaled = sem("tok_w_scaled")
        blk_full = sem("tok_blk_full")
        blk_free = sem("tok_blk_free")
        ssq_row = sem("tok_ssq_row_ready")
        ssq_full = sem("tok_ssq_full")
        sums = sem("tok_w_sums")
        bc_full = sem("tok_bc_full")
        acc_full = sem("tok_acc_full")
        gathered = sem("tok_gathered")
        chunk_used = sem("tok_chunk_used")
        var_ready = sem("tok_var_ready")
        rstd_ready = sem("tok_rstd_ready")
        half_set = sem("tok_half_set")
        dve_steps = sem("tok_dve_steps")
        block = ctx.enter_context(nc.Block())
        NB = -(-XCOLS // 512)
        W3 = NCHUNK // 3

        @block.sync
        def _(sp):
            sp.dma_start(gb[:, :, :], a["tok_gb"]).then_inc(small_in, 16)
            sp.dma_start(bias[:, :], a["tok_b"].partition_broadcast(P)).then_inc(small_in, 16)
            cut = XCOLS // 2
            sp.dma_start(xg[0][:, 0:cut], a["x_grid01"][:, 0:cut]).then_inc(x_in[0], 16)
            sp.dma_start(w_raw[:, 0:W3, :], a["tok_w"][:, 0:W3, :]).then_inc(w_in[0], 16)
            sp.dma_start(xg[0][:, cut:], a["x_grid01"][:, cut:]).then_inc(x_rest_in, 16)
            for i in range(1, 3):
                sp.dma_start(w_raw[:, W3 * i:W3 * (i + 1), :], a["tok_w"][:, W3 * i:W3 * (i + 1), :]).then_inc(w_in[i], 16)
            for i, shift in ((1, 5), (2, -4)):
                sp.dma_start(xg[i][0:64, :], a["x_grid2"][:, 8:8 + XCOLS]).then_inc(x_in[i], 16)
                sp.dma_start(xg[i][64:128, :], a["x_grid2"][:, 8 + shift:8 + shift + XCOLS]).then_inc(x_in[i], 16)

        @block.scalar
        def _(act):
            act.wait_ge(small_in, 32)
            for c in range(NCHUNK):
                if c == 4:
                    act.wait_ge(x_in[0], 16)
                    act.wait_ge(x_rest_in, 16)
                    nc.scalar.activation(sq[:, :], xg[0][:, :], ACT.Square).then_inc(squares, 1)
                act.wait_ge(w_in[c // W3], 16)
                nc.scalar.activation(w_gam[:, c, 0:D], w_raw[:, c, :], ACT.Copy, scale=gb[:, 0, c:c + 1]).then_inc(w_scaled, 1)
            act.wait_ge(x_in[1], 32)
            nc.scalar.activation(blk[0:64, :], xg[1][0:64, :], ACT.Square).then_inc(squares, 1)

        @block.gpsimd
        def _(pool):
            nc.gpsimd.memset(ones[:, :], 1.0).then_inc(ones_set, 1)
            nc.gpsimd.memset(w_gam[:, :, D:D + 1], 1.0).then_inc(ones_set, 1)
            nc.gpsimd.memset(half[:, :], -0.5).then_inc(half_set, 1)
            pool.wait_ge(half_set, 1)
            for hh in range(2):
                for k, (src, dst) in enumerate(((1, 2), (4, 5))):
                    pool.wait_ge(var_ready, 2 * hh + k + 1)
                    nc.gpsimd.tensor_tensor(st[:, src, hh * HT:(hh + 1) * HT], st[:, src, hh * HT:(hh + 1) * HT],
                                            half[:, 0:1].broadcast_to([P, HT]), ALU.pow).then_inc(rstd_ready, 1)

        @block.tensor
        def _(pe):
            def region(t):
                return acc[t // 2][:, 256 * (t % 2):256 * (t % 2) + D + 1]

            def product(hh):
                for c in range(NCHUNK):
                    if hh == 0:
                        pe.wait_ge(w_scaled, c + 1)
                        if c == 0:
                            pe.wait_ge(ones_set, 2)
                    pe.wait_ge(gathered, hh * NCHUNK + c + 1)
                    for t in range(HT):
                        mm = nc.tensor.matmul(region(hh * HT + t), xc[c % 3][:, t * P:(t + 1) * P], w_gam[:, c, :],
                                              start=(c == 0 and t % 2 == 0), stop=(c == NCHUNK - 1), skip_group_check=True)
                    mm.then_inc(chunk_used, 1)
                    if hh == 0 and 16 <= c < 16 + NB:
                        block_sums(c - 16)
                    if hh == 1 and c == 9:
                        spread_sums()
                    if hh == 1 and c == 19:
                        turn_squares()

            def block_sums(n):
                if n == 0:
                    pe.wait_ge(sq_ready, 1)
                w = min(512, XCOLS - 512 * n)
                if n >= 2:
                    pe.wait_ge(blk_free, n - 1)
                nc.tensor.matmul(blk_ps[n % 2][0:1, 0:w], ones[:, 0:1], sq[:, 512 * n:512 * n + w],
                                 start=True, stop=True).then_inc(blk_full, 1)

            def spread_sums():
                pe.wait_ge(sums, 4)
                nc.tensor.matmul(bc_ps[:, 0:D], ones[:, :], wsum[:, :], start=True, stop=True)
                nc.tensor.matmul(bc_ps[:, D:2 * D], ones[:, :], wbeta[:, :], start=True, stop=True).then_inc(bc_full, 1)

            def turn_squares():
                pe.wait_ge(ssq_row, 1)
                flat = ssq[:, :, :, :].rearrange("p b i j -> p (b i j)")
                for t in range(NT):
                    mm = nc.tensor.matmul(ssq_ps[:, t:t + 1], flat[:, t * P:(t + 1) * P], ones[0:1, 0:1], start=True, stop=True)
                mm.then_inc(ssq_full, 1)

            product(0)
            product(1)

        @block.vector
        def _(dve):
            step = Steps(dve, dve_steps)
            grids = [x[:, :].rearrange("p (b y x) -> p b y x", b=IMG, y=GRID) for x in xg]

            def gather(hh, c):
                src, dy, dx = chunks[c]
                n = hh * NCHUNK + c
                if n >= 3:
                    dve.wait_ge(chunk_used, n - 2)
                if n in (0, 20):
                    dve.wait_ge(x_in[1 if src else 0], 32 if src else 16)
                if n == NCHUNK:
                    dve.wait_ge(x_rest_in, 16)
                if src == 2:
                    dve.wait_ge(x_in[2], 32)
                y, x = place(dy), place(dx)
                out = xc[n % 3][:, :].rearrange("p (b i j) -> p b i j", b=HIMG, i=4)
                nc.vector.tensor_copy(out, grids[src][:, hh * HIMG:(hh + 1) * HIMG, y:y + 4, x:x + 4]).then_inc(gathered, 1)

            def finish(hh):
                dve.wait_ge(chunk_used, (hh + 1) * NCHUNK)
                ts = slice(hh * HT, (hh + 1) * HT)
                for b in range(2):
                    tt = slice(hh * HT + 2 * b, hh * HT + 2 * b + 2)
                    total = acc[2 * hh + b][:, :].rearrange("p (t n) -> p t n", t=2)[:, :, D]
                    step(nc.vector.tensor_scalar(st[:, 0, tt], total, -1.0 / PDIM, None, ALU.mult))
                step(nc.vector.tensor_tensor(st[:, 1, ts], st[:, 0, ts], st[:, 0, ts], ALU.mult))
                step(nc.vector.tensor_tensor(st[:, 1, ts], st[:, 3, ts], st[:, 1, ts], ALU.subtract))
                nc.vector.tensor_scalar(st[:, 1, ts], st[:, 1, ts], EPS, None, ALU.add).then_inc(var_ready, 1)
                for t in range(hh * HT, hh * HT + HT):
                    step(nc.vector.scalar_tensor_tensor(kept.h[:, t, :], cols[:, :], st[:, 0, t:t + 1],
                                                        acc[t // 2][:, 256 * (t % 2):256 * (t % 2) + D], ALU.mult, ALU.add))
                dve.wait_ge(rstd_ready, 2 * hh + 1)
                for t in range(hh * HT, hh * HT + HT):
                    step(nc.vector.scalar_tensor_tensor(kept.h[:, t, :], kept.h[:, t, :], st[:, 1, t:t + 1], bias[:, :], ALU.mult, ALU.add))
                    step(nc.vector.bn_stats(bn[:, t, 0:6], kept.h[:, t, :]))
                    step(nc.vector.bn_aggr(bn[:, t, 6:8], bn[:, t, 0:6]))
                nc.vector.tensor_scalar(st[:, 4, ts], bn[:, ts, 7], EPS, None, ALU.add).then_inc(var_ready, 1)
                dve.wait_ge(rstd_ready, 2 * hh + 2)
                for t in range(hh * HT, hh * HT + HT):
                    step(nc.vector.tensor_scalar(kept.x[:, t, :], kept.h[:, t, :], bn[:, t, 6:7], st[:, 4, t:t + 1], ALU.subtract, ALU.mult))

            dve.wait_ge(small_in, 32)
            for c in range(NCHUNK):
                gather(0, c)
                dve.wait_ge(w_in[c // W3], 16)
                if c == 0:
                    step(nc.vector.tensor_scalar(wbeta[:, :], w_raw[:, 0, :], gb[:, 1, 0:1], None, ALU.mult))
                else:
                    step(nc.vector.scalar_tensor_tensor(wbeta[:, :], w_raw[:, c, :], gb[:, 1, c:c + 1], wbeta[:, :], ALU.mult, ALU.add))
                if c == 14:
                    dve.wait_ge(squares, 2)
                    nc.vector.tensor_tensor(sq[0:64, :], sq[0:64, :], blk[0:64, :], ALU.add).then_inc(sq_ready, 1)
                    dve.wait_ge(sq_ready, 1)
                if 17 <= c < 17 + NB:
                    n = c - 17
                    w = min(512, XCOLS - 512 * n)
                    dve.wait_ge(blk_full, n + 1)
                    nc.vector.tensor_copy(blk[0:1, 512 * n:512 * n + w], blk_ps[n % 2][0:1, 0:w]).then_inc(blk_free, 1)
            dve.wait_ge(w_scaled, NCHUNK)
            dve.wait_ge(blk_free, NB)
            g = blk[0:1, :].rearrange("p (b y x) -> p b y x", b=IMG, y=GRID)
            for c in range(NCHUNK):
                gather(1, c)
                if 2 <= c < 5:
                    part = slice((c - 2) * D // 3, (c - 1) * D // 3)
                    nc.vector.tensor_reduce(wsum[:, part], w_gam[:, :, part].rearrange("p c n -> p n c"), AX.X, ALU.add).then_inc(sums, 1)
                elif c == 5:
                    nc.vector.tensor_copy(bn[:, 0, 0:1], wbeta[:, 0:1]).then_inc(sums, 1)
                elif c == 6:
                    step(nc.vector.tensor_tensor(r2[:, :, :, :], g[:, :, :, 0:4], g[:, :, :, 5:9], ALU.add))
                elif c == 8:
                    step(nc.vector.tensor_tensor(r4[:, :, :, :], g[:, :, :, 4:8], g[:, :, :, 1:5], ALU.add))
                elif c == 10:
                    step(nc.vector.tensor_tensor(r4[:, :, :, :], r4[:, :, :, :], r2[:, :, :, :], ALU.add))
                elif c == 12:
                    step(nc.vector.tensor_tensor(ssq[:, :, :, :], r2[:, :, 0:4, :], r2[:, :, 5:9, :], ALU.add))
                elif 13 <= c < 16:
                    d = (0, 1, -1)[c - 13]
                    step(nc.vector.tensor_tensor(ssq[:, :, :, :], ssq[:, :, :, :], r4[:, :, place(d):place(d) + 4, :], ALU.add))
                elif c == 16:
                    nc.vector.tensor_tensor(ssq[:, :, :, :], ssq[:, :, :, :], r4[:, :, place(2):place(2) + 4, :], ALU.add).then_inc(ssq_row, 1)
                elif c == 17:
                    dve.wait_ge(bc_full, 1)
                    nc.vector.tensor_copy(cols[:, :], bc_ps[:, 0:D]).then_inc(sums, 1)
                    step(nc.vector.tensor_tensor(bias[:, :], bias[:, :], bc_ps[:, D:2 * D], ALU.add))
                    dve.wait_ge(sums, 5)
                elif c == 23:
                    dve.wait_ge(ssq_full, 1)
                    step(nc.vector.tensor_scalar(st[:, 3, :], ssq_ps[:, 0:NT], 1.0 / PDIM, None, ALU.mult))
                    finish(0)
            finish(1)


class Ring:

    def __init__(self, banks, full, free, plan):
        self.banks, self.fulls, self.frees = banks, full, free
        self.at = {name: n for n, name in enumerate(plan)}
        assert len(self.at) == len(plan)

    def bank(self, name):
        return self.banks[self.at[name] % len(self.banks)]

    def full(self, name):
        return self.fulls[self.at[name] % len(self.banks)]

    def free(self, name):
        return self.frees[self.at[name] % len(self.banks)]

    def wait_free(self, eng, name):
        n = self.at[name] // len(self.banks)
        if n:
            eng.wait_ge(self.free(name), n)

    def wait_full(self, eng, name):
        eng.wait_ge(self.full(name), self.at[name] // len(self.banks) + 1)

    def wait_read(self, eng, name):
        eng.wait_ge(self.free(name), self.at[name] // len(self.banks) + 1)


CI = 2 * D // P
NS = 16
RANK = 12
PAD = SEQ + 3


def mamba(nc, a, kept):
    ctx, sb, bank, sem = scope(nc)
    units = [(hh, d) for hh in range(2) for d in range(2)]
    with ctx:
        w_bm = sb("mam_bm_in_w", [HD2, 2, 2 * D])
        b_bm = sb("mam_bm_in_b", [HD2, 4])
        w_in = sb("mam_in_w", [HD2, 2, 4 * D])
        w_xp = sb("mam_xproj_w", [P, CI, 2 * NS + RANK])
        w_dt = sb("mam_dt_w", [44, 2 * D])
        w_out = sb("mam_out_w", [P, CI, D])
        w_bo = sb("mam_bm_out_w", [HD2, 2, D])
        cst = sb("mam_channel", [P, CI, 7 + NS])
        rows = sb("mam_rows", [P, 3, D])
        decay = sb("mam_decay", [P, CI, NS])
        pick = sb("mam_pick", [3 * 2 * NS, 2 * NS, P], BF16)
        ones_bf = sb("mam_ones", [3 * 2 * NS, P], BF16)
        xT = sb("mam_xT", [HD2, 2, HTOK])
        xd = sb("mam_xd", [HD2, 2, HTOK])
        xpad = sb("mam_xpad", [P, CI, HIMG, PAD])
        conv = sb("mam_conv", [P, CI, HTOK])
        u = sb("mam_u", [P, CI, HTOK])
        gate = [sb(f"mam_gate{d}", [P, CI, HTOK]) for d in range(2)]
        bc = sb("mam_bc", [44, HTOK])
        rest = sb("mam_rest", [2 * NS, HTOK])
        mid = sb("mam_mid", [2 * NS, HTOK], BF16)
        bc3 = sb("mam_bc3", [3 * 2 * NS, HTOK], BF16)
        dtx = sb("mam_dt_pre", [P, CI, HTOK])
        dte = sb("mam_dt_exp", [P, CI, HTOK])
        dt1 = sb("mam_dt_one", [P, CI, HTOK])
        dtl = sb("mam_dt_log", [P, CI, HTOK])
        dt = sb("mam_dt", [P, CI, HTOK])
        dtu = sb("mam_dtu", [P, CI, HTOK])
        b_sb = [sb(f"mam_b{i}", [P, HTOK]) for i in range(2)]
        da = [sb(f"mam_da{i}", [P, CI, HTOK]) for i in range(2)]
        dbu = [sb(f"mam_dbu{i}", [P, CI, HTOK]) for i in range(2)]
        state = [sb(f"mam_state{i}", [P, CI, HTOK]) for i in range(2)]
        hc = [sb(f"mam_hc{i}", [P, CI, HTOK]) for i in range(2)]
        sumT = sb("mam_sumT", [HD2, 2, HTOK])
        res = sb("mam_res", [P, HT, D])
        bn = sb("mam_bn", [P, HT, 8])
        var = sb("mam_var", [P, 2, HT])
        half = sb("mam_neg_half", [P, 1])
        g_bank = [bank(f"mam_g{i}") for i in range(2)]
        b_bank = bank("mam_b_ps")
        c_bank = [bank(f"mam_c_ps{i}") for i in range(2)]
        y_bank = [bank(f"mam_y{i}") for i in range(3)]

        plan = []
        for hh in range(2):
            plan += [("xT", hh, m) for m in range(2)]
            for d in range(2):
                plan += [(n, hh, d, m) for n, k in (("xd", 2), ("c", CI), ("z", CI), ("proj", 1), ("dt", CI)) for m in range(k)]
            plan += [("sum", hh, m) for m in range(2)] + [("out", hh, t) for t in range(HT)]
        ring = Ring(g_bank, [sem(f"mam_g_full{i}") for i in range(2)], [sem(f"mam_g_free{i}") for i in range(2)], plan)
        w_sem = [sem(f"mam_w_in{i}") for i in range(4)]
        setup = sem("mam_setup")
        decay_ready = sem("mam_decay_ready")
        conv_ready, u_ready = sem("mam_conv_ready"), sem("mam_u_ready")
        bc_ready, exp_ready, one_ready, log_ready, dt_ready = (
            sem(f"mam_{n}_ready") for n in ("bc3", "dt_exp", "dt_one", "dt_log", "dt"))
        b_full, b_ready, c_full, da_ready, dbu_ready, scanned, hc_ready, hc_free = (
            sem(f"mam_{n}") for n in ("b_full", "b_ready", "c_full", "da_ready", "dbu_ready", "scanned", "hc_ready", "hc_free"))
        y_read, gated = sem("mam_y_read"), sem("mam_gated")
        var_ready, rstd_ready = sem("mam_var_ready"), sem("mam_rstd_ready")
        act_steps, dve_steps = sem("mam_act_steps"), sem("mam_dve_steps")
        block = ctx.enter_context(nc.Block())

        @block.sync
        def _(sp):
            for n, (dst, name) in enumerate(((w_bm[:, :, :], "mam_bm_in_w"), (b_bm[:, :], "mam_bm_in_b"), (w_in[:, :, :], "mam_in_w"),
                                             (cst[:, :, :], "mam_channel"))):
                sp.dma_start(dst, a[name]).then_inc(w_sem[0], 16)
            for dst, name in ((w_xp[:, :, :], "mam_xproj_w"), (w_dt[32:44, :], "mam_dt_w"), (w_out[:, :, :], "mam_out_w"),
                              (w_bo[:, :, :], "mam_bm_out_w")):
                sp.dma_start(dst, a[name]).then_inc(w_sem[1], 16)
            sp.dma_start(rows[:, :, :], a["mam_rows"].partition_broadcast(P)).then_inc(w_sem[2], 16)

        @block.gpsimd
        def _(pool):
            nc.gpsimd.memset(ones_bf[:, :], 1.0).then_inc(setup, 1)
            nc.gpsimd.memset(half[:, :], -0.5).then_inc(setup, 1)
            nc.gpsimd.memset(xpad[:, :, :, 0:3], 0.0).then_inc(setup, 1)
            for i in range(2):
                nc.gpsimd.memset(da[i][:, :, :].rearrange("p c (b t) -> p c b t", t=SEQ)[:, :, :, 0:1], 0.0).then_inc(setup, 1)
            pool.wait_ge(setup, 5)
            for n, (hh, d) in enumerate(units):
                pool.wait_ge(dt_ready, CI * (n + 1))

                def drive(s):
                    for j in range(2):
                        k = s + j
                        pool.wait_ge(b_ready, n * NS + k + 1)
                        pool.wait_ge(scanned, n * NS + k + 1)
                        nc.gpsimd.tensor_tensor(dbu[j][:, :, :], dtu[:, :, :], b_sb[j][:, :].unsqueeze(1).broadcast_to([P, CI, HTOK]),
                                                ALU.mult).then_inc(dbu_ready, 1)

                with pool.Fori(0, NS // 2) as i:
                    drive(i * 2)
                if d == 1:
                    for k in range(2):
                        pool.wait_ge(var_ready, 2 * hh + k + 1)
                        nc.gpsimd.tensor_tensor(var[:, k, :], var[:, k, :], half[:, 0:1].broadcast_to([P, HT]), ALU.pow).then_inc(rstd_ready, 1)

        @block.scalar
        def _(act):
            step = Steps(act, act_steps)
            act.wait_ge(w_sem[0], 64)
            step(nc.scalar.activation(decay[:, :, :], cst[:, :, 7:7 + NS], ACT.Exp))
            nc.scalar.mul(decay[:, :, :], decay[:, :, :], -1.0).then_inc(decay_ready, 1)
            act.wait_ge(decay_ready, 1)
            act.wait_ge(setup, 5)
            for n, (hh, d) in enumerate(units):
                if d == 0:
                    for m in range(2):
                        ring.wait_full(act, ("xT", hh, m))
                        nc.scalar.copy(xT[:, m, :], ring.bank(("xT", hh, m))[0:HD2, :]).then_inc(ring.free(("xT", hh, m)), 1)
                for m in range(2):
                    use = ("xd", hh, d, m)
                    ring.wait_full(act, use)
                    nc.scalar.activation(xd[:, m, :], ring.bank(use)[0:HD2, :], ACT.Identity,
                                         bias=b_bm[:, 2 * d + m:2 * d + m + 1]).then_inc(ring.free(use), 1)
                for c in range(CI):
                    use = ("c", hh, d, c)
                    ring.wait_full(act, use)
                    if c == 0 and n:
                        act.wait_ge(conv_ready, CI * n)
                    x_t = xpad[:, c, :, 3:PAD] if d == 0 else xpad[:, c, :, PAD - 1:2:-1]
                    nc.scalar.copy(x_t, ring.bank(use)[:, :].rearrange("p (b t) -> p b t", t=SEQ)).then_inc(ring.free(use), 1)
                def silu_z(c):
                    use = ("z", hh, d, c)
                    ring.wait_full(act, use)
                    nc.scalar.activation(gate[d][:, c, :], ring.bank(use)[:, :], ACT.Silu).then_inc(ring.free(use), 1)

                def silu_u(c):
                    act.wait_ge(conv_ready, CI * n + c + 1)
                    nc.scalar.activation(u[:, c, :], conv[:, c, :], ACT.Silu).then_inc(u_ready, 1)

                silu_z(0)
                silu_u(0)
                silu_z(1)
                silu_z(2)
                silu_u(1)
                silu_u(2)
                use = ("proj", hh, d, 0)
                ring.wait_full(act, use)
                nc.scalar.copy(bc[:, :], ring.bank(use)[0:44, :]).then_inc(ring.free(use), 1)
                nc.scalar.preload_act_table_set("natural_log_exp_and_others")
                for c in range(CI):
                    use = ("dt", hh, d, c)
                    ring.wait_full(act, use)
                    step(nc.scalar.activation(dte[:, c, :], ring.bank(use)[:, :], ACT.Abs, bias=cst[:, c, 5:6]))
                    nc.scalar.activation(dtx[:, c, :], ring.bank(use)[:, :], ACT.Identity, bias=cst[:, c, 5:6]).then_inc(ring.free(use), 1)
                    nc.scalar.activation(dte[:, c, :], dte[:, c, :], ACT.Exp, scale=-1.0).then_inc(exp_ready, 1)
                for c in range(CI):
                    act.wait_ge(one_ready, CI * n + c + 1)
                    nc.scalar.activation(dtl[:, c, :], dt1[:, c, :], ACT.Ln).then_inc(log_ready, 1)
                act.wait_ge(dt_ready, CI * (n + 1))

                def decays(s):
                    for j in range(2):
                        k = s + j
                        act.wait_ge(b_full, n * NS + k + 1)
                        act.wait_ge(dbu_ready, n * NS + k + 1)
                        nc.scalar.copy(b_sb[j][:, :], b_bank[:, :]).then_inc(b_ready, 1)
                        act.wait_ge(scanned, n * NS + k + 1)
                        for c in range(CI):
                            t1 = dt[:, c, :].rearrange("p (b t) -> p b t", t=SEQ)[:, :, 1:SEQ]
                            o1 = da[j][:, c, :].rearrange("p (b t) -> p b t", t=SEQ)[:, :, 1:SEQ]
                            nc.scalar.activation(o1, t1, ACT.Exp, scale=decay[:, c, bass.ds(k, 1)]).then_inc(da_ready, 1)

                with act.Fori(0, NS // 2) as i:
                    decays(i * 2)
                if d == 1:
                    for m in range(2):
                        use = ("sum", hh, m)
                        ring.wait_full(act, use)
                        nc.scalar.copy(sumT[:, m, :], ring.bank(use)[0:HD2, :]).then_inc(ring.free(use), 1)

        @block.tensor
        def _(pe):
            for n, (hh, d) in enumerate(units):
                if d == 0:
                    if hh == 0:
                        pe.wait_ge(w_sem[0], 64)
                    for m in range(2):
                        use = ("xT", hh, m)
                        ring.wait_free(pe, use)
                        for t in range(HT):
                            mm = nc.tensor.transpose(ring.bank(use)[0:HD2, t * P:(t + 1) * P],
                                                     kept.x[:, hh * HT + t, m * HD2:(m + 1) * HD2], kept.ident[:, :])
                        mm.then_inc(ring.full(use), 1)
                    for m in range(2):
                        ring.wait_read(pe, ("xT", hh, m))
                for m in range(2):
                    use = ("xd", hh, d, m)
                    ring.wait_free(pe, use)
                    for k in range(2):
                        mm = nc.tensor.matmul(ring.bank(use)[0:HD2, :], w_bm[:, k, d * D + m * HD2:d * D + (m + 1) * HD2], xT[:, k, :],
                                              start=(k == 0), stop=(k == 1))
                    mm.then_inc(ring.full(use), 1)
                for m in range(2):
                    ring.wait_read(pe, ("xd", hh, d, m))
                for name, first in (("c", 0), ("z", CI)):
                    for c in range(CI):
                        use = (name, hh, d, c)
                        ring.wait_free(pe, use)
                        for k in range(2):
                            mm = nc.tensor.matmul(ring.bank(use)[:, :], w_in[:, k, (first + c) * P:(first + c + 1) * P], xd[:, k, :],
                                                  start=(k == 0), stop=(k == 1))
                        mm.then_inc(ring.full(use), 1)
                use = ("proj", hh, d, 0)
                ring.wait_free(pe, use)
                pe.wait_ge(w_sem[1], 64)
                for k in range(CI):
                    pe.wait_ge(u_ready, CI * n + k + 1)
                    mm = nc.tensor.matmul(ring.bank(use)[0:44, :], w_xp[:, k, :], u[:, k, :], start=(k == 0), stop=(k == CI - 1))
                mm.then_inc(ring.full(use), 1)
                ring.wait_read(pe, use)
                for c in range(CI):
                    use = ("dt", hh, d, c)
                    ring.wait_free(pe, use)
                    nc.tensor.matmul(ring.bank(use)[:, :], w_dt[32:44, c * P:(c + 1) * P], bc[32:44, :], start=True, stop=True).then_inc(ring.full(use), 1)
                pe.wait_ge(bc_ready, n + 1)
                if n:
                    pe.wait_ge(y_read, CI * n)

                def spread_b(k):
                    need(pe, b_ready, n * NS + k)
                    nc.tensor.matmul(b_bank[:, :], pick[:, bass.ds(k, 1), :].rearrange("p a b -> p (a b)"), bc3[:, :], start=True, stop=True).then_inc(b_full, 1)

                def spread_c(k, j):
                    pe.wait_ge(hc_ready, n * NS + k + 1)
                    nc.tensor.matmul(c_bank[j][:, :], pick[:, bass.ds(k + NS, 1), :].rearrange("p a b -> p (a b)"), bc3[:, :], start=True, stop=True).then_inc(c_full, 1)

                def add(k, j, first=False, last=False):
                    pe.wait_ge(hc_ready, n * NS + k + 3)
                    for c in range(CI):
                        mm = nc.tensor.matmul(y_bank[c][:, :], kept.ident[:, :], hc[j][:, c, :], start=first, stop=last)
                    mm.then_inc(hc_free, 1)

                spread_b(0)
                spread_c(0, 0)
                spread_b(1)
                spread_c(1, 1)
                spread_b(2)
                spread_b(3)
                add(0, 0, first=True)
                with pe.Fori(0, NS // 2 - 2) as i:
                    for j in range(2):
                        spread_c(i * 2 + 2 + j, j)
                        spread_b(i * 2 + 4 + j)
                        add(i * 2 + 1 + j, 1 - j)
                spread_c(NS - 2, 0)
                add(NS - 3, 1)
                spread_c(NS - 1, 1)
                add(NS - 2, 0)
                add(NS - 1, 1, last=True)
                if d == 1:
                    for m in range(2):
                        use = ("sum", hh, m)
                        ring.wait_free(pe, use)
                        pe.wait_ge(gated, 2 * CI * (hh + 1))
                        for e in range(2):
                            for k in range(CI):
                                mm = nc.tensor.matmul(ring.bank(use)[0:HD2, :], w_out[:, k, m * HD2:(m + 1) * HD2], gate[e][:, k, :],
                                                      start=(e == 0 and k == 0), stop=(e == 1 and k == CI - 1))
                        mm.then_inc(ring.full(use), 1)
                    for m in range(2):
                        ring.wait_read(pe, ("sum", hh, m))
                    for t in range(HT):
                        use = ("out", hh, t)
                        ring.wait_free(pe, use)
                        for k in range(2):
                            mm = nc.tensor.matmul(ring.bank(use)[:, 0:D], sumT[:, k, t * P:(t + 1) * P], w_bo[:, k, :], start=(k == 0), stop=(k == 1))
                        mm.then_inc(ring.full(use), 1)

        @block.vector
        def _(dve):
            step = Steps(dve, dve_steps)
            dve.wait_ge(setup, 5)
            for s in (scanned, hc_ready, hc_free, dbu_ready):
                dve.sem_inc(s, 2)
            step(nc.vector.tensor_tensor(pick[:, :, :], kept.pick_rows[0:96, :].unsqueeze(2).broadcast_to([96, 32, P]),
                                         ones_bf[:, :].unsqueeze(1).broadcast_to([96, 32, P]), ALU.mult))
            dve.wait_ge(w_sem[0], 64)
            dve.wait_ge(w_sem[2], 16)
            for n, (hh, d) in enumerate(units):
                for c in range(CI):
                    use = ("c", hh, d, c)
                    ring.wait_read(dve, use)
                    out = conv[:, c, :].rearrange("p (b t) -> p b t", t=SEQ)
                    if c == 0 and n:
                        dve.wait_ge(u_ready, CI * n)
                    step(nc.vector.tensor_scalar(out, xpad[:, c, :, 0:SEQ], cst[:, c, 0:1], cst[:, c, 4:5], ALU.mult, ALU.add))
                    for k in range(1, 4):
                        ins = nc.vector.scalar_tensor_tensor(out, xpad[:, c, :, k:k + SEQ], cst[:, c, k:k + 1], out, ALU.mult, ALU.add)
                        if k == 3:
                            ins.then_inc(conv_ready, 1)
                        else:
                            step(ins)
                use = ("proj", hh, d, 0)
                ring.wait_read(dve, use)
                step(nc.vector.tensor_copy(bc3[0:32, :], bc[0:32, :]))
                step(nc.vector.tensor_tensor(rest[:, :], bc[0:32, :], bc3[0:32, :], ALU.subtract))
                step(nc.vector.tensor_copy(mid[:, :], rest[:, :]))
                step(nc.vector.tensor_copy(bc3[32:64, :], mid[:, :]))
                step(nc.vector.tensor_tensor(rest[:, :], rest[:, :], mid[:, :], ALU.subtract))
                nc.vector.tensor_copy(bc3[64:96, :], rest[:, :]).then_inc(bc_ready, 1)
                for c in range(CI):
                    dve.wait_ge(exp_ready, CI * n + c + 1)
                    nc.vector.tensor_scalar(dt1[:, c, :], dte[:, c, :], 1.0, None, ALU.add).then_inc(one_ready, 1)
                for c in range(CI):
                    dve.wait_ge(one_ready, CI * n + c + 1)
                    step(nc.vector.scalar_tensor_tensor(dte[:, c, :], dt1[:, c, :], -1.0, dte[:, c, :], ALU.add, ALU.subtract))
                    if c == 0:
                        for k in range(CI):
                            ring.wait_read(dve, ("dt", hh, d, k))
                        dve.wait_ge(u_ready, CI * (n + 1))
                    step(nc.vector.scalar_tensor_tensor(dte[:, c, :], dtx[:, c, :], 0.0, dte[:, c, :], ALU.max, ALU.subtract))
                    dve.wait_ge(log_ready, CI * n + c + 1)
                    step(nc.vector.tensor_tensor(dt[:, c, :], dtl[:, c, :], dte[:, c, :], ALU.add))
                    nc.vector.tensor_tensor(dtu[:, c, :], dt[:, c, :], u[:, c, :], ALU.mult).then_inc(dt_ready, 1)

                def scan(k, j):
                    dve.wait_ge(da_ready, CI * (n * NS + k + 1))
                    dve.wait_ge(dbu_ready, n * NS + k + 3)
                    dve.wait_ge(hc_ready, n * NS + k + 1)
                    nc.vector.tensor_tensor_scan(state[j][:, :, :].rearrange("p c t -> p (c t)"), da[j][:, :, :].rearrange("p c t -> p (c t)"),
                                                 dbu[j][:, :, :].rearrange("p c t -> p (c t)"), 0.0, ALU.mult, ALU.add).then_inc(scanned, 1)

                def times_c(k, j):
                    dve.wait_ge(scanned, n * NS + k + 3)
                    dve.wait_ge(c_full, n * NS + k + 1)
                    dve.wait_ge(hc_free, n * NS + k + 1)
                    nc.vector.tensor_tensor(hc[j][:, :, :], state[j][:, :, :], c_bank[j][:, :].unsqueeze(1).broadcast_to([P, CI, HTOK]),
                                            ALU.mult).then_inc(hc_ready, 1)

                scan(0, 0)
                with dve.Fori(0, NS // 2 - 1) as i:
                    for j in range(2):
                        scan(i * 2 + 1 + j, 1 - j)
                        times_c(i * 2 + j, j)
                scan(NS - 1, 1)
                times_c(NS - 2, 0)
                times_c(NS - 1, 1)
                dve.wait_ge(hc_free, n * NS + NS + 2)
                for c in range(CI):
                    use = ("z", hh, d, c)
                    ring.wait_read(dve, use)
                    nc.vector.scalar_tensor_tensor(conv[:, c, :], u[:, c, :], cst[:, c, 6:7], y_bank[c][:, :], ALU.mult, ALU.add).then_inc(y_read, 1)
                    dve.wait_ge(y_read, CI * n + c + 1)
                    y = conv[:, c, :].rearrange("p (b t) -> p b t", t=SEQ)
                    g = gate[d][:, c, :].rearrange("p (b t) -> p b t", t=SEQ)
                    nc.vector.tensor_tensor(g, g, y if d == 0 else y[:, :, ::-1], ALU.mult).then_inc(gated, 1)
                if d == 0:
                    continue
                hs, xs = kept.h[:, hh * HT:(hh + 1) * HT, :], kept.x[:, hh * HT:(hh + 1) * HT, :]
                wide = [rows[:, k:k + 1, :].broadcast_to([P, HT, D]) for k in range(3)]
                step(nc.vector.tensor_tensor(res[:, :, :], xs, wide[0], ALU.add))
                for t in range(HT):
                    use = ("out", hh, t)
                    ring.wait_full(dve, use)
                    nc.vector.tensor_tensor(res[:, t, :], res[:, t, :], ring.bank(use)[:, 0:D], ALU.add).then_inc(ring.free(use), 1)
                    ring.wait_read(dve, use)
                    step(nc.vector.bn_stats(bn[:, t, 0:6], res[:, t, :]))
                    step(nc.vector.bn_aggr(bn[:, t, 6:8], bn[:, t, 0:6]))
                nc.vector.tensor_scalar(var[:, 0, :], bn[:, :, 7], EPS, None, ALU.add).then_inc(var_ready, 1)
                dve.wait_ge(rstd_ready, 2 * hh + 1)
                for t in range(HT):
                    step(nc.vector.tensor_scalar(res[:, t, :], res[:, t, :], bn[:, t, 6:7], var[:, 0, t:t + 1], ALU.subtract, ALU.mult))
                step(nc.vector.tensor_tensor(res[:, :, :], res[:, :, :], wide[1], ALU.mult))
                step(nc.vector.tensor_tensor(res[:, :, :], res[:, :, :], wide[2], ALU.add))
                step(nc.vector.tensor_tensor(hs, hs, res[:, :, :], ALU.add))
                for t in range(HT):
                    step(nc.vector.bn_stats(bn[:, t, 0:6], hs[:, t, :]))
                    step(nc.vector.bn_aggr(bn[:, t, 6:8], bn[:, t, 0:6]))
                nc.vector.tensor_scalar(var[:, 1, :], bn[:, :, 7], EPS, None, ALU.add).then_inc(var_ready, 1)
                dve.wait_ge(rstd_ready, 2 * hh + 2)
                for t in range(HT):
                    step(nc.vector.tensor_scalar(xs[:, t, :], hs[:, t, :], bn[:, t, 6:7], var[:, 1, t:t + 1], ALU.subtract, ALU.mult))


SLOTS, F = 64, 768
FC = F // P
WR = 4


def need(eng, sem, value):
    if not isinstance(value, int) or value > 0:
        eng.wait_ge(sem, value)


def slot_experts(nc, a, kept):
    ctx, sb, bank, sem = scope(nc)
    with ctx:
        w1 = [sb(f"ffn_w1_{i}", [HD2 + 1, 2, F]) for i in range(WR)]
        w2 = [sb(f"ffn_w2_{i}", [P, FC, D]) for i in range(WR)]
        slots = sb("ffn_slots", [SLOTS, D])
        scale = sb("ffn_scale", [SLOTS, 1])
        b2 = sb("ffn_b2", [SLOTS, D])
        gain = sb("ffn_norm_w", [P, D])
        slT = sb("ffn_slT", [HD2, 2, SLOTS])
        xn = sb("ffn_xn", [P, NT, D])
        sqr = kept.n
        xnT = sb("ffn_xnT", [HD2, 2, TOK])
        st = sb("ffn_stats", [P, 8, NT])
        sst = sb("ffn_slot_stats", [SLOTS, 2])
        half = sb("ffn_neg_half", [P, 1])
        logit = sb("ffn_logit", [P, NT, SLOTS])
        comb = sb("ffn_combine", [P, NT, SLOTS])
        disp = sb("ffn_dispatch", [SLOTS, IMG, SEQ])
        dst = sb("ffn_dispatch_stats", [SLOTS, 2, IMG])
        disp_bd = [sb(f"ffn_dispatch_bd{i}", [P, TPI, SLOTS]) for i in range(2)]
        yT = sb("ffn_yT", [HD2 + 1, 2, SLOTS, IMG])
        ys = [sb(f"ffn_ys{i}", [HD2 + 1, 2, IMG]) for i in range(2)]
        g = [sb(f"ffn_g{i}", [IMG, F]) for i in range(2)]
        gT = [sb(f"ffn_gT{i}", [P, FC, IMG]) for i in range(2)]
        y2 = [sb(f"ffn_y2_{i}", [IMG, D]) for i in range(WR)]
        y2s = sb("ffn_y2s", [SLOTS, IMG, D])
        combT = sb("ffn_combT", [SLOTS, TOK])
        comb_bd = [sb(f"ffn_combine_bd{i}", [SLOTS, TPI, P]) for i in range(2)]
        bn = sb("ffn_bn", [P, NT, 8])
        big = [bank(f"ffn_big{i}", (P, 1024)) for i in range(2)]
        mid = [bank(f"ffn_mid{i}") for i in range(2)]
        low = [bank(f"ffn_low{i}") for i in range(2)]
        w1_in = [sem(f"ffn_w1_in{i}") for i in range(WR)]
        w2_in = [sem(f"ffn_w2_in{i}") for i in range(WR)]
        small_in = sem("ffn_small_in")
        y_out = [sem(f"ffn_y_out{i}") for i in range(WR)]
        y_in = [sem(f"ffn_y_in{i}") for i in range(2)]
        y_dram = nc.dram_tensor("ffn_y_scratch", [SLOTS, IMG, D], F32, kind="Internal").ap()
        setup = sem("ffn_setup")
        pow_asked, pow_done = sem("ffn_pow_asked"), sem("ffn_pow_done")
        pe_pre, dve_pre, act_pre = sem("ffn_pe_pre"), sem("ffn_dve_pre"), sem("ffn_act_pre")
        ys_ready, fc1_done, gelu_done, t_done, gT_ready, fc2_done, y2_ready = (
            sem(f"ffn_{n}") for n in ("ys_ready", "fc1_done", "gelu_done", "t_done", "gT_ready", "fc2_done", "y2_ready"))
        comb_bd_ready, comb_used, bd_ready, bd_used = (sem(f"ffn_{n}") for n in ("comb_bd_ready", "comb_used", "bd_ready", "bd_used"))
        yT_full, yT_ready, g_waited = sem("ffn_yT_full"), sem("ffn_yT_ready"), sem("ffn_g_waited")
        dve_steps = sem("ffn_dve_steps")
        block = ctx.enter_context(nc.Block())
        LOOPS = SLOTS // WR - 1

        @block.sync
        def _(sp):
            for dst_, name in ((slots[:, :], "ffn_slots"), (scale[:, :], "ffn_scale"), (b2[:, :], "ffn_b2")):
                sp.dma_start(dst_, a[name]).then_inc(small_in, 16)
            sp.dma_start(gain[:, :], a["ffn_norm_w"].partition_broadcast(P)).then_inc(small_in, 16)

            def load(i, c):
                n = i * WR + c
                need(sp, fc1_done, n - WR + 1)
                sp.dma_start(w1[c][0:HD2, :, :], a["ffn_w1"][bass.ds(n, 1), :, :].rearrange("s (p k) f -> p (s k) f", k=2)).then_inc(w1_in[c], 16)
                sp.dma_start(w1[c][HD2:HD2 + 1, 0, :], a["ffn_b1"][bass.ds(n, 1), :]).then_inc(w1_in[c], 16)
                need(sp, fc2_done, n - WR + 1)
                sp.dma_start(w2[c][:, :, :], a["ffn_w2"][bass.ds(n, 1), :, :].rearrange("s (p c) d -> p (s c) d", c=FC)).then_inc(w2_in[c], 16)

            def store(i, c):
                n = i * WR + c
                sp.wait_ge(y2_ready, n + 1)
                sp.dma_start(y_dram[bass.ds(n, 1), :, :].rearrange("s b d -> b (s d)"), y2[c][:, :]).then_inc(y_out[c], 16)

            for c in range(WR):
                load(0, c)
            with sp.Fori(0, LOOPS) as i:
                for c in range(WR):
                    load(i + 1, c)
                    store(i, c)
            for c in range(WR):
                store(LOOPS, c)
            for c in range(WR):
                sp.wait_ge(y_out[c], (LOOPS + 2) * 16)
            for k in range(2):
                sp.dma_start(y2s[:, k * HIMG:(k + 1) * HIMG, :], y_dram[:, k * HIMG:(k + 1) * HIMG, :]).then_inc(y_in[k], 16)

        @block.gpsimd
        def _(pool):
            nc.gpsimd.memset(half[:, :], -0.5).then_inc(setup, 1)
            pool.wait_ge(setup, 1)
            nc.gpsimd.memset(yT[HD2:HD2 + 1, :, :, :], 1.0).then_inc(setup, 1)
            for i in range(2):
                pool.wait_ge(setup, 2 + i)
                nc.gpsimd.memset(comb_bd[i][:, :, :], 0.0).then_inc(setup, 1)
            pool.wait_ge(setup, 4)
            for k, (t, n) in enumerate(((sst[:, 0:1], SLOTS), (st[:, 0, :], P), (st[:, 1, :], P), (st[:, 7, :], P))):
                pool.wait_ge(pow_asked, k + 1)
                width = t.shape[1]
                nc.gpsimd.tensor_tensor(t, t, half[0:n, 0:1].broadcast_to([n, width]), ALU.pow).then_inc(pow_done, 1)
                if k == 2:
                    pool.wait_ge(yT_ready, 2 * NT)

                    def stage(n, j):
                        need(pool, fc1_done, n - 1)
                        nc.gpsimd.tensor_copy(ys[j][:, :, :], yT[:, :, bass.ds(n, 1), :].rearrange("p k s b -> p (k s) b")).then_inc(ys_ready, 1)

                    stage(0, 0)
                    stage(1, 1)
                    with pool.Fori(0, SLOTS // 2 - 1) as i:
                        for j in range(2):
                            stage(i * 2 + 2 + j, j)

        @block.scalar
        def _(act):
            act.wait_ge(dve_pre, 5)
            nc.scalar.activation(comb[:, :, :], comb[:, :, :], ACT.Exp).then_inc(act_pre, 1)
            act.wait_ge(dve_pre, 6)
            nc.scalar.activation(disp[:, :, :], disp[:, :, :], ACT.Exp).then_inc(act_pre, 1)
            for t in range(NT):
                for m in range(2):
                    act.wait_ge(yT_full, 2 * t + m + 1)
                    out = yT[0:HD2, m, :, t * TPI:(t + 1) * TPI].rearrange("p s b -> p b s")
                    nc.scalar.copy(out, big[t % 2][0:HD2, m * 512:(m + 1) * 512].rearrange("p (b s) -> p b s", s=SLOTS)).then_inc(yT_ready, 1)

            def gelu(n, j):
                act.wait_ge(fc1_done, n + 1)
                need(act, t_done, n - 1)
                nc.scalar.activation(g[j][:, :], big[j][0:IMG, 0:F], ACT.Gelu).then_inc(gelu_done, 1)

            gelu(0, 0)
            gelu(1, 1)
            with act.Fori(0, SLOTS // 2 - 1) as i:
                for j in range(2):
                    gelu(i * 2 + 2 + j, j)

        @block.tensor
        def _(pe):
            pe.wait_ge(dve_pre, 1)
            for k in range(2):
                mm = nc.tensor.transpose(low[0][0:HD2, k * 64:(k + 1) * 64], slots[:, k:D:2], kept.ident[0:SLOTS, 0:SLOTS])
            mm.then_inc(pe_pre, 1)
            pe.wait_ge(dve_pre, 3)
            for k in range(2):
                for t in range(NT):
                    mm = nc.tensor.transpose(big[k][0:HD2, t * P:(t + 1) * P], xn[:, t, k:D:2], kept.ident[:, :])
                mm.then_inc(pe_pre, 1)
            pe.wait_ge(dve_pre, 4)
            for t in range(NT):
                for k in range(2):
                    mm = nc.tensor.matmul(low[1][:, t * SLOTS:(t + 1) * SLOTS], xnT[:, k, t * P:(t + 1) * P], slT[:, k, :], start=(k == 0), stop=(k == 1))
            mm.then_inc(pe_pre, 1)
            pe.wait_ge(dve_pre, 5)
            for t in range(NT):
                mm = nc.tensor.transpose(big[0][0:SLOTS, t * P:(t + 1) * P], logit[:, t, :], kept.ident[:, :])
            mm.then_inc(pe_pre, 1)
            pe.wait_ge(dve_pre, 7)
            for t in range(NT):
                mm = nc.tensor.transpose(big[1][0:SLOTS, t * P:(t + 1) * P], comb[:, t, :], kept.ident[:, :])
            mm.then_inc(pe_pre, 1)
            pe.wait_ge(dve_pre, 8)
            flat = disp[:, :, :].rearrange("p b t -> p (b t)")
            for t in range(NT):
                mm = nc.tensor.transpose(low[0][:, t * SLOTS:(t + 1) * SLOTS], flat[:, t * P:(t + 1) * P], kept.ident[0:SLOTS, 0:SLOTS])
            mm.then_inc(pe_pre, 1)
            pe.wait_ge(dve_pre, 9)
            for t in range(NT):
                pe.wait_ge(bd_ready, t + 1)
                if t >= 2:
                    pe.wait_ge(yT_ready, 2 * (t - 1))
                for m in range(2):
                    mm = nc.tensor.matmul(big[t % 2][0:HD2, m * 512:(m + 1) * 512], xn[:, t, m:D:2],
                                          disp_bd[t % 2][:, :, :].rearrange("p b s -> p (b s)"), start=True, stop=True)
                    mm.then_inc(yT_full, 1)
            pe.wait_ge(yT_ready, 2 * NT)

            def fc1(i, c):
                n, j = i * WR + c, c % 2
                need(pe, gelu_done, n - 1)
                pe.wait_ge(ys_ready, n + 1)
                pe.wait_ge(w1_in[c % WR], (i + c // WR + 1) * 32)
                for lo, hi in ((0, 512), (512, F)):
                    nc.tensor.matmul(big[j][0:IMG, lo:hi], ys[j][:, 0, :], w1[c % WR][:, 0, lo:hi], start=True, stop=False)
                    mm = nc.tensor.matmul(big[j][0:IMG, lo:hi], ys[j][0:HD2, 1, :], w1[c % WR][0:HD2, 1, lo:hi], start=False, stop=True)
                mm.then_inc(fc1_done, 1)

            def turn(i, c):
                n, j = i * WR + c, c % 2
                pe.wait_ge(gelu_done, n + 1)
                need(pe, gT_ready, n - 1)
                pe.sem_inc(g_waited, 1)
                for k in range(FC):
                    mm = nc.tensor.transpose(mid[j][:, k * IMG:(k + 1) * IMG], g[j][:, k:F:FC], kept.ident[0:IMG, 0:IMG])
                mm.then_inc(t_done, 1)

            def fc2(i, c):
                n, j = i * WR + c, c % 2
                pe.wait_ge(gT_ready, n + 1)
                need(pe, y2_ready, n - 1)
                pe.wait_ge(w2_in[c % WR], (i + c // WR + 1) * 16)
                for k in range(FC):
                    mm = nc.tensor.matmul(low[j][0:IMG, 0:D], gT[j][:, k, :], w2[c % WR][:, k, :], start=(k == 0), stop=(k == FC - 1))
                mm.then_inc(fc2_done, 1)

            for s in range(WR):
                fc1(0, s)
                if s >= 1:
                    turn(0, s - 1)
                if s >= 2:
                    fc2(0, s - 2)
            with pe.Fori(0, LOOPS) as i:
                for s in range(WR, 2 * WR):
                    fc1(i, s)
                    turn(i, s - 1)
                    fc2(i, s - 2)
            turn(LOOPS, WR - 1)
            fc2(LOOPS, WR - 2)
            fc2(LOOPS, WR - 1)
            for t in range(NT):
                if t % HT == 0:
                    pe.wait_ge(y_in[t // HT], 16)
                pe.wait_ge(comb_bd_ready, t + 1)
                if t >= 2:
                    pe.wait_ge(comb_used, t - 1)
                else:
                    pe.wait_ge(y2_ready, SLOTS)
                nc.tensor.matmul(low[t % 2][:, 0:D], combT[:, t * P:(t + 1) * P], b2[:, :], start=True, stop=False)
                for b in range(TPI):
                    mm = nc.tensor.matmul(low[t % 2][:, 0:D], comb_bd[t % 2][:, b, :], y2s[:, t * TPI + b, :], start=False, stop=(b == TPI - 1))
                mm.then_inc(pe_pre, 1)

        @block.vector
        def _(dve):
            step = Steps(dve, dve_steps)
            dve.wait_ge(small_in, 64)
            step(nc.vector.tensor_tensor(sqr[0:SLOTS, 0, :], slots[:, :], slots[:, :], ALU.mult))
            step(nc.vector.tensor_reduce(sst[:, 0:1], sqr[0:SLOTS, 0, :], AX.X, ALU.add))
            nc.vector.tensor_scalar(sst[:, 0:1], sst[:, 0:1], EPS * EPS, None, ALU.max).then_inc(pow_asked, 1)
            step(nc.vector.tensor_tensor(sqr[:, :, :], kept.x[:, :, :], kept.x[:, :, :], ALU.mult))
            step(nc.vector.tensor_reduce(st[:, 0, :], sqr[:, :, :], AX.X, ALU.add))
            nc.vector.tensor_scalar(st[:, 0, :], st[:, 0, :], 1.0 / D, EPS, ALU.mult, ALU.add).then_inc(pow_asked, 1)
            dve.wait_ge(pow_done, 1)
            nc.vector.tensor_scalar(slots[:, :], slots[:, :], sst[:, 0:1], scale[:, 0:1], ALU.mult, ALU.mult).then_inc(dve_pre, 1)
            dve.wait_ge(pow_done, 2)
            for t in range(NT):
                step(nc.vector.scalar_tensor_tensor(xn[:, t, :], kept.x[:, t, :], st[:, 0, t:t + 1], gain[:, :], ALU.mult, ALU.mult))
            dve.wait_ge(pe_pre, 1)
            nc.vector.tensor_copy(slT[:, :, :], low[0][0:HD2, 0:2 * SLOTS].rearrange("p (k s) -> p k s", k=2)).then_inc(dve_pre, 1)
            nc.vector.tensor_tensor(sqr[:, :, :], xn[:, :, :], xn[:, :, :], ALU.mult).then_inc(dve_pre, 1)
            dve.wait_ge(dve_pre, 3)
            step(nc.vector.tensor_reduce(st[:, 1, :], sqr[:, :, :], AX.X, ALU.add))
            nc.vector.tensor_scalar(st[:, 1, :], st[:, 1, :], EPS * EPS, None, ALU.max).then_inc(pow_asked, 1)
            dve.wait_ge(pe_pre, 3)
            step(nc.vector.tensor_copy(xnT[:, 0, :], big[0][0:HD2, :]))
            nc.vector.tensor_copy(xnT[:, 1, :], big[1][0:HD2, :]).then_inc(dve_pre, 1)
            dve.wait_ge(pow_done, 3)
            dve.wait_ge(pe_pre, 4)
            step(nc.vector.tensor_tensor(logit[:, :, :], low[1][:, :].rearrange("p (t s) -> p t s", s=SLOTS),
                                         st[:, 1, :].unsqueeze(2).broadcast_to([P, NT, SLOTS]), ALU.mult))
            step(nc.vector.tensor_reduce(st[:, 2, :], logit[:, :, :], AX.X, ALU.max))
            nc.vector.tensor_tensor(comb[:, :, :], logit[:, :, :], st[:, 2, :].unsqueeze(2).broadcast_to([P, NT, SLOTS]), ALU.subtract).then_inc(dve_pre, 1)
            dve.wait_ge(pe_pre, 5)
            lt = big[0][0:SLOTS, :].rearrange("p (b t) -> p b t", t=SEQ)
            step(nc.vector.tensor_reduce(dst[:, 0, :], lt, AX.X, ALU.max))
            nc.vector.tensor_tensor(disp[:, :, :], lt, dst[:, 0, :].unsqueeze(2).broadcast_to([SLOTS, IMG, SEQ]), ALU.subtract).then_inc(dve_pre, 1)
            dve.wait_ge(act_pre, 1)
            step(nc.vector.tensor_reduce(st[:, 3, :], comb[:, :, :], AX.X, ALU.add))
            step(nc.vector.reciprocal(st[:, 3, :], st[:, 3, :]))
            nc.vector.tensor_tensor(comb[:, :, :], comb[:, :, :], st[:, 3, :].unsqueeze(2).broadcast_to([P, NT, SLOTS]), ALU.mult).then_inc(dve_pre, 1)
            dve.wait_ge(act_pre, 2)
            step(nc.vector.tensor_reduce(dst[:, 1, :], disp[:, :, :], AX.X, ALU.add))
            step(nc.vector.reciprocal(dst[:, 1, :], dst[:, 1, :]))
            nc.vector.tensor_tensor(disp[:, :, :], disp[:, :, :], dst[:, 1, :].unsqueeze(2).broadcast_to([SLOTS, IMG, SEQ]), ALU.mult).then_inc(dve_pre, 1)
            dve.wait_ge(pe_pre, 6)
            nc.vector.tensor_copy(combT[:, :], big[1][0:SLOTS, :]).then_inc(dve_pre, 1)
            dve.wait_ge(pe_pre, 7)
            for t in range(NT):
                if t >= 2:
                    dve.wait_ge(yT_full, 2 * (t - 1))
                nc.vector.tensor_tensor(disp_bd[t % 2][:, :, :], low[0][:, t * SLOTS:(t + 1) * SLOTS].unsqueeze(1).broadcast_to([P, TPI, SLOTS]),
                                        kept.same_image[:, :].unsqueeze(2).broadcast_to([P, TPI, SLOTS]), ALU.mult).then_inc(bd_ready, 1)
            dve.wait_ge(bd_ready, NT)
            dve.wait_ge(setup, 4)
            for c in range(WR):
                dve.sem_inc(y_out[c], 16)

            def turned(i, c):
                n, j = i * WR + c, c % 2
                dve.wait_ge(t_done, n + 1)
                need(dve, fc2_done, n - 1)
                nc.vector.tensor_copy(gT[j][:, :, :], mid[j][:, 0:FC * IMG].rearrange("p (k b) -> p k b", b=IMG)).then_inc(gT_ready, 1)

            def output(i, c):
                n, j = i * WR + c, c % 2
                dve.wait_ge(fc2_done, n + 1)
                dve.wait_ge(y_out[c % WR], (i + c // WR + 1) * 16)
                nc.vector.tensor_copy(y2[c % WR][:, :], low[j][0:IMG, 0:D]).then_inc(y2_ready, 1)

            for s in range(1, WR):
                turned(0, s - 1)
                if s >= 2:
                    output(0, s - 2)
            with dve.Fori(0, LOOPS) as i:
                for s in range(WR, 2 * WR):
                    turned(i, s - 1)
                    output(i, s - 2)
            turned(LOOPS, WR - 1)
            output(LOOPS, WR - 2)
            output(LOOPS, WR - 1)
            for t in range(NT):
                j = t % 2
                if t >= 2:
                    dve.wait_ge(pe_pre, 7 + t - 1)
                src = combT[:, t * P:(t + 1) * P].rearrange("p (b t) -> p b t", t=SEQ)
                nc.vector.tensor_copy(diagonal(comb_bd[j]), src).then_inc(comb_bd_ready, 1)
                if t >= 1:
                    finish_tile(nc, dve, step, t - 1, pe_pre, comb_used, low, kept, bn, st)
            finish_tile(nc, dve, step, NT - 1, pe_pre, comb_used, low, kept, bn, st)
            nc.vector.tensor_scalar(st[:, 7, :], bn[:, :, 7], EPS, None, ALU.add).then_inc(pow_asked, 1)
            dve.wait_ge(pow_done, 4)
            for t in range(NT):
                step(nc.vector.tensor_scalar(kept.x[:, t, :], kept.h[:, t, :], bn[:, t, 6:7], st[:, 7, t:t + 1], ALU.subtract, ALU.mult))


def diagonal(t):
    v = t[:, :, 0:SEQ]
    (ps, pn), (bs, bn), (ts, tn) = v.ap
    return bass.AP(v.tensor, v.offset, [[ps, pn], [bs + SEQ, bn], [ts, tn]])


def finish_tile(nc, dve, step, t, pe_pre, comb_used, low, kept, bn, st):
    dve.wait_ge(pe_pre, 7 + t + 1)
    nc.vector.tensor_tensor(kept.h[:, t, :], kept.h[:, t, :], low[t % 2][:, 0:D], ALU.add).then_inc(comb_used, 1)
    dve.wait_ge(comb_used, t + 1)
    step(nc.vector.bn_stats(bn[:, t, 0:6], kept.h[:, t, :]))
    step(nc.vector.bn_aggr(bn[:, t, 6:8], bn[:, t, 0:6]))


TAPS = 2 * SEQ - 1
L = 12


def position(nc, a, kept):
    ctx, sb, bank, sem = scope(nc)
    with ctx:
        w = sb("pos_w", [HD2, 2, TAPS, HD2])
        cols = sb("pos_cols", [HD2, 2])
        rows = sb("pos_rows", [P, 2, D])
        xT = sb("pos_xT", [HD2, 2, TOK])
        pT = sb("pos_pT", [HD2, 2, TOK])
        bn = sb("pos_bn", [P, NT, 8])
        var = sb("pos_var", [P, NT])
        half = sb("pos_neg_half", [P, 1])
        acc = [bank(f"pos_acc{i}") for i in range(4)]
        turn = [bank(f"pos_turn{i}") for i in range(2)]
        w_in = sem("pos_w_in")
        small_in = sem("pos_small_in")
        turned, xT_ready, conv_done, pos_ready, back_full, back_read = (
            sem(f"pos_{n}") for n in ("turned", "xT_ready", "conv_done", "gelu_done", "back_full", "back_read"))
        half_set, pow_asked, pow_done, dve_steps = (sem(f"pos_{n}") for n in ("half_set", "pow_asked", "pow_done", "dve_steps"))
        block = ctx.enter_context(nc.Block())

        @block.sync
        def _(sp):
            sp.dma_start(w[:, :, :, :], a["pos_w"]).then_inc(w_in, 16)
            sp.dma_start(cols[:, :], a["pos_b"]).then_inc(small_in, 16)
            sp.dma_start(rows[:, :, :], a["pos_rows"].partition_broadcast(P)).then_inc(small_in, 16)

        @block.gpsimd
        def _(pool):
            nc.gpsimd.memset(half[:, :], -0.5).then_inc(half_set, 1)
            pool.wait_ge(half_set, 1)
            pool.wait_ge(pow_asked, 1)
            nc.gpsimd.tensor_tensor(var[:, :], var[:, :], half[:, 0:1].broadcast_to([P, NT]), ALU.pow).then_inc(pow_done, 1)

        @block.scalar
        def _(act):
            act.wait_ge(small_in, 32)
            for n in range(4):
                hh, m = n // 2, n % 2
                act.wait_ge(conv_done, n + 1)
                nc.scalar.activation(pT[:, m, hh * HTOK:(hh + 1) * HTOK], acc[n][0:HD2, :], ACT.Gelu, bias=cols[:, m:m + 1]).then_inc(pos_ready, 1)

        @block.tensor
        def _(pe):
            for n in range(4):
                hh, m = n // 2, n % 2
                if n >= 2:
                    pe.wait_ge(xT_ready, n - 1)
                for t in range(HT):
                    mm = nc.tensor.transpose(turn[n % 2][0:HD2, t * P:(t + 1) * P], kept.x[:, hh * HT + t, m * HD2:(m + 1) * HD2], kept.ident[:, :])
                mm.then_inc(turned, 1)
            pe.wait_ge(w_in, 16)
            x = xT[:, :, :].rearrange("p m (b t) -> p m b t", t=SEQ)
            for n in range(4):
                hh, m = n // 2, n % 2
                pe.wait_ge(xT_ready, n + 1)
                out = acc[n][0:HD2, :].rearrange("p (b t) -> p b t", t=SEQ)
                order = sorted(range(-(SEQ - 1), SEQ), key=abs)
                for off in order:
                    lo, hi = max(0, -off), min(SEQ, SEQ - off)
                    mm = nc.tensor.matmul(out[:, :, lo:hi], w[:, m, off + SEQ - 1, :], x[:, m, hh * HIMG:(hh + 1) * HIMG, lo + off:hi + off],
                                          start=(off == 0), stop=(off == order[-1]), skip_group_check=True)
                mm.then_inc(conv_done, 1)
                if n == 3:
                    for t in range(NT):
                        pe.wait_ge(pos_ready, 2 * (t // HT + 1))
                        if t >= 2:
                            pe.wait_ge(back_read, t - 1)
                        for k in range(2):
                            mm = nc.tensor.transpose(turn[t % 2][:, k * HD2:(k + 1) * HD2], pT[:, k, t * P:(t + 1) * P], kept.ident[0:HD2, 0:HD2])
                        mm.then_inc(back_full, 1)

        @block.vector
        def _(dve):
            step = Steps(dve, dve_steps)
            for n in range(4):
                hh, m = n // 2, n % 2
                dve.wait_ge(turned, n + 1)
                nc.vector.tensor_copy(xT[:, m, hh * HTOK:(hh + 1) * HTOK], turn[n % 2][0:HD2, :]).then_inc(xT_ready, 1)
            for t in range(NT):
                dve.wait_ge(back_full, t + 1)
                nc.vector.tensor_tensor(kept.n[:, t, :], kept.x[:, t, :], turn[t % 2][:, 0:D], ALU.add).then_inc(back_read, 1)
                dve.wait_ge(back_read, t + 1)
                step(nc.vector.bn_stats(bn[:, t, 0:6], kept.n[:, t, :]))
                step(nc.vector.bn_aggr(bn[:, t, 6:8], bn[:, t, 0:6]))
            nc.vector.tensor_scalar(var[:, :], bn[:, :, 7], EPS, None, ALU.add).then_inc(pow_asked, 1)
            dve.wait_ge(pow_done, 1)
            for t in range(NT):
                step(nc.vector.tensor_scalar(kept.n[:, t, :], kept.n[:, t, :], bn[:, t, 6:7], var[:, t:t + 1], ALU.subtract, ALU.mult))
            dve.wait_ge(small_in, 32)
            step(nc.vector.tensor_tensor(kept.r[:, :, :], kept.n[:, :, :], rows[:, 0:1, :].broadcast_to([P, NT, D]), ALU.mult))
            step(nc.vector.tensor_tensor(kept.r[:, :, :], kept.r[:, :, :], rows[:, 1:2, :].broadcast_to([P, NT, D]), ALU.add))


class LoopRing(Ring):

    def __init__(self, banks, full, free, plan):
        super().__init__(banks, full, free, plan)
        assert len(plan) % len(banks) == 0
        self.per = len(plan) // len(banks)
        self.before = 0

    def credit(self, eng):
        for free in self.frees:
            eng.sem_inc(free, 1)

    def count(self, i, name):
        return i * self.per + self.at[name] // len(self.banks)

    def wait_free(self, eng, name, i):
        eng.wait_ge(self.free(name), self.count(i, name) + 1)

    def wait_full(self, eng, name, i):
        eng.wait_ge(self.full(name), self.count(i, name) + 1)

    def wait_read(self, eng, name, i):
        eng.wait_ge(self.free(name), self.count(i, name) + 2)


HEADS = 12
HC = HEADS // 2
HU = HC // 2
NU = HT * 4
LAG_T, LAG_PV = 3, 5
OUT_AT = (2, 3, 5, 7)
PR = 8
PT = 4
SCALE = 0.25


def encoder(nc, a, kept):
    ctx, sb, bank, sem = scope(nc)
    with ctx:
        w_qkv = sb("enc_w_qkv", [HD2, 2, 3 * D])
        c_qk = sb("enc_c_qk", [HD2, 4])
        w_o = sb("enc_w_o", [HD2, 2, D])
        w_1 = sb("enc_w_1", [HD2, 2, F])
        w_2 = sb("enc_w_2", [P, FC, D])
        c_b = sb("enc_c_b", [HD2, 6])
        c_1 = sb("enc_c_1", [P, FC])
        rows = sb("enc_rows", [P, 6, D])
        c_n = sb("enc_c_n", [HD2, 4])
        hT = sb("enc_hT", [HD2, 2, 2, HTOK])
        h1T = sb("enc_h1T", [HD2, 2, 2, HTOK])
        qT = sb("enc_qT", [HD2 + TPI, 2, HTOK])
        kT = sb("enc_kT", [HD2, 2, HTOK])
        kbd = sb("enc_kbd", [HD2 + TPI, 2, HC, HTOK])
        vbd = [sb(f"enc_vbd{i}", [P, HT, 2, HC, HD2]) for i in range(2)]
        pr = [sb(f"enc_p{i}", [P, HU, P]) for i in range(PR)]
        mx = sb("enc_mx", [P, PR, HU])
        rs = sb("enc_rs", [P, PR, HU])
        pT = [sb(f"enc_pT{i}", [P, HU, P]) for i in range(PT)]
        oT = sb("enc_oT", [HD2, 2, HTOK])
        gT = sb("enc_gT", [P, 2, FC, HTOK])
        shift = sb("enc_shift", [P, D])
        bn = sb("enc_bn", [P, NT, 8])
        var = sb("enc_var", [P, 4, HT])
        half = sb("enc_neg_half", [P, 1])
        ring = LoopRing([bank(f"enc_g{i}") for i in range(2)], [sem(f"enc_g_full{i}") for i in range(2)], [sem(f"enc_g_free{i}") for i in range(2)],
                        [(n, 0, k) for n, k in (("q", 0), ("k", 0), ("q", 1), ("k", 1))] + [("v", 0, t) for t in range(HT)]
                        + [("t2", 1, m) for m in range(2)]
                        + [(n, 1, k) for n, k in (("q", 0), ("k", 0), ("q", 1), ("k", 1))] + [("v", 1, t) for t in range(HT)]
                        + [("o", 0, t) for t in range(HT)] + [("t1", 0, m) for m in range(2)] + [("f", 0, m) for m in range(FC)]
                        + [("o", 1, t) for t in range(HT)] + [("g", 0, t) for t in range(HT - 1)] + [("t1", 1, m) for m in range(2)]
                        + [("g", 0, HT - 1)]
                        + [("f", 1, m) for m in range(FC)] + [("t2", 0, m) for m in range(2)] + [("g", 1, t) for t in range(HT)])
        s_bank = [bank(f"enc_s{i}") for i in range(2)]
        t_bank = [bank(f"enc_t{i}") for i in range(2)]
        o_bank = [bank(f"enc_o{i}") for i in range(2)]
        a_in, b_in, n_in = (sem(f"enc_{n}_in") for n in ("attn_w", "rest_w", "norm_cols"))
        setup, mask_set, stats_waited = sem("enc_setup"), sem("enc_mask_set"), sem("enc_stats_waited")
        hT_ready, n_used, kbd_act, kbd_dve, s_full, max_done, exp_done, recip_done, norm_done, t_full, pt_ready, pv_done = (
            sem(f"enc_{n}") for n in ("hT_ready", "n_used", "kbd_act", "kbd_dve", "s_full", "max_done", "exp_done", "recip_done",
                                      "norm_done", "t_full", "pt_ready", "pv_done"))
        first_hT, oT_ready, n_ready, var_ready, rstd_ready, r_biased, r_ready = (
            sem(f"enc_{n}") for n in ("first_hT", "oT_ready", "n_ready", "var_ready", "rstd_ready", "r_biased", "r_ready"))
        shift_ready = sem("enc_shift_ready")
        dve_steps, pool_steps = sem("enc_dve_steps"), sem("enc_pool_steps")
        pe_first = sem("enc_first_turned")
        block = ctx.enter_context(nc.Block())

        def tiles(g):
            return slice(g * HT, (g + 1) * HT)

        @block.sync
        def _(sp):
            def attn_w(l):
                sp.dma_start(w_qkv[:, :, :], a["enc_w_qkv"][bass.ds(l, 1), :, :, :].rearrange("l p k n -> p (l k) n")).then_inc(a_in, 16)
                sp.dma_start(c_qk[:, :], a["enc_c_qk"][bass.ds(l, 1), :, :].rearrange("l p k -> p (l k)")).then_inc(a_in, 16)

            def rest_w(l):
                sp.dma_start(w_o[:, :, :], a["enc_w_o"][bass.ds(l, 1), :, :, :].rearrange("l p k n -> p (l k) n")).then_inc(b_in, 16)
                sp.dma_start(rows[:, :, :], a["enc_rows"][bass.ds(l, 1), :, :].partition_broadcast(P)).then_inc(b_in, 16)
                sp.dma_start(c_b[:, :], a["enc_c_b"][bass.ds(l, 1), :, :].rearrange("l p k -> p (l k)")).then_inc(b_in, 16)
                sp.dma_start(w_1[:, :, :], a["enc_w_1"][bass.ds(l, 1), :, :, :].rearrange("l p k n -> p (l k) n")).then_inc(b_in, 16)
                sp.dma_start(c_1[:, :], a["enc_c_1"][bass.ds(l, 1), :, :].rearrange("l p k -> p (l k)")).then_inc(b_in, 16)
                sp.dma_start(w_2[:, :, :], a["enc_w_2"][bass.ds(l, 1), :, :, :].rearrange("l p k n -> p (l k) n")).then_inc(b_in, 16)

            def norm_cols(l):
                sp.dma_start(c_n[:, :], a["enc_c_n"][bass.ds(l, 1), :, :].rearrange("l p k -> p (l k)")).then_inc(n_in, 16)

            norm_cols(0)
            attn_w(0)
            rest_w(0)
            with sp.Fori(0, L - 1) as l:
                sp.wait_ge(n_used, l + 1)
                norm_cols(l + 1)
                sp.wait_ge(exp_done, 2 * NU * (l + 1) + 2)
                attn_w(l + 1)
                sp.wait_ge(r_ready, 4 * (l + 1))
                rest_w(l + 1)
            sp.wait_ge(n_used, L)
            norm_cols(L)

        @block.gpsimd
        def _(pool):
            step = Steps(pool, pool_steps)
            for s, size in ((exp_done, 2), (pt_ready, 2), (pv_done, PT), (t_full, PR)):
                pool.sem_inc(s, size)
            nc.gpsimd.memset(half[:, :], -0.5).then_inc(setup, 1)
            for i in range(2):
                pool.wait_ge(setup, 1 + i)
                nc.gpsimd.memset(vbd[i][:, :, :, :, :], 0.0).then_inc(setup, 1)
            pool.wait_ge(setup, 3)
            per_layer = 4
            with pool.Fori(0, L) as l:
                step.enter(l, per_layer)

                def rstd(k):
                    pool.wait_ge(var_ready, 4 * l + k + 1)
                    nc.gpsimd.tensor_tensor(var[:, k, :], var[:, k, :], half[:, 0:1].broadcast_to([P, HT]), ALU.pow).then_inc(rstd_ready, 1)

                def normalise(g, u):
                    n = 2 * NU * l + g * NU + u
                    pool.wait_ge(recip_done, n + 1)
                    nc.gpsimd.tensor_tensor(pr[u % PR][:, :, :], pr[u % PR][:, :, :], rs[:, u % PR, :].unsqueeze(2).broadcast_to([P, HU, P]),
                                            ALU.mult).then_inc(norm_done, 1)

                def bias(g):
                    nc.gpsimd.tensor_tensor(kept.r[:, tiles(g), :], kept.r[:, tiles(g), :], rows[:, 0:1, :].broadcast_to([P, HT, D]), ALU.add).then_inc(r_biased, 1)

                def residual(g, k, second):
                    pool.wait_ge(n_ready, 4 * l + k + 2)
                    step(nc.gpsimd.tensor_tensor(kept.r[:, tiles(g), :], kept.n[:, tiles(g), :], rows[:, 4 if second else 1, :].unsqueeze(1).broadcast_to([P, HT, D]), ALU.mult))
                    add = rows[:, 5, :] if second else shift[:, :]
                    nc.gpsimd.tensor_tensor(kept.r[:, tiles(g), :], kept.r[:, tiles(g), :], add.unsqueeze(1).broadcast_to([P, HT, D]), ALU.add).then_inc(r_ready, 1)
                    pool.wait_ge(r_ready, 4 * l + k + 1)

                for u in range(NU):
                    normalise(0, u)
                    if u == 8:
                        pool.wait_ge(b_in, 96 * (l + 1))
                        nc.gpsimd.tensor_tensor(shift[:, :], rows[:, 2, :], rows[:, 3, :], ALU.add).then_inc(shift_ready, 1)
                        pool.wait_ge(shift_ready, l + 1)
                        bias(0)
                    if u == 12:
                        bias(1)
                for u in range(NU):
                    normalise(1, u)
                    if u == OUT_AT[-1] - 1:
                        rstd(0)
                residual(0, 0, False)
                rstd(1)
                residual(1, 1, False)
                rstd(2)
                residual(0, 2, True)
                rstd(3)
                residual(1, 3, True)
            step.leave(L)
            pool.wait_ge(var_ready, 4 * L + 1)
            nc.gpsimd.tensor_tensor(bn[:, :, 7], bn[:, :, 7], half[:, 0:1].broadcast_to([P, NT]), ALU.pow).then_inc(rstd_ready, 1)

        @block.scalar
        def _(act):
            act.wait_ge(n_in, 16)
            for m in range(2):
                act.wait_ge(pe_first, m + 1)
                nc.scalar.activation(hT[:, 0, m, :], o_bank[m][0:HD2, :], ACT.Identity, bias=c_n[:, 2 + m:3 + m], scale=c_n[:, m:m + 1]).then_inc(first_hT, 1)
            act.wait_ge(setup, 3)
            with act.Fori(0, L) as l:
                def qk(g):
                    for k in range(2):
                        for name, dst, col in (("q", qT, k), ("k", kT, 2 + k)):
                            use = (name, g, k)
                            ring.wait_full(act, use, l)
                            nc.scalar.activation(dst[0:HD2, k, :], ring.bank(use)[0:HD2, :], ACT.Identity, bias=c_qk[:, col:col + 1]).then_inc(ring.free(use), 1)
                            if (k, name) == (0, "k"):
                                ring.wait_read(act, use, l)
                                masked_k(HU)
                                masked_k(HU + 1)
                            elif (k, name) == (1, "q"):
                                masked_k(HU + 2)

                def masked_k(h):
                    nc.scalar.activation(kbd[0:HD2, 0, h, :], kT[:, 0, :], ACT.Copy, scale=kept.head_rows[:, h:h + 1]).then_inc(kbd_act, 1)

                def values(g, ts):
                    for t in ts:
                        use = ("v", g, t)
                        ring.wait_full(act, use, l)
                        nc.scalar.copy(own_columns(vbd[g], t), ring.bank(use)[:, 0:D].rearrange("p (c h d) -> p c h d", c=2, h=HC)).then_inc(ring.free(use), 1)

                def exponent(g, u):
                    n = 2 * NU * l + g * NU + u
                    act.wait_ge(max_done, n + 1)
                    act.wait_ge(t_full, n + 1)
                    for h in range(HU):
                        ins = nc.scalar.activation(pr[u % PR][:, h, :], s_bank[u % 2][:, h * P:(h + 1) * P], ACT.Exp, scale=SCALE,
                                                   bias=mx[:, u % PR, h:h + 1], accum_out=rs[:, u % PR, h:h + 1])
                    ins.then_inc(exp_done, 1)

                def attended(g):
                    act.wait_ge(pv_done, 2 * NU * l + (g + 1) * NU + PT)
                    for m in range(2):
                        nc.scalar.activation(oT[:, m, :], o_bank[m][0:HD2, :], ACT.Identity, bias=c_b[:, m:m + 1]).then_inc(oT_ready, 1)

                def gain(use, dst, cols):
                    m = use[2]
                    ring.wait_full(act, use, l)
                    nc.scalar.activation(dst[:, use[1], m, :], ring.bank(use)[0:HD2, :], ACT.Identity,
                                         bias=cols[:, m + 2:m + 3], scale=cols[:, m:m + 1]).then_inc(ring.free(use), 1)

                def gelu(g, m):
                    use = ("f", g, m)
                    ring.wait_full(act, use, l)
                    nc.scalar.activation(gT[:, g, m, :], ring.bank(use)[:, :], ACT.Gelu, bias=c_1[:, m:m + 1]).then_inc(ring.free(use), 1)

                nc.scalar.preload_act_table(ACT.Exp)
                act.wait_ge(a_in, 32 * (l + 1))
                qk(0)
                values(0, (0, 1, 2))
                for u in range(NU):
                    exponent(0, u)
                    if u == 0:
                        values(0, (3,))
                    if u == NU // 2:
                        for m in range(2):
                            gain(("t2", 1, m), hT, c_n)
                        for m in range(2):
                            ring.wait_read(act, ("t2", 1, m), l)
                        act.sem_inc(n_used, 1)
                qk(1)
                values(1, (0, 1))
                act.wait_ge(b_in, 96 * (l + 1))
                attended(0)
                values(1, (2,))
                for u in range(NU):
                    exponent(1, u)
                    if u == 0:
                        values(1, (3,))
                    if u == NU - 2:
                        for m in range(2):
                            gain(("t1", 0, m), h1T, c_b[:, 2:6])
                for m in range(FC):
                    gelu(0, m)
                    if m == 2:
                        attended(1)
                for m in range(2):
                    gain(("t1", 1, m), h1T, c_b[:, 2:6])
                for m in range(FC):
                    gelu(1, m)
                act.wait_ge(n_in, 16 * (l + 2))
                for m in range(2):
                    gain(("t2", 0, m), hT, c_n)

        @block.tensor
        def _(pe):
            for m in range(2):
                for t in range(HT):
                    mm = nc.tensor.transpose(o_bank[m][0:HD2, t * P:(t + 1) * P], kept.n[:, t, m * HD2:(m + 1) * HD2], kept.ident[:, :])
                mm.then_inc(pe_first, 1)
            pe.wait_ge(first_hT, 2)
            pe.wait_ge(mask_set, 4)
            ring.credit(pe)
            pe.sem_inc(oT_ready, 1)
            with pe.Fori(0, L) as l:
                def qk(g):
                    for k in range(2):
                        for name, first in (("q", 0), ("k", D)):
                            use = (name, g, k)
                            ring.wait_free(pe, use, l)
                            for j in range(2):
                                mm = nc.tensor.matmul(ring.bank(use)[0:HD2, :], w_qkv[:, j, first + k * HD2:first + (k + 1) * HD2], hT[:, g, j, :],
                                                      start=(j == 0), stop=(j == 1))
                            mm.then_inc(ring.full(use), 1)

                def values(g, ts):
                    for t in ts:
                        use = ("v", g, t)
                        ring.wait_free(pe, use, l)
                        for j in range(2):
                            mm = nc.tensor.matmul(ring.bank(use)[:, 0:D], hT[:, g, j, t * P:(t + 1) * P], w_qkv[:, j, 2 * D:3 * D],
                                                  start=(j == 0), stop=(j == 1))
                        mm.then_inc(ring.full(use), 1)

                def scores(g, u):
                    n = 2 * NU * l + g * NU + u
                    t, c, hf = u // 4, u // 2 % 2, u % 2
                    if u == 0:
                        ring.wait_read(pe, ("k", g, 1), l)
                        ring.wait_read(pe, ("q", g, 1), l)
                    if u < 4:
                        if u == 1:
                            pe.wait_ge(kbd_act, HU * (2 * l + g + 1))
                        else:
                            pe.wait_ge(kbd_dve, 3 * HU * (2 * l + g) + HU * max(u, 1))
                    pe.wait_ge(exp_done, n + 1)
                    out = s_bank[u % 2][:, 0:HU * P].rearrange("p (h t) -> p h t", h=HU)
                    nc.tensor.matmul(out, qT[:, c, t * P:(t + 1) * P], kbd[:, c, hf * HU:(hf + 1) * HU, t * P:(t + 1) * P],
                                     start=True, stop=True).then_inc(s_full, 1)

                def turn(g, u):
                    n = 2 * NU * l + g * NU + u
                    pe.wait_ge(norm_done, n + 1)
                    pe.wait_ge(pt_ready, n + 1)
                    for h in range(HU):
                        mm = nc.tensor.transpose(t_bank[u % 2][:, h * P:(h + 1) * P], pr[u % PR][:, h, :], kept.ident[:, :])
                    mm.then_inc(t_full, 1)

                def pv(g, u):
                    n = 2 * NU * l + g * NU + u
                    t, c, hf = u // 4, u // 2 % 2, u % 2
                    if u == 0:
                        ring.wait_read(pe, ("v", g, HT - 1), l)
                        ring.wait_read(pe, ("v", g, HT - 2), l)
                        pe.wait_ge(oT_ready, 2 * (2 * l + g) + 1)
                    pe.wait_ge(pt_ready, n + 1 + 2)
                    for h in range(HU):
                        mm = nc.tensor.matmul(o_bank[c][0:HD2, t * P:(t + 1) * P], vbd[g][:, t, c, hf * HU + h, :], pT[u % PT][:, h, :],
                                              start=(hf == 0 and h == 0), stop=(hf == 1 and h == HU - 1))
                    mm.then_inc(pv_done, 1)

                def unit_tail(g):
                    pv(g, NU - 5)
                    pv(g, NU - 4)
                    turn(g, NU - 1)
                    for u in range(NU - 3, NU):
                        pv(g, u)

                def units(g):
                    for u in range(NU):
                        scores(g, u)
                        if u < 2:
                            values(g, (2 + u,))
                        if g == 1 and u in OUT_AT:
                            out_proj(0, (OUT_AT.index(u),))
                        if u >= LAG_T:
                            turn(g, u - LAG_T)
                        if u >= LAG_PV:
                            pv(g, u - LAG_PV)
                        if g == 0 and u == NU // 2:
                            pe.wait_ge(n_ready, 4 * l + 1)
                            turn_norm("t2", 1)
                        if g == 1 and u == NU - 2:
                            pe.wait_ge(n_ready, 4 * l + 2)
                            turn_norm("t1", 0)

                def turn_norm(name, g):
                    for m in range(2):
                        use = (name, g, m)
                        ring.wait_free(pe, use, l)
                        for t in range(HT):
                            mm = nc.tensor.transpose(ring.bank(use)[0:HD2, t * P:(t + 1) * P], kept.n[:, g * HT + t, m * HD2:(m + 1) * HD2], kept.ident[:, :])
                        mm.then_inc(ring.full(use), 1)

                def out_proj(g, ts):
                    if ts[0] == 0:
                        pe.wait_ge(oT_ready, 2 * (2 * l + g + 1) + 1)
                    for t in ts:
                        use = ("o", g, t)
                        ring.wait_free(pe, use, l)
                        for j in range(2):
                            mm = nc.tensor.matmul(ring.bank(use)[:, 0:D], oT[:, j, t * P:(t + 1) * P], w_o[:, j, :], start=(j == 0), stop=(j == 1))
                        mm.then_inc(ring.full(use), 1)

                def ffn_in(g, ms):
                    for m in ms:
                        use = ("f", g, m)
                        ring.wait_free(pe, use, l)
                        if m == 0:
                            for j in range(2):
                                ring.wait_read(pe, ("t1", g, j), l)
                        for j in range(2):
                            mm = nc.tensor.matmul(ring.bank(use)[:, :], w_1[:, j, m * P:(m + 1) * P], h1T[:, g, j, :], start=(j == 0), stop=(j == 1))
                        mm.then_inc(ring.full(use), 1)

                def ffn_out(g, ts):
                    if ts[0] == 0:
                        for m in (FC - 2, FC - 1):
                            ring.wait_read(pe, ("f", g, m), l)
                    for t in ts:
                        use = ("g", g, t)
                        ring.wait_free(pe, use, l)
                        for m in range(FC):
                            mm = nc.tensor.matmul(ring.bank(use)[:, 0:D], gT[:, g, m, t * P:(t + 1) * P], w_2[:, m, :], start=(m == 0), stop=(m == FC - 1))
                        mm.then_inc(ring.full(use), 1)

                pe.wait_ge(a_in, 32 * (l + 1))
                qk(0)
                values(0, (0, 1))
                units(0)
                turn(0, NU - 3)
                for m in range(2):
                    ring.wait_read(pe, ("t2", 1, m), l)
                qk(1)
                turn(0, NU - 2)
                values(1, (0, 1))
                unit_tail(0)
                pe.wait_ge(b_in, 96 * (l + 1))
                units(1)
                turn(1, NU - 3)
                ffn_in(0, range(1))
                turn(1, NU - 2)
                ffn_in(0, range(1, 3))
                unit_tail(1)
                ffn_in(0, range(3, FC))
                out_proj(1, range(HT))
                ffn_out(0, range(HT - 1))
                pe.wait_ge(n_ready, 4 * l + 3)
                turn_norm("t1", 1)
                ffn_out(0, (HT - 1,))
                ffn_in(1, range(FC))
                pe.wait_ge(n_ready, 4 * l + 4)
                turn_norm("t2", 0)
                ffn_out(1, range(HT))
                for m in range(2):
                    ring.wait_read(pe, ("t2", 0, m), l)

        @block.vector
        def _(dve):
            step = Steps(dve, dve_steps)
            dve.sem_inc(n_ready, 1)
            own = kept.image_rows[:, :].unsqueeze(1)
            for c in range(2):
                rows_q = qT[HD2:, c, :].rearrange("p (t n) -> p t n", n=P)
                nc.vector.tensor_copy(rows_q, own.broadcast_to([TPI, HT, P])).then_inc(mask_set, 1)
                rows_k = kbd[HD2:, c, :, :].rearrange("p h (t n) -> p (h t) n", n=P)
                nc.vector.tensor_scalar(rows_k, own.broadcast_to([TPI, HC * HT, P]), -1.0, BIG, ALU.add, ALU.mult).then_inc(mask_set, 1)
            with dve.Fori(0, L) as l:
                step.enter(l, DVE_STEPS)

                def masked_k(g, c, heads):
                    ring.wait_read(dve, ("k", g, c), l)
                    for h in heads:
                        nc.vector.tensor_scalar(kbd[0:HD2, c, h, :], kT[:, c, :], kept.head_rows[:, h:h + 1], None, ALU.mult).then_inc(kbd_dve, 1)

                def maxima(g, u):
                    sc = s_bank[u % 2][:, 0:HU * P].rearrange("p (h t) -> p h t", h=HU)
                    dve.wait_ge(s_full, 2 * NU * l + g * NU + u + 1)
                    step(nc.vector.tensor_reduce(mx[:, u % PR, :], sc, AX.X, ALU.max))
                    nc.vector.tensor_scalar(mx[:, u % PR, :], mx[:, u % PR, :], -SCALE, None, ALU.mult).then_inc(max_done, 1)

                def inverse(g, u):
                    dve.wait_ge(exp_done, 2 * NU * l + g * NU + u + 1 + 2)
                    nc.vector.reciprocal(rs[:, u % PR, :], rs[:, u % PR, :]).then_inc(recip_done, 1)

                def probs(g, u):
                    n = 2 * NU * l + g * NU + u
                    dve.wait_ge(t_full, n + 1 + PR)
                    dve.wait_ge(pv_done, n + 1)
                    nc.vector.tensor_copy(pT[u % PT][:, :, :], t_bank[u % 2][:, 0:HU * P].rearrange("p (h t) -> p h t", h=HU)).then_inc(pt_ready, 1)

                def unit(g, u):
                    maxima(g, u)
                    if u >= 1:
                        inverse(g, u - 1)
                    if u >= LAG_T:
                        probs(g, u - LAG_T)

                def norm_tile(name, g, t):
                    use, a_t = (name, g, t), g * HT + t
                    ring.wait_full(dve, use, l)
                    nc.vector.tensor_tensor(kept.n[:, a_t, :], kept.r[:, a_t, :], ring.bank(use)[:, 0:D], ALU.add).then_inc(ring.free(use), 1)
                    ring.wait_read(dve, use, l)
                    step(nc.vector.bn_stats(bn[:, a_t, 0:6], kept.n[:, a_t, :]))
                    dve.sem_inc(stats_waited, 1)
                    step(nc.vector.bn_aggr(bn[:, a_t, 6:8], bn[:, a_t, 0:6]))

                def norm_var(g, k):
                    nc.vector.tensor_scalar(var[:, k, :], bn[:, tiles(g), 7], EPS, None, ALU.add).then_inc(var_ready, 1)

                def norm_end(g, k):
                    dve.wait_ge(rstd_ready, 4 * l + k + 1)
                    for t in range(HT):
                        a_t = g * HT + t
                        ins = nc.vector.tensor_scalar(kept.n[:, a_t, :], kept.n[:, a_t, :], bn[:, a_t, 6:7], var[:, k, t:t + 1], ALU.subtract, ALU.mult)
                        if t == HT - 1:
                            ins.then_inc(n_ready, 1)
                        else:
                            step(ins)

                def norm(name, g, k):
                    for t in range(HT):
                        norm_tile(name, g, t)
                    norm_var(g, k)
                    norm_end(g, k)

                low, high = range(HU), range(HU, HC)
                masked_k(0, 0, low)
                masked_k(0, 1, low)
                masked_k(0, 1, high)
                for u in range(NU):
                    unit(0, u)
                inverse(0, NU - 1)
                probs(0, NU - 3)
                masked_k(1, 0, low)
                probs(0, NU - 2)
                masked_k(1, 1, low)
                probs(0, NU - 1)
                masked_k(1, 1, high)
                dve.wait_ge(r_biased, 2 * l + 2)
                for u in range(NU):
                    unit(1, u)
                    if u in OUT_AT:
                        norm_tile("o", 0, OUT_AT.index(u))
                    if u == OUT_AT[-1] + 1:
                        norm_var(0, 0)
                    if u == NU - 4:
                        norm_end(0, 0)
                inverse(1, NU - 1)
                for u in range(NU - LAG_T, NU):
                    probs(1, u)
                norm("o", 1, 1)
                dve.wait_ge(r_ready, 4 * l + 1)
                norm("g", 0, 2)
                dve.wait_ge(r_ready, 4 * l + 2)
                norm("g", 1, 3)
            step.leave(L)
            dve.wait_ge(r_ready, 4 * L)
            step(nc.vector.tensor_tensor(kept.h[:, :, :], kept.h[:, :, :], kept.r[:, :, :], ALU.add))
            for t in range(NT):
                step(nc.vector.bn_stats(bn[:, t, 0:6], kept.h[:, t, :]))
                step(nc.vector.bn_aggr(bn[:, t, 6:8], bn[:, t, 0:6]))
            nc.vector.tensor_scalar(bn[:, :, 7], bn[:, :, 7], EPS, None, ALU.add).then_inc(var_ready, 1)
            dve.wait_ge(rstd_ready, 4 * L + 1)
            for t in range(NT):
                step(nc.vector.tensor_scalar(kept.x[:, t, :], kept.h[:, t, :], bn[:, t, 6:7], bn[:, t, 7:8], ALU.subtract, ALU.mult))


DVE_STEPS = 2 * NU + 2 * HT * 2 * 2 + 4 * (HT - 1)


def own_columns(v, t):
    w = v[:, t, :, :, 0:D // HEADS]
    (ps, pn), (cs, cn), (hs, hn), (ds, dn) = w.ap
    return bass.AP(w.tensor, w.offset, [[ps, pn], [cs, cn], [hs + D // HEADS, hn], [ds, dn]])


E = 16
RMS_EPS = 1e-6
NB = NT + E - 1
WB = 4


def experts(nc, a, kept):
    ctx, sb, bank, sem = scope(nc)
    with ctx:
        w_i = [sb(f"moe_wi{i}", [HD2, 2, F]) for i in range(WB)]
        w_o = [sb(f"moe_wo{i}", [P, FC, D]) for i in range(WB)]
        gain = sb("moe_ln_w", [P, D])
        w_r = sb("moe_w_router", [HD2, 2, E])
        rank = sb("moe_rank", [P, E])
        steps8 = sb("moe_steps", [P, NT])
        numbers = sb("moe_block_numbers", [1, NB])
        earlier = sb("moe_earlier", [P, P])
        ones = sb("moe_ones", [P, P])
        zeros = sb("moe_zeros", [P, D])
        sqr = sb("moe_sqr", [P, NT, D])
        ms = sb("moe_ms", [P, NT])
        half = sb("moe_neg_half", [P, 1])
        nT = sb("moe_normedT", [HD2, 2, TOK])
        prob = sb("moe_p", [P, NT, E])
        first = sb("moe_first", [P, NT, E])
        st = sb("moe_stats", [P, 3, NT])
        before = sb("moe_before", [P, NT + 1, E])
        blocks = sb("moe_blocks", [P, 3, E])
        more = sb("moe_more", [P, E, NT])
        place_f = sb("moe_place_f", [P, NT, E])
        sum_f = sb("moe_place_sum", [P, NT])
        place_of = sb("moe_place", [P, NT], U32)
        past = sb("moe_past", [1, NB, E])
        ids_f = sb("moe_ids_f", [1, NB])
        ids = sb("moe_ids", [1, NB], I32)
        xs = [sb(f"moe_x{i}", [P, D]) for i in range(WB)]
        xT = [sb(f"moe_xT{i}", [HD2, 2, P]) for i in range(2)]
        hid = [sb(f"moe_hid{i}", [P, F]) for i in range(2)]
        hT = sb("moe_hidT", [P, FC, P])
        ys = [sb(f"moe_y{i}", [P, D]) for i in range(2)]
        h_bank = [bank(f"moe_h{i}", (P, 1024)) for i in range(2)]
        t_bank = bank("moe_t", (P, 1024))
        x_bank = bank("moe_xt")
        o_bank = bank("moe_o")
        small_in = sem("moe_small_in")
        setup, zeroed, scattered = sem("moe_setup"), sem("moe_zeroed"), sem("moe_scattered")
        wi_in, wo_in, x_in = ([sem(f"moe_{n}{i}") for i in range(WB)] for n in ("wi_in", "wo_in", "x_in"))
        stored = [sem(f"moe_stored{i}") for i in range(2)]
        gathered = [sem(f"moe_gathered{i}") for i in range(2)]
        pow_asked, pow_done = sem("moe_pow_asked"), sem("moe_pow_done")
        turned, nT_ready, logits_done, exp_asked, exp_done, first_ready, counted, ids_ready, place_ready = (
            sem(f"moe_{n}") for n in ("turned", "nT_ready", "logits_done", "exp_asked", "exp_done", "first_ready", "counted", "ids_ready", "place_ready"))
        xt_full, xT_ready, fc1_done, relu_done, t_done, hT_ready, fc2_done, y_ready = (
            sem(f"moe_{n}") for n in ("xt_full", "xT_ready", "fc1_done", "relu_done", "t_done", "hT_ready", "fc2_done", "y_ready"))
        dve_steps = sem("moe_dve_steps")
        x_dram = nc.dram_tensor("moe_x_scratch", [NB * P, D], F32, kind="Internal").ap()
        y_dram = nc.dram_tensor("moe_y_scratch", [NB * P, D], F32, kind="Internal").ap()
        block = ctx.enter_context(nc.Block())
        ROUNDS = (NB - 3) // 2
        assert NB == 2 * ROUNDS + 3

        @block.sync
        def _(sp):
            for dst, name in ((gain, "moe_ln_w"), (rank, "moe_rank"), (steps8, "moe_steps")):
                sp.dma_start(dst[:, :], a[name].partition_broadcast(P)).then_inc(small_in, 16)
            sp.dma_start(w_r[:, :, :], a["moe_w_router"]).then_inc(small_in, 16)
            sp.dma_start(numbers[:, :], a["moe_numbers"]).then_inc(small_in, 16)
            sp.dma_start(earlier[:, :], a["moe_earlier"]).then_inc(small_in, 16)
            sp.wait_ge(setup, 3)
            sp.dma_start(x_dram.rearrange("(p r) d -> p r d", r=NB), zeros[:, :].unsqueeze(1).broadcast_to([P, NB, D])).then_inc(zeroed, 16)

            def weights(b, w, old):
                e = sp.value_load(ids[0:1, bass.ds(b, 1)], min_val=0, max_val=E - 1)
                if old:
                    sp.wait_ge(fc1_done, b - WB + 1)
                sp.dma_start(w_i[w][:, :, :], a["moe_wi"][bass.ds(e, 1), :, :, :].rearrange("e p k f -> (e p) k f")).then_inc(wi_in[w], 16)
                if old:
                    sp.wait_ge(fc2_done, b - WB + 2)
                sp.dma_start(w_o[w][:, :, :], a["moe_wo"][bass.ds(e, 1), :, :, :].rearrange("e p c d -> (e p) c d")).then_inc(wo_in[w], 16)

            def tokens(b, w, old):
                if old:
                    sp.wait_ge(xt_full, b - WB + 1)
                sp.dma_start(xs[w][:, :], x_dram[bass.ds(b * P, P), :]).then_inc(x_in[w], 16)

            def store(b, j):
                sp.wait_ge(y_ready, b + 1)
                sp.dma_start(y_dram[bass.ds(b * P, P), :], ys[j][:, :]).then_inc(stored[j], 16)

            sp.wait_ge(ids_ready, 1)
            for w in range(WB):
                weights(w, w, False)
            sp.wait_ge(scattered, 16 * NT)
            for w in range(WB):
                tokens(w, w, False)
            rounds = NB // WB - 1
            with sp.Fori(0, rounds) as i:
                for w in range(WB):
                    tokens(i * WB + w + WB, w, True)
                    weights(i * WB + w + WB, w, True)
                    store(i * WB + w, w % 2)
            for b in range(rounds * WB, NB):
                if b + WB < NB:
                    tokens(b + WB, b % WB, True)
                    weights(b + WB, b % WB, True)
                store(b, b % 2)

        @block.gpsimd
        def _(pool):
            nc.gpsimd.memset(half[:, :], -0.5).then_inc(setup, 1)
            nc.gpsimd.memset(zeros[:, :], 0.0).then_inc(setup, 1)
            nc.gpsimd.memset(before[:, 0, :], 0.0).then_inc(setup, 1)
            nc.gpsimd.memset(ones[:, :], 1.0).then_inc(setup, 1)
            pool.wait_ge(setup, 4)
            pool.wait_ge(pow_asked, 1)
            nc.gpsimd.tensor_tensor(ms[:, :], ms[:, :], half[:, 0:1].broadcast_to([P, NT]), ALU.pow).then_inc(pow_done, 1)
            pool.wait_ge(pow_asked, 3)
            pool.wait_ge(zeroed, 16)
            pool.wait_ge(place_ready, 1)
            for t in range(NT):
                nc.gpsimd.indirect_dma_start(x_dram, bass.IndirectOffsetOnAxis(ap=place_of[:, t:t + 1], axis=0), kept.n[:, t, :], None).then_inc(scattered, 16)
            for j in range(2):
                pool.wait_ge(stored[j], 16 * ((NB + 1 - j) // 2 + 1))
            for t in range(NT):
                nc.gpsimd.indirect_dma_start(kept.r[:, t, :], None, y_dram, bass.IndirectOffsetOnAxis(ap=place_of[:, t:t + 1], axis=0)).then_inc(gathered[t // HT], 16)

        @block.scalar
        def _(act):
            act.wait_ge(exp_asked, 1)
            nc.scalar.activation(prob[:, :, :], prob[:, :, :], ACT.Exp).then_inc(exp_done, 1)

            def relu(b, j):
                act.wait_ge(fc1_done, b + 1)
                act.wait_ge(t_done, b + 1)
                nc.scalar.activation(hid[j][:, :], h_bank[j][:, 0:F], ACT.Relu).then_inc(relu_done, 1)

            with act.Fori(0, NB // 2) as i:
                for j in range(2):
                    relu(i * 2 + j, j)
            relu(NB - 1, 0)

        @block.tensor
        def _(pe):
            pe.sem_inc(relu_done, 2)
            pe.sem_inc(t_done, 2)
            pe.sem_inc(fc2_done, 1)
            pe.sem_inc(hT_ready, 1)
            for n in range(4):
                hh, k = n // 2, n % 2
                if k == 0:
                    pe.wait_ge(pow_asked, 2 + hh)
                if n >= 2:
                    pe.wait_ge(nT_ready, n - 1)
                for t in range(HT):
                    mm = nc.tensor.transpose(h_bank[n % 2][0:HD2, t * P:(t + 1) * P], kept.n[:, hh * HT + t, k * HD2:(k + 1) * HD2], kept.ident[:, :])
                mm.then_inc(turned, 1)
            pe.wait_ge(nT_ready, 4)
            pe.wait_ge(small_in, 96)
            for t in range(NT):
                for k in range(2):
                    mm = nc.tensor.matmul(x_bank[:, t * E:(t + 1) * E], nT[:, k, t * P:(t + 1) * P], w_r[:, k, :], start=(k == 0), stop=(k == 1))
            mm.then_inc(logits_done, 1)
            pe.wait_ge(setup, 4)
            pe.wait_ge(first_ready, 1)
            flat = first[:, :, :].rearrange("p t e -> p (t e)")
            nc.tensor.matmul(o_bank[:, 0:NT * E], earlier[:, :], flat, start=True, stop=True)
            nc.tensor.matmul(t_bank[:, 0:NT * E], ones[:, :], flat, start=True, stop=True).then_inc(counted, 1)

            def turn_x(b, w, n, old=True):
                pe.wait_ge(x_in[w], 16 * n)
                if old:
                    pe.wait_ge(xT_ready, b)
                for k in range(2):
                    mm = nc.tensor.transpose(x_bank[0:HD2, k * P:(k + 1) * P], xs[w][:, k * HD2:(k + 1) * HD2], kept.ident[:, :])
                mm.then_inc(xt_full, 1)

            def fc1(b, j, w, n):
                pe.wait_ge(wi_in[w], 16 * n)
                pe.wait_ge(xT_ready, b + 1)
                pe.wait_ge(relu_done, b + 1)
                for lo, hi in ((0, 512), (512, F)):
                    for k in range(2):
                        mm = nc.tensor.matmul(h_bank[j][:, lo:hi], xT[j][:, k, :], w_i[w][:, k, lo:hi], start=(k == 0), stop=(k == 1))
                mm.then_inc(fc1_done, 1)

            def turn_h(b, j):
                pe.wait_ge(relu_done, b + 3)
                pe.wait_ge(hT_ready, b + 1)
                for m in range(FC):
                    mm = nc.tensor.transpose(t_bank[:, m * P:(m + 1) * P], hid[j][:, m * P:(m + 1) * P], kept.ident[:, :])
                mm.then_inc(t_done, 1)

            def fc2(b, w, n, old=True):
                pe.wait_ge(wo_in[w], 16 * n)
                pe.wait_ge(hT_ready, b + 2)
                if old:
                    pe.wait_ge(y_ready, b)
                for m in range(FC):
                    mm = nc.tensor.matmul(o_bank[:, 0:D], hT[:, m, :], w_o[w][:, m, :], start=(m == 0), stop=(m == FC - 1))
                mm.then_inc(fc2_done, 1)

            pe.wait_ge(place_ready, 1)
            turn_x(0, 0, 1, False)
            turn_x(1, 1, 1)
            fc1(0, 0, 0, 1)
            turn_x(2, 2, 1)
            turn_h(0, 0)
            fc1(1, 1, 1, 1)
            fc2(0, 0, 1, False)
            assert (NB - 3) % WB == 0
            with pe.Fori(0, (NB - 3) // WB) as i:
                for w in range(1, WB + 1):
                    b, j = i * WB + w, w % 2
                    turn_x(b + 2, (w + 2) % WB, i + (w + 2) // WB + 1)
                    turn_h(b, j)
                    fc1(b + 1, 1 - j, (w + 1) % WB, i + (w + 1) // WB + 1)
                    fc2(b, w % WB, i + w // WB + 1)
            turn_h(NB - 2, 1)
            fc1(NB - 1, 0, (NB - 1) % WB, (NB - 1) // WB + 1)
            fc2(NB - 2, (NB - 2) % WB, (NB - 2) // WB + 1)
            turn_h(NB - 1, 0)
            fc2(NB - 1, (NB - 1) % WB, (NB - 1) // WB + 1)

        @block.vector
        def _(dve):
            step = Steps(dve, dve_steps)
            for j in range(2):
                dve.sem_inc(stored[j], 16)
            step(nc.vector.tensor_tensor(sqr[:, :, :], kept.x[:, :, :], kept.x[:, :, :], ALU.mult))
            step(nc.vector.tensor_reduce(ms[:, :], sqr[:, :, :], AX.X, ALU.add))
            nc.vector.tensor_scalar(ms[:, :], ms[:, :], 1.0 / D, RMS_EPS, ALU.mult, ALU.add).then_inc(pow_asked, 1)
            dve.wait_ge(small_in, 96)
            dve.wait_ge(pow_done, 1)
            for t in range(NT):
                ins = nc.vector.scalar_tensor_tensor(kept.n[:, t, :], kept.x[:, t, :], ms[:, t:t + 1], gain[:, :], ALU.mult, ALU.mult)
                if t % HT == HT - 1:
                    ins.then_inc(pow_asked, 1)
                else:
                    step(ins)
            for n in range(4):
                hh, k = n // 2, n % 2
                dve.wait_ge(turned, n + 1)
                nc.vector.tensor_copy(nT[:, k, hh * HTOK:(hh + 1) * HTOK], h_bank[n % 2][0:HD2, 0:HTOK]).then_inc(nT_ready, 1)
            dve.wait_ge(logits_done, 1)
            lg = x_bank[:, 0:NT * E].rearrange("p (t e) -> p t e", e=E)
            each = [P, NT, E]
            step(nc.vector.tensor_reduce(st[:, 0, :], lg, AX.X, ALU.max))
            nc.vector.tensor_tensor(prob[:, :, :], lg, st[:, 0, :].unsqueeze(2).broadcast_to(each), ALU.subtract).then_inc(exp_asked, 1)
            dve.wait_ge(exp_done, 1)
            step(nc.vector.tensor_reduce(st[:, 0, :], prob[:, :, :], AX.X, ALU.max))
            step(nc.vector.tensor_tensor(first[:, :, :], prob[:, :, :], st[:, 0, :].unsqueeze(2).broadcast_to(each), ALU.is_equal))
            step(nc.vector.tensor_tensor(first[:, :, :], first[:, :, :], rank[:, :].unsqueeze(1).broadcast_to(each), ALU.mult))
            step(nc.vector.tensor_reduce(st[:, 2, :], first[:, :, :], AX.X, ALU.max))
            nc.vector.tensor_tensor(first[:, :, :], first[:, :, :], st[:, 2, :].unsqueeze(2).broadcast_to(each), ALU.is_equal).then_inc(first_ready, 1)
            step(nc.vector.tensor_reduce(st[:, 1, :], prob[:, :, :], AX.X, ALU.add))
            step(nc.vector.reciprocal(st[:, 1, :], st[:, 1, :]))
            step(nc.vector.tensor_tensor(st[:, 1, :], st[:, 0, :], st[:, 1, :], ALU.mult))
            dve.wait_ge(first_ready, 1)
            dve.wait_ge(setup, 4)
            dve.wait_ge(counted, 1)
            for t in range(NT):
                step(nc.vector.tensor_tensor(before[:, t + 1, :], before[:, t, :], t_bank[:, t * E:(t + 1) * E], ALU.add))
            step(nc.vector.tensor_tensor(more[:, :, :], before[:, NT, :].unsqueeze(2).broadcast_to([P, E, NT]),
                                         steps8[:, :].unsqueeze(1).broadcast_to([P, E, NT]), ALU.is_gt))
            step(nc.vector.tensor_reduce(blocks[:, 0, :], more[:, :, :], AX.X, ALU.add))
            step(nc.vector.tensor_tensor_scan(blocks[:, 1, :], ones[:, 0:E], blocks[:, 0, :], 0.0, ALU.mult, ALU.add))
            step(nc.vector.tensor_tensor(past[:, :, :], numbers[:, :].unsqueeze(2).broadcast_to([1, NB, E]),
                                         blocks[0:1, 1:2, :].broadcast_to([1, NB, E]), ALU.is_ge))
            step(nc.vector.tensor_reduce(ids_f[:, :], past[:, :, :], AX.X, ALU.add))
            nc.vector.tensor_scalar(ids[:, :], ids_f[:, :], float(E - 1), None, ALU.min).then_inc(ids_ready, 1)
            step(nc.vector.tensor_tensor(blocks[:, 2, :], blocks[:, 1, :], blocks[:, 0, :], ALU.subtract))
            step(nc.vector.tensor_scalar(blocks[:, 2, :], blocks[:, 2, :], float(P), None, ALU.mult))
            step(nc.vector.tensor_tensor(place_f[:, :, :], o_bank[:, 0:NT * E].rearrange("p (t e) -> p t e", e=E), before[:, 0:NT, :], ALU.add))
            step(nc.vector.tensor_tensor(place_f[:, :, :], place_f[:, :, :], blocks[:, 2:3, :].broadcast_to(each), ALU.add))
            step(nc.vector.tensor_tensor(place_f[:, :, :], place_f[:, :, :], first[:, :, :], ALU.mult))
            step(nc.vector.tensor_reduce(sum_f[:, :], place_f[:, :, :], AX.X, ALU.add))
            nc.vector.tensor_copy(place_of[:, :], sum_f[:, :]).then_inc(place_ready, 1)
            step(nc.vector.tensor_tensor(kept.h[:, :, :], kept.h[:, :, :], kept.x[:, :, :], ALU.add))

            def copy_x(b, j, old=True):
                dve.wait_ge(xt_full, b + 1)
                if old:
                    dve.wait_ge(fc1_done, b - 1)
                nc.vector.tensor_copy(xT[j][:, :, :], x_bank[0:HD2, 0:2 * P].rearrange("p (k t) -> p k t", k=2)).then_inc(xT_ready, 1)

            def copy_h(b):
                dve.wait_ge(t_done, b + 3)
                dve.wait_ge(fc2_done, b + 1)
                nc.vector.tensor_copy(hT[:, :, :], t_bank[:, 0:F].rearrange("p (m t) -> p m t", t=P)).then_inc(hT_ready, 1)

            def copy_y(b, j, n):
                dve.wait_ge(fc2_done, b + 2)
                dve.wait_ge(stored[j], 16 * n)
                nc.vector.tensor_copy(ys[j][:, :], o_bank[:, 0:D]).then_inc(y_ready, 1)

            copy_x(0, 0, False)
            copy_x(1, 1, False)
            with dve.Fori(0, ROUNDS) as i:
                for j in range(2):
                    copy_x(i * 2 + j + 2, j)
                    copy_h(i * 2 + j)
                    copy_y(i * 2 + j, j, i + 1)
            copy_x(NB - 1, 0)
            for b in range(NB - 3, NB):
                copy_h(b)
                copy_y(b, b % 2, b // 2 + 1)
            for t in range(NT):
                if t % HT == 0:
                    dve.wait_ge(gathered[t // HT], 16 * HT)
                step(nc.vector.scalar_tensor_tensor(kept.h[:, t, :], kept.r[:, t, :], st[:, 1, t:t + 1], kept.h[:, t, :], ALU.mult, ALU.add))



CONSTANTS = {"ident": (P, P), "pick_rows": (HD2, 2 * NS), "same_image": (P, TPI), "head_rows": (HD2, HC), "image_rows": (TPI, P)}


class Kept:
    pass


def build(nc, a, out):
    with ExitStack() as ctx:
        kept = Kept()
        kept.h, kept.x, kept.n, kept.r = (ctx.enter_context(nc.sbuf_tensor("s_kept_" + n, [P, NT, D], F32)) for n in "hxnr")
        const = {name: ctx.enter_context(nc.sbuf_tensor("s_kept_" + name, list(shape), F32)) for name, shape in CONSTANTS.items()}
        kept.ident, kept.pick_rows, kept.same_image, kept.head_rows, kept.image_rows = const.values()
        const_in = ctx.enter_context(nc.semaphore("const_in"))
        stored = ctx.enter_context(nc.semaphore("out_stored"))
        with nc.Block() as block:
            @block.sync
            def _(sp):
                for name, tile in const.items():
                    sp.dma_start(tile[:, :], a[name]).then_inc(const_in, 16)
                sp.wait_ge(const_in, 16 * len(const))
        tokenize(nc, a, kept)
        mamba(nc, a, kept)
        slot_experts(nc, a, kept)
        position(nc, a, kept)
        encoder(nc, a, kept)
        experts(nc, a, kept)
        with nc.Block() as block:
            @block.sync
            def _(sp):
                sp.dma_start(out.rearrange("(t b) n d -> (b n) t d", t=NT), kept.h[:, :, :]).then_inc(stored, 16)
                sp.wait_ge(stored, 16)



def lay_out(v):
    v = {k: np.asarray(x) for k, x in v.items()}
    o = {}
    stack = lambda fn: np.ascontiguousarray(np.stack([fn(layer) for layer in range(L)]))

    def by_rows(w, rows=HD2):
        return np.ascontiguousarray(w.reshape(-1, rows, w.shape[1]).transpose(1, 0, 2))

    def column(b, rows=HD2):
        return np.ascontiguousarray(b.reshape(-1, rows).T)

    n = SIDE // BLK
    blocks = v["x"].reshape(IMG, CH, n, BLK, n, BLK).transpose(1, 3, 5, 0, 2, 4)
    grid = np.zeros((CH, BLK, BLK, IMG, GRID, GRID), blocks.dtype)
    at = [i // 2 + (GRID // 2 + 1) * (i % 2) for i in range(n)]
    grid[..., np.ix_(at, at)[0], np.ix_(at, at)[1]] = blocks
    o["x_grid01"] = np.ascontiguousarray(grid[0:2].reshape(P, XCOLS))
    o["x_grid2"] = np.pad(grid[2].reshape(P // 2, XCOLS), ((0, 0), (8, 8)))

    def patch_rows(w):
        w = np.moveaxis(w, -1, 0).reshape(2, BLK, 2, BLK, len(SHIFTS), CH, -1)
        cells = [(s, dy) for s in range(len(SHIFTS)) for dy in range(2)]
        out = [w[dy, :, dx, :, s, 0:2].transpose(2, 0, 1, 3).reshape(P, -1) for s, dy in cells for dx in range(2)]
        out += [w[dy, :, :, :, s, 2].transpose(1, 0, 2, 3).reshape(P, -1) for s, dy in cells]
        return np.ascontiguousarray(np.stack(out, 1))

    o["tok_w"] = patch_rows(v["L0_tok_W"])
    o["tok_gb"] = np.stack([patch_rows(v["L0_tok_ln_" + k])[:, :, 0] for k in ("gamma", "beta")], 1)
    o["tok_b"] = v["L0_tok_b"][None]

    m = {k[8:]: x for k, x in v.items() if k.startswith("L0_attn_")}
    o["mam_bm_in_w"], o["mam_bm_in_b"] = by_rows(m["bm_in_w"].T), column(m["bm_in_b"])
    o["mam_in_w"] = by_rows(m["m_in_w"].T)
    o["mam_xproj_w"] = by_rows(np.concatenate([m["m_xproj_w"][RANK:], m["m_xproj_w"][:RANK]]).T, P)
    o["mam_dt_w"] = np.ascontiguousarray(m["m_dt_w"].T)
    o["mam_out_w"], o["mam_bm_out_w"] = by_rows(m["m_out_w"].T, P), by_rows(m["bm_out_w"].T)
    o["mam_channel"] = by_rows(np.concatenate([m["m_conv_w"], m["m_conv_b"][:, None], m["m_dt_b"][:, None], m["m_D"][:, None], m["m_A_log"]], 1), P)
    o["mam_rows"] = np.stack([m["bm_out_b"], m["ln_g"], m["ln_b"]])[None]

    for name, key in (("slots", "slots"), ("b2", "fc2_bias"), ("w1", "fc1_weight"), ("b1", "fc1_bias"), ("w2", "fc2_weight")):
        o["ffn_" + name] = v["L0_ffn_" + key]
    o["ffn_scale"], o["ffn_norm_w"] = v["L0_ffn_scale"][:, None], v["L0_ffn_norm_weight"][None]

    e = {k[8:]: x for k, x in v.items() if k.startswith("L1_attn_")}
    w = e["pos_conv_w"]
    group, mid = w.shape[1], w.shape[2] // 2
    pos = np.zeros((HD2, 2, TAPS, HD2), w.dtype)
    for k in range(2):
        for at in range(0, HD2, group):
            taps = w[k * HD2 + at:k * HD2 + at + group, :, mid - SEQ + 1:mid + SEQ]
            pos[at:at + group, k, :, at:at + group] = taps.transpose(1, 2, 0)
    o["pos_w"], o["pos_b"], o["pos_rows"] = pos, column(e["pos_conv_b"]), np.stack([e["ln0_g"], e["ln0_b"]])[None]
    o["enc_w_qkv"] = stack(lambda l: by_rows(np.concatenate([e[n][l] for n in ("Wq", "Wk", "Wv")], 1)))
    o["enc_c_qk"] = stack(lambda l: np.concatenate([column(e["bq"][l]), column(e["bk"][l])], 1))
    o["enc_w_o"], o["enc_w_1"] = (stack(lambda l: by_rows(e[n][l])) for n in ("Wo", "W1"))
    o["enc_w_2"] = stack(lambda l: by_rows(e["W2"][l], P))
    o["enc_c_b"] = stack(lambda l: np.concatenate([column(e[n][l]) for n in ("bv", "ln1_g", "ln1_b")], 1))
    o["enc_c_1"] = stack(lambda l: column(e["b1"][l], P))
    o["enc_rows"] = stack(lambda l: np.stack([e[n][l] for n in ("bo", "ln1_g", "ln1_b", "b2", "ln2_g", "ln2_b")]))
    before = [(e["ln0_g"], e["ln0_b"])] + list(zip(e["ln2_g"], e["ln2_b"]))
    o["enc_c_n"] = np.stack([np.concatenate([column(g), column(b)], 1) for g, b in before])

    o["moe_ln_w"], o["moe_w_router"] = v["L1_ffn_ln_w"][None], by_rows(v["L1_ffn_w_router"])
    o["moe_wi"] = np.stack([by_rows(w) for w in v["L1_ffn_wi"]])
    o["moe_wo"] = np.stack([by_rows(w, P) for w in v["L1_ffn_wo"]])

    p = np.arange(P)
    o["moe_rank"] = np.arange(E, 0, -1, dtype=np.float32)[None]
    o["moe_steps"] = (P * np.arange(NT, dtype=np.float32))[None]
    o["moe_numbers"] = np.arange(NB, dtype=np.float32)[None]
    o["moe_earlier"] = np.triu(np.ones((P, P), np.float32), 1)
    o["ident"] = np.eye(P, dtype=np.float32)
    o["pick_rows"] = (p[:HD2, None] % (2 * NS) == np.arange(2 * NS)).astype(np.float32)
    o["same_image"] = (p[:, None] // SEQ == np.arange(TPI)).astype(np.float32)
    o["image_rows"] = np.ascontiguousarray(o["same_image"].T)
    o["head_rows"] = (p[:HD2, None] // (D // HEADS) == np.arange(HC)).astype(np.float32)
    return {k: np.ascontiguousarray(x) for k, x in o.items()}


def kernel(**inputs):
    import concourse.bacc as _bacc
    from concourse.bass_utils import run_bass_kernel_spmd as _run

    nc = _bacc.Bacc("TRN2", target_bir_lowering=False, num_devices=1)
    arrays = lay_out(inputs)
    a = {name: nc.dram_tensor(name, list(x.shape), mybir.dt.from_np(x.dtype), kind="ExternalInput").ap() for name, x in arrays.items()}
    out = nc.dram_tensor("out", [IMG, SEQ, D], F32, kind="ExternalOutput").ap()
    build(nc, a, out)
    r = _run(nc, [arrays], core_ids=[0])
    return r.results[0]["out"]
```
